# Optimizing a Trainium2 kernel written in Bass

```python
import numpy as np
import jax
import jax.numpy as jnp

def _softmax(x, axis=-1):
    return jax.nn.softmax(x, axis=axis)

def _gelu(x):
    return jax.nn.gelu(x, approximate=True)

def _silu(x):
    return jax.nn.silu(x)

def _sigmoid(x):
    return jax.nn.sigmoid(x)

def _layernorm(x, axis=-1, eps=1e-05):
    m = jnp.mean(x, axis=axis, keepdims=True)
    v = jnp.var(x, axis=axis, keepdims=True)
    return (x - m) / jnp.sqrt(v + eps)

def _scatter_add(tgt, idx, src, axis=0):
    return tgt.at[idx].add(src)

def _segment_sum(src, seg, n):
    return jax.ops.segment_sum(src, seg, n)
kernel_name = 'mk_decoder_preln_d2_seqx_r8_af0021'

def setup_inputs(seed: int=0):
    np.random.seed(seed)
    _w = jnp.asarray

    def _rec_inputs():
        import jax
        import jax.numpy as jnp
        _rk = jax.random.key(seed)
        x = -0.0002928 + 1 * jax.random.normal(jax.random.fold_in(_rk, 1), (4, 512, 128), jnp.float32)
        _lenS = 512 - jax.random.randint(jax.random.fold_in(_rk, 7), (4,), 0, max(1, 512 // 4) + 1, jnp.int32)
        _lenS2 = 32 - jax.random.randint(jax.random.fold_in(_rk, 8), (4,), 0, max(1, 32 // 4) + 1, jnp.int32)
        _ctx_1024P = jax.random.normal(jax.random.fold_in(_rk, 11), (4, 16, 128), jnp.float32)
        _ctx_1024c = jax.random.dirichlet(jax.random.fold_in(_rk, 511), 0.3 * jnp.ones((16,), jnp.float32), (4, 32))
        _ctx_1024t = jnp.einsum('bsk,bkd->bsd', _ctx_1024c, _ctx_1024P)
        _ctx_1024t = _ctx_1024t * jax.lax.rsqrt(jnp.mean(jnp.square(_ctx_1024t)) + 1e-12) * 0.953939
        ctx_1024 = -1.39393e-06 + 0.999914 * (_ctx_1024t + 0.3 * jax.random.normal(jax.random.fold_in(_rk, 611), (4, 32, 128), jnp.float32))
        _validS = jnp.arange(512)[None, :] < _lenS[:, None]
        _validS2 = jnp.arange(32)[None, :] < _lenS2[:, None]
        _causal = jnp.tril(jnp.ones((512, 512), dtype=bool))
        mask_BxSxS2_bf0 = jnp.logical_not(jnp.ones((4, 512, 32), dtype=bool))
        mask_Bx1xSxS2_ik1 = jnp.where(jnp.broadcast_to(_validS2[:, None, None, :], (4, 1, 512, 32)), 1, 0).astype(jnp.int32)
        return (x, ctx_1024, mask_BxSxS2_bf0, mask_Bx1xSxS2_ik1)
    x, ctx_1024, mask_BxSxS2_bf0, mask_Bx1xSxS2_ik1 = _rec_inputs()

    def _L0_attn_setup():
        import jax, jax.numpy as jnp
        import numpy as np
        import math
        B_SZ, T, D_IN, D_OUT, N = (8, 512, 128, 128, 64)
        RMIN, RMAX, MAX_PHASE = (0.9, 1.0, 6.283)
        key = jax.random.key(seed)
        ks = jax.random.split(key, 9)
        x = jax.random.normal(ks[0], (B_SZ, T, D_IN), dtype=jnp.float32)
        u1 = jax.random.uniform(ks[1], (N,), dtype=jnp.float32)
        u2 = jax.random.uniform(ks[2], (N,), dtype=jnp.float32)
        nu_log = jnp.log(-0.5 * jnp.log(u1 * (RMAX + RMIN) * (RMAX - RMIN) + RMIN ** 2))
        theta_log = jnp.log(MAX_PHASE * u2)
        lam_mod = jnp.exp(-jnp.exp(nu_log))
        gamma_log = jnp.log(jnp.sqrt(1.0 - jnp.square(lam_mod)))
        B_re = jax.random.normal(ks[3], (N, D_IN), dtype=jnp.float32) / math.sqrt(2 * D_IN)
        B_im = jax.random.normal(ks[4], (N, D_IN), dtype=jnp.float32) / math.sqrt(2 * D_IN)
        C_re = jax.random.normal(ks[5], (D_OUT, N), dtype=jnp.float32) / math.sqrt(N)
        C_im = jax.random.normal(ks[6], (D_OUT, N), dtype=jnp.float32) / math.sqrt(N)
        D = jax.random.normal(ks[7], (D_OUT, D_IN), dtype=jnp.float32) / math.sqrt(D_IN)
        return {'x': x, 'nu_log': nu_log, 'theta_log': theta_log, 'gamma_log': gamma_log, 'B_re': B_re, 'B_im': B_im, 'C_re': C_re, 'C_im': C_im, 'D': D}
    _L0_attn_all = _L0_attn_setup()
    _L0_attn_in = {k: v for k, v in _L0_attn_all.items() if k in ('nu_log', 'theta_log', 'gamma_log', 'B_re', 'B_im', 'C_re', 'C_im', 'D')}
    del _L0_attn_all

    def _L0_xattn_setup():
        import jax, jax.numpy as jnp
        import numpy as np
        import math
        B, LQ, LK = (2, 256, 256)
        DIM = 128
        H = 16
        DH = DIM // H
        key = jax.random.key(seed)
        ks = jax.random.split(key, 12)
        s = 1.0 / math.sqrt(DIM)
        return {'query': jax.random.normal(ks[0], (B, LQ, DIM), jnp.float32), 'key': jax.random.normal(ks[1], (B, LK, DIM), jnp.float32), 'value': jax.random.normal(ks[2], (B, LK, DIM), jnp.float32), 'mask': jnp.zeros((B, LQ, LK), dtype=bool), 'Wq': jax.random.normal(ks[3], (DIM, DIM), jnp.float32) * s, 'bq': jax.random.normal(ks[4], (DIM,), jnp.float32) * s, 'Wk': jax.random.normal(ks[5], (DIM, DIM), jnp.float32) * s, 'bk': jax.random.normal(ks[6], (DIM,), jnp.float32) * s, 'Wv': jax.random.normal(ks[7], (DIM, DIM), jnp.float32) * s, 'bv': jax.random.normal(ks[8], (DIM,), jnp.float32) * s, 'Wo': jax.random.normal(ks[9], (DIM, DIM), jnp.float32) * s, 'bo': jax.random.normal(ks[10], (DIM,), jnp.float32) * s}
    _L0_xattn_all = _L0_xattn_setup()
    _L0_xattn_in = {k: v for k, v in _L0_xattn_all.items() if k in ('Wq', 'bq', 'Wk', 'bk', 'Wv', 'bv', 'Wo', 'bo')}
    del _L0_xattn_all

    def _L0_ffn_setup():
        import jax, jax.numpy as jnp
        import numpy as np
        H = 128
        I = 64
        E = 8
        TOP_K = 2
        N_SHARED = 2
        SHARED_I = I * N_SHARED
        SCALE = 2.5
        NORM_TOPK = True
        B, S = (2, 128)

        def _swiglu(x, wg, wu, wd):
            g = x @ wg.T
            u = x @ wu.T
            return jax.nn.silu(g) * u @ wd.T
        key = jax.random.key(seed)
        ks = jax.random.split(key, 8)
        std = 0.02
        return {'hidden_states': jax.random.normal(ks[0], (B, S, H), jnp.float32), 'gate_weight': jax.random.normal(ks[1], (E, H), jnp.float32) * std, 'w_gate': jax.random.normal(ks[2], (E, I, H), jnp.float32) * std, 'w_up': jax.random.normal(ks[3], (E, I, H), jnp.float32) * std, 'w_down': jax.random.normal(ks[4], (E, H, I), jnp.float32) * std, 'ws_gate': jax.random.normal(ks[5], (SHARED_I, H), jnp.float32) * std, 'ws_up': jax.random.normal(ks[6], (SHARED_I, H), jnp.float32) * std, 'ws_down': jax.random.normal(ks[7], (H, SHARED_I), jnp.float32) * std}
    _L0_ffn_all = _L0_ffn_setup()
    _L0_ffn_in = {k: v for k, v in _L0_ffn_all.items() if k in ('gate_weight', 'w_gate', 'w_up', 'w_down', 'ws_gate', 'ws_up', 'ws_down')}
    del _L0_ffn_all

    def _L1_attn_setup():
        import jax, jax.numpy as jnp
        import numpy as np
        H = 8
        DIM = 128
        DH = DIM // H // 2
        B, N = (2, 256)
        LAMBDA_INIT = 0.5
        COS_MIN, COS_MAX = (0.0, 15.0)
        ALPHA = 0.5
        COS_EPS = 1e-06
        RMS_EPS = 1e-05
        RAW_INIT = float(np.log(1.0 / 15.0 / (1.0 - 1.0 / 15.0)))

        def _l2norm(t):
            return t / jnp.maximum(jnp.linalg.norm(t, axis=-1, keepdims=True), COS_EPS)
        key = jax.random.key(seed)
        ks = jax.random.split(key, 10)
        s = 1.0 / np.sqrt(DIM)
        return {'x': jax.random.normal(ks[0], (B, N, DIM), jnp.float32), 'Wq': jax.random.normal(ks[1], (DIM, DIM), jnp.float32) * s, 'Wk': jax.random.normal(ks[2], (DIM, DIM), jnp.float32) * s, 'Wv': jax.random.normal(ks[3], (DIM, DIM), jnp.float32) * s, 'Wo': jax.random.normal(ks[4], (DIM, DIM), jnp.float32) * s, 'bo': jnp.zeros((DIM,), jnp.float32), 'lambda_q1': jax.random.normal(ks[5], (DH,), jnp.float32) * 0.1, 'lambda_k1': jax.random.normal(ks[6], (DH,), jnp.float32) * 0.1, 'lambda_q2': jax.random.normal(ks[7], (DH,), jnp.float32) * 0.1, 'lambda_k2': jax.random.normal(ks[8], (DH,), jnp.float32) * 0.1, 'delta_gain': jax.random.normal(ks[9], (H,), jnp.float32) * 0.1, 'cos_head_delta': jnp.zeros((H,), jnp.float32), 'cos_logit_scale_raw': jnp.float32(RAW_INIT), 'subln_weight': jnp.ones((2 * DH,), jnp.float32)}
    _L1_attn_all = _L1_attn_setup()
    _L1_attn_in = {k: v for k, v in _L1_attn_all.items() if k in ('Wq', 'Wk', 'Wv', 'Wo', 'bo', 'lambda_q1', 'lambda_k1', 'lambda_q2', 'lambda_k2', 'delta_gain', 'cos_head_delta', 'cos_logit_scale_raw', 'subln_weight')}
    del _L1_attn_all

    def _L1_xattn_setup():
        import jax, jax.numpy as jnp
        import numpy as np
        DIM = 128
        HEADS = 16
        HEAD_DIM = DIM // HEADS
        key = jax.random.key(seed)
        ks = jax.random.split(key, 12)
        B, Tq, Tk = (2, 256, 256)
        inp = {'query': jax.random.normal(ks[0], (B, Tq, DIM), jnp.float32), 'key': jax.random.normal(ks[1], (B, Tk, DIM), jnp.float32), 'value': jax.random.normal(ks[2], (B, Tk, DIM), jnp.float32), 'mask': jax.random.randint(ks[3], (B, 1, Tq, Tk), 0, 2, jnp.int32), 'wq': jax.random.uniform(ks[4], (DIM, DIM), jnp.float32, -1.0, 1.0) * np.sqrt(6.0 / (2 * DIM)), 'wk': jax.random.uniform(ks[5], (DIM, DIM), jnp.float32, -1.0, 1.0) * np.sqrt(6.0 / (2 * DIM)), 'wv': jax.random.uniform(ks[6], (DIM, DIM), jnp.float32, -1.0, 1.0) * np.sqrt(6.0 / (2 * DIM)), 'wo': jax.random.uniform(ks[7], (DIM, DIM), jnp.float32, -1.0, 1.0) * np.sqrt(6.0 / (2 * DIM)), 'bq': jnp.zeros((DIM,), jnp.float32), 'bk': jnp.zeros((DIM,), jnp.float32), 'bv': jnp.zeros((DIM,), jnp.float32), 'bo': jnp.zeros((DIM,), jnp.float32)}
        return inp
    _L1_xattn_all = _L1_xattn_setup()
    _L1_xattn_in = {k: v for k, v in _L1_xattn_all.items() if k in ('wq', 'wk', 'wv', 'wo', 'bq', 'bk', 'bv', 'bo')}
    del _L1_xattn_all

    def _L1_ffn_setup():
        import jax, jax.numpy as jnp
        import numpy as np
        EPS = 1e-05

        def _quantize(W):
            gamma = jnp.mean(jnp.abs(W))
            return jnp.clip(jnp.round(W / (gamma + EPS)), -1.0, 1.0)
        key = jax.random.key(seed)
        k_x, k_w1, k_b1, k_w2, k_b2 = jax.random.split(key, 5)
        n_embd = 128
        d_ff = 4 * n_embd
        B, S = (4, 512)
        bound1 = 1.0 / np.sqrt(n_embd)
        bound2 = 1.0 / np.sqrt(d_ff)
        x = jax.random.normal(k_x, (B, S, n_embd), dtype=jnp.float32)
        W1 = jax.random.uniform(k_w1, (d_ff, n_embd), jnp.float32, -bound1, bound1)
        b1 = jax.random.uniform(k_b1, (d_ff,), jnp.float32, -bound1, bound1)
        W2 = jax.random.uniform(k_w2, (n_embd, d_ff), jnp.float32, -bound2, bound2)
        b2 = jax.random.uniform(k_b2, (n_embd,), jnp.float32, -bound2, bound2)
        return {'x': x, 'W1': W1, 'b1': b1, 'W2': W2, 'b2': b2}
    _L1_ffn_all = _L1_ffn_setup()
    _L1_ffn_in = {k: v for k, v in _L1_ffn_all.items() if k in ('W1', 'b1', 'W2', 'b2')}
    del _L1_ffn_all
    return {'x': x, 'ctx_1024': ctx_1024, 'mask_BxSxS2_bf0': mask_BxSxS2_bf0, 'mask_Bx1xSxS2_ik1': mask_Bx1xSxS2_ik1, 'L0_attn_nu_log': _L0_attn_in['nu_log'], 'L0_attn_theta_log': _L0_attn_in['theta_log'], 'L0_attn_gamma_log': _L0_attn_in['gamma_log'], 'L0_attn_B_re': _L0_attn_in['B_re'], 'L0_attn_B_im': _L0_attn_in['B_im'], 'L0_attn_C_re': _L0_attn_in['C_re'], 'L0_attn_C_im': _L0_attn_in['C_im'], 'L0_attn_D': _L0_attn_in['D'], 'L0_xattn_Wq': _L0_xattn_in['Wq'], 'L0_xattn_bq': _L0_xattn_in['bq'], 'L0_xattn_Wk': _L0_xattn_in['Wk'], 'L0_xattn_bk': _L0_xattn_in['bk'], 'L0_xattn_Wv': _L0_xattn_in['Wv'], 'L0_xattn_bv': _L0_xattn_in['bv'], 'L0_xattn_Wo': _L0_xattn_in['Wo'], 'L0_xattn_bo': _L0_xattn_in['bo'], 'L0_ffn_gate_weight': _L0_ffn_in['gate_weight'], 'L0_ffn_w_gate': _L0_ffn_in['w_gate'], 'L0_ffn_w_up': _L0_ffn_in['w_up'], 'L0_ffn_w_down': _L0_ffn_in['w_down'], 'L0_ffn_ws_gate': _L0_ffn_in['ws_gate'], 'L0_ffn_ws_up': _L0_ffn_in['ws_up'], 'L0_ffn_ws_down': _L0_ffn_in['ws_down'], 'L1_attn_Wq': _L1_attn_in['Wq'], 'L1_attn_Wk': _L1_attn_in['Wk'], 'L1_attn_Wv': _L1_attn_in['Wv'], 'L1_attn_Wo': _L1_attn_in['Wo'], 'L1_attn_bo': _L1_attn_in['bo'], 'L1_attn_lambda_q1': _L1_attn_in['lambda_q1'], 'L1_attn_lambda_k1': _L1_attn_in['lambda_k1'], 'L1_attn_lambda_q2': _L1_attn_in['lambda_q2'], 'L1_attn_lambda_k2': _L1_attn_in['lambda_k2'], 'L1_attn_delta_gain': _L1_attn_in['delta_gain'], 'L1_attn_cos_head_delta': _L1_attn_in['cos_head_delta'], 'L1_attn_cos_logit_scale_raw': _L1_attn_in['cos_logit_scale_raw'], 'L1_attn_subln_weight': _L1_attn_in['subln_weight'], 'L1_xattn_wq': _L1_xattn_in['wq'], 'L1_xattn_wk': _L1_xattn_in['wk'], 'L1_xattn_wv': _L1_xattn_in['wv'], 'L1_xattn_wo': _L1_xattn_in['wo'], 'L1_xattn_bq': _L1_xattn_in['bq'], 'L1_xattn_bk': _L1_xattn_in['bk'], 'L1_xattn_bv': _L1_xattn_in['bv'], 'L1_xattn_bo': _L1_xattn_in['bo'], 'L1_ffn_W1': _L1_ffn_in['W1'], 'L1_ffn_b1': _L1_ffn_in['b1'], 'L1_ffn_W2': _L1_ffn_in['W2'], 'L1_ffn_b2': _L1_ffn_in['b2']}

def reference(x, ctx_1024, mask_BxSxS2_bf0, mask_Bx1xSxS2_ik1, L0_attn_nu_log, L0_attn_theta_log, L0_attn_gamma_log, L0_attn_B_re, L0_attn_B_im, L0_attn_C_re, L0_attn_C_im, L0_attn_D, L0_xattn_Wq, L0_xattn_bq, L0_xattn_Wk, L0_xattn_bk, L0_xattn_Wv, L0_xattn_bv, L0_xattn_Wo, L0_xattn_bo, L0_ffn_gate_weight, L0_ffn_w_gate, L0_ffn_w_up, L0_ffn_w_down, L0_ffn_ws_gate, L0_ffn_ws_up, L0_ffn_ws_down, L1_attn_Wq, L1_attn_Wk, L1_attn_Wv, L1_attn_Wo, L1_attn_bo, L1_attn_lambda_q1, L1_attn_lambda_k1, L1_attn_lambda_q2, L1_attn_lambda_k2, L1_attn_delta_gain, L1_attn_cos_head_delta, L1_attn_cos_logit_scale_raw, L1_attn_subln_weight, L1_xattn_wq, L1_xattn_wk, L1_xattn_wv, L1_xattn_wo, L1_xattn_bq, L1_xattn_bk, L1_xattn_bv, L1_xattn_bo, L1_ffn_W1, L1_ffn_b1, L1_ffn_W2, L1_ffn_b2):
    import jax
    import jax.numpy as jnp

    def _L0_attn_ref(x, nu_log, theta_log, gamma_log, B_re, B_im, C_re, C_im, D):
        import jax, jax.numpy as jnp
        import numpy as np
        import math
        B_SZ, T, D_IN, D_OUT, N = (8, 512, 128, 128, 64)
        RMIN, RMAX, MAX_PHASE = (0.9, 1.0, 6.283)
        lam = jnp.exp(-jnp.exp(nu_log) + 1j * jnp.exp(theta_log))
        gamma = jnp.exp(gamma_log)
        Bmat = B_re + 1j * B_im
        Bu = jnp.einsum('bti,ni->btn', x.astype(Bmat.dtype), Bmat) * gamma
        A = jnp.broadcast_to(lam, Bu.shape)

        def combine(e1, e2):
            a1, b1 = e1
            a2, b2 = e2
            return (a1 * a2, a2 * b1 + b2)
        _, states = jax.lax.associative_scan(combine, (A, Bu), axis=1)
        Cmat = C_re + 1j * C_im
        y = jnp.einsum('btn,on->bto', states, Cmat).real + jnp.einsum('bti,oi->bto', x, D)
        return y

    def _L0_xattn_ref(query, key, value, mask, Wq, bq, Wk, bk, Wv, bv, Wo, bo):
        import jax, jax.numpy as jnp
        import numpy as np
        import math
        B, LQ, LK = (2, 256, 256)
        DIM = 128
        H = 16
        DH = DIM // H
        b = query.shape[0]

        def shape(x):
            return x.reshape(b, -1, H, DH).transpose(0, 2, 1, 3)
        q = shape(query @ Wq.T + bq)
        k = shape(key @ Wk.T + bk)
        v = shape(value @ Wv.T + bv)
        q = q / math.sqrt(DH)
        scores = jnp.einsum('bhqd,bhkd->bhqk', q, k).astype(jnp.float32)
        scores = jnp.where(mask[:, None, :, :], jnp.float32(-1e+18), scores)
        attn = jax.nn.softmax(scores, axis=-1).astype(q.dtype)
        context = jnp.einsum('bhqk,bhkd->bhqd', attn, v)
        context = context.transpose(0, 2, 1, 3).reshape(b, -1, H * DH)
        return context @ Wo.T + bo

    def _L0_ffn_ref(hidden_states, gate_weight, w_gate, w_up, w_down, ws_gate, ws_up, ws_down):
        import jax, jax.numpy as jnp
        import numpy as np
        H = 128
        I = 64
        E = 8
        TOP_K = 2
        N_SHARED = 2
        SHARED_I = I * N_SHARED
        SCALE = 2.5
        NORM_TOPK = True
        B, S = (2, 128)

        def _swiglu(x, wg, wu, wd):
            g = x @ wg.T
            u = x @ wu.T
            return jax.nn.silu(g) * u @ wd.T
        b, s, h = hidden_states.shape
        x = hidden_states.reshape(-1, h)
        shared_out = _swiglu(x, ws_gate, ws_up, ws_down)
        logits = x.astype(jnp.float32) @ gate_weight.astype(jnp.float32).T
        scores = jax.nn.sigmoid(logits)
        topk_w, topk_idx = jax.lax.top_k(scores, TOP_K)
        if TOP_K > 1 and NORM_TOPK:
            topk_w = topk_w / (topk_w.sum(-1, keepdims=True) + 1e-20)
        topk_w = topk_w * SCALE
        onehot = jax.nn.one_hot(topk_idx, E, dtype=topk_w.dtype)
        combine = jnp.einsum('tk,tke->te', topk_w, onehot)
        g = jnp.einsum('th,eih->tei', x, w_gate)
        u = jnp.einsum('th,eih->tei', x, w_up)
        hmid = jax.nn.silu(g) * u
        y = jnp.einsum('tei,ehi->teh', hmid, w_down)
        routed_out = jnp.einsum('te,teh->th', combine, y)
        out = (routed_out + shared_out).reshape(b, s, h)
        return out

    def _L1_attn_ref(x, Wq, Wk, Wv, Wo, bo, lambda_q1, lambda_k1, lambda_q2, lambda_k2, delta_gain, cos_head_delta, cos_logit_scale_raw, subln_weight):
        import jax, jax.numpy as jnp
        import numpy as np
        H = 8
        DIM = 128
        DH = DIM // H // 2
        B, N = (2, 256)
        LAMBDA_INIT = 0.5
        COS_MIN, COS_MAX = (0.0, 15.0)
        ALPHA = 0.5
        COS_EPS = 1e-06
        RMS_EPS = 1e-05
        RAW_INIT = float(np.log(1.0 / 15.0 / (1.0 - 1.0 / 15.0)))

        def _l2norm(t):
            return t / jnp.maximum(jnp.linalg.norm(t, axis=-1, keepdims=True), COS_EPS)
        b, n, c = x.shape
        q = (x @ Wq.T).reshape(b, n, H, 2, DH).transpose(0, 2, 3, 1, 4)
        k = (x @ Wk.T).reshape(b, n, H, 2, DH).transpose(0, 2, 3, 1, 4)
        v = (x @ Wv.T).reshape(b, n, H, 2 * DH).transpose(0, 2, 1, 3)
        q1, q2 = (q[:, :, 0], q[:, :, 1])
        k1, k2 = (k[:, :, 0], k[:, :, 1])
        gscale = COS_MIN + (COS_MAX - COS_MIN) * jax.nn.sigmoid(cos_logit_scale_raw)
        head_delta = cos_head_delta - cos_head_delta.mean()
        cos_scale = (gscale * (1.0 + ALPHA * jnp.tanh(head_delta))).reshape(1, H, 1, 1)
        L1 = jnp.einsum('bhnd,bhmd->bhnm', _l2norm(q1), _l2norm(k1)) * cos_scale
        L2 = jnp.einsum('bhnd,bhmd->bhnm', _l2norm(q2), _l2norm(k2)) * cos_scale
        L1 = jnp.nan_to_num(L1)
        L2 = jnp.nan_to_num(L2)
        G = jnp.tanh(delta_gain.reshape(1, H, 1, 1) * (L1 - L2))
        A1 = jax.nn.softmax((L1 + G).astype(jnp.float32), axis=-1).astype(x.dtype)
        A2 = jax.nn.softmax((L2 - G).astype(jnp.float32), axis=-1).astype(x.dtype)
        lambda_1 = jnp.exp(jnp.sum(lambda_q1 * lambda_k1))
        lambda_2 = jnp.exp(jnp.sum(lambda_q2 * lambda_k2))
        lambda_full = (lambda_1 - lambda_2 + LAMBDA_INIT).astype(x.dtype)
        attn = A1 - lambda_full * A2
        y = jnp.einsum('bhnm,bhmd->bhnd', attn, v)
        y = y * jax.lax.rsqrt(jnp.mean(y * y, axis=-1, keepdims=True) + RMS_EPS) * subln_weight
        y = y * (1.0 - LAMBDA_INIT)
        y = y.transpose(0, 2, 1, 3).reshape(b, n, c)
        return y @ Wo.T + bo

    def _L1_xattn_ref(query, key, value, mask, wq, wk, wv, wo, bq, bk, bv, bo):
        import jax, jax.numpy as jnp
        import numpy as np
        DIM = 128
        HEADS = 16
        HEAD_DIM = DIM // HEADS
        B, Tq, C = query.shape
        Tk = key.shape[1]
        scale = 1.0 / np.sqrt(HEAD_DIM)
        q = (query @ wq.T + bq).reshape(B, Tq, HEADS, HEAD_DIM).transpose(0, 2, 1, 3)
        k = (key @ wk.T + bk).reshape(B, Tk, HEADS, HEAD_DIM).transpose(0, 2, 1, 3)
        v = (value @ wv.T + bv).reshape(B, Tk, HEADS, HEAD_DIM).transpose(0, 2, 1, 3)
        scores = jnp.einsum('bhqd,bhkd->bhqk', q, k) * scale
        scores = jnp.clip(scores, -100.0, 100.0)
        scores = jnp.where(mask == 0, -jnp.inf, scores)
        attn = jax.nn.softmax(scores, axis=-1)
        out = jnp.einsum('bhqk,bhkd->bhqd', attn, v)
        out = out.transpose(0, 2, 1, 3).reshape(B, Tq, HEADS * HEAD_DIM)
        return out @ wo.T + bo

    def _L1_ffn_ref(x, W1, b1, W2, b2):
        import jax, jax.numpy as jnp
        import numpy as np
        EPS = 1e-05

        def _quantize(W):
            gamma = jnp.mean(jnp.abs(W))
            return jnp.clip(jnp.round(W / (gamma + EPS)), -1.0, 1.0)
        Wq1 = _quantize(W1)
        Wq2 = _quantize(W2)
        h = jax.nn.relu(jnp.einsum('bsd,fd->bsf', x, Wq1) + b1)
        out = jnp.einsum('bsf,df->bsd', h, Wq2) + b2
        return out
    x = x + _L0_attn_ref(_layernorm(x, axis=-1), L0_attn_nu_log, L0_attn_theta_log, L0_attn_gamma_log, L0_attn_B_re, L0_attn_B_im, L0_attn_C_re, L0_attn_C_im, L0_attn_D)
    x = x + _L0_xattn_ref(_layernorm(x, axis=-1), ctx_1024, ctx_1024, mask_BxSxS2_bf0, L0_xattn_Wq, L0_xattn_bq, L0_xattn_Wk, L0_xattn_bk, L0_xattn_Wv, L0_xattn_bv, L0_xattn_Wo, L0_xattn_bo)
    x = x + _L0_ffn_ref(_layernorm(x, axis=-1), L0_ffn_gate_weight, L0_ffn_w_gate, L0_ffn_w_up, L0_ffn_w_down, L0_ffn_ws_gate, L0_ffn_ws_up, L0_ffn_ws_down)
    x = x + _L1_attn_ref(_layernorm(x, axis=-1), L1_attn_Wq, L1_attn_Wk, L1_attn_Wv, L1_attn_Wo, L1_attn_bo, L1_attn_lambda_q1, L1_attn_lambda_k1, L1_attn_lambda_q2, L1_attn_lambda_k2, L1_attn_delta_gain, L1_attn_cos_head_delta, L1_attn_cos_logit_scale_raw, L1_attn_subln_weight)
    x = x + _L1_xattn_ref(_layernorm(x, axis=-1), ctx_1024, ctx_1024, mask_Bx1xSxS2_ik1, L1_xattn_wq, L1_xattn_wk, L1_xattn_wv, L1_xattn_wo, L1_xattn_bq, L1_xattn_bk, L1_xattn_bv, L1_xattn_bo)
    x = x + _L1_ffn_ref(_layernorm(x, axis=-1), L1_ffn_W1, L1_ffn_b1, L1_ffn_W2, L1_ffn_b2)
    return x

_drawn_inputs = setup_inputs


def setup_inputs(seed=0):
    import zlib

    import numpy as np

    out = dict(_drawn_inputs(seed))
    spreads = {'L1_attn_bo': (0.0, 0.526),
     'L1_attn_cos_head_delta': (0.0, 2.0),
     'L1_attn_subln_weight': (1.0, 0.6),
     'L1_xattn_bq': (0.0, 1.863),
     'L1_xattn_bk': (0.0, 2.0),
     'L1_xattn_bv': (0.0, 0.495),
     'L1_xattn_bo': (0.0, 0.485)}
    factors = {'L0_xattn_bq': 3.38,
     'L0_xattn_bk': 200.0,
     'L0_ffn_gate_weight': 8.0,
     'L0_ffn_w_gate': 8.0,
     'L0_ffn_w_up': 8.0,
     'L0_ffn_w_down': 8.0,
     'L0_ffn_ws_gate': 8.0,
     'L0_ffn_ws_up': 8.0,
     'L0_ffn_ws_down': 8.0,
     'L1_attn_lambda_q1': 200.0,
     'L1_attn_lambda_k1': 8.0,
     'L1_attn_lambda_q2': 47.192,
     'L1_attn_lambda_k2': 43.192,
     'L1_attn_delta_gain': 13.491,
     'L1_ffn_b1': 8.0,
     'L1_ffn_b2': 200.0}
    for name, (base, spread) in spreads.items():
        noise = np.random.default_rng([zlib.crc32(name.encode()), seed]).standard_normal(out[name].shape)
        drawn = base * np.exp(spread * noise) if base else spread * noise
        out[name] = jnp.asarray(drawn.astype(out[name].dtype))
    for name, factor in factors.items():
        out[name] = (out[name] * factor).astype(out[name].dtype)
    return out
```

```python
import numpy as np
import concourse.bass as bass
from concourse import mybir
from contextlib import ExitStack

F32 = mybir.dt.float32
BF16 = mybir.dt.bfloat16
I32 = mybir.dt.int32
U8 = mybir.dt.uint8
ALU = mybir.AluOpType
ACT = mybir.ActivationFunctionType
AX = mybir.AxisListType

B, T, D = 4, 512, 128
P = 128
NT = T // P
STREAMS = 2
NSTATE = 64
CTX = 32
XH, XD = 16, 8
HG = P // CTX
NG = XH // HG
XSCALE = 1.0 / float(np.sqrt(XD))
EXPERTS, EI = 8, 64
EPC = P // EI
RCH = EXPERTS // EPC
FCH = RCH + 1
ROUTE_SCALE = 2.5
AH, AD = 8, 8
MAPS = 2
HV = 2 * AD
F1CH = 4
LN_EPS = 1e-5
RMS_EPS = 1e-5
WARM_UP = 40
BIG = 3.0e38

WCOLS, _at = {}, 0
for _name, _n in [("bt1", 128), ("bt2", 128), ("wc1", 128), ("wc2", 128), ("dt", 128),
                  ("f1w1", 512), ("f1w2", 512),
                  ("x0q", 128), ("x0k", 128), ("x0v", 128), ("x0o", 128),
                  ("gate", EXPERTS), ("wg", FCH * P), ("wu", FCH * P), ("wd", FCH * P),
                  ("aqkv", 384), ("ao", 128),
                  ("x1q", 128), ("x1k", 128), ("x1v", 128), ("x1o", 128)]:
    WCOLS[_name] = (_at, _at + _n)
    _at += _n
WTOTAL = _at
COLS = {n: i for i, n in enumerate(["nu", "theta", "gamma", "bq0", "bk0", "bq1", "bk1",
                                    "b1_0", "b1_1", "b1_2", "b1_3"])}
ROWS, _at = {}, 0
for _name, _n in [("bv0", 128), ("bv1", 128), ("bo_x0", 128), ("bo_a", 128), ("bo_x1", 128), ("b2", 128),
                  ("gain", AH), ("head_delta", AH), ("raw", 1), ("lq1", AD), ("lk1", AD), ("lq2", AD),
                  ("lk2", AD), ("subln", HV)]:
    ROWS[_name] = (_at, _at + _n)
    _at += _n
RTOTAL = _at
QPART = (0, 0, 0, 1, 1, 2)
KPART = (0, 1, 2, 0, 1, 0)
RUNS = ((0, 3), (3, 2), (5, 1))
KROWS = len(QPART) * AD
MAP2 = 64


def build(nc, x_in, ctx_in, m0_in, m1_in, w_in, cols_in, rows_in, out):
    ctx = ExitStack()
    with ctx:
        def sb(name, shape, dt=F32):
            return ctx.enter_context(nc.sbuf_tensor(name, shape, dt))

        sems = {}

        def sig(name):
            if name not in sems:
                sems[name] = ctx.enter_context(nc.semaphore(name))
            return sems[name]

        wt = sb("wt", [P, WTOTAL])
        cols = sb("cols", [P, len(COLS)])
        rows = sb("rows", [P, RTOTAL])
        ident = sb("ident", [P, P])
        identb = sb("identb", [P, P], BF16)
        mask_k = sb("mask_k", [P, HG, CTX])
        mask_v = sb("mask_v", [P, NG, HG, XD])
        head_sum = sb("head_sum", [P, 32])
        expert_rows = sb("expert_rows", [3 * EXPERTS, RCH, P], BF16)
        lower = sb("lower", [P, NT, EXPERTS, EXPERTS])
        neg_half = sb("neg_half", [P, 32])
        rot_in_c = sb("rot_in_c", [P, T])
        rot_in_s = sb("rot_in_s", [P, T])
        rot_out_c = sb("rot_out_c", [P, T])
        rot_out_s = sb("rot_out_s", [P, T])
        decay = sb("decay", [P, 1])
        bq_scaled = sb("bq_scaled", [P, 2])
        lam = sb("lam", [P, 1])
        qscale = sb("qscale", [P, MAPS, AH])
        sub_half = sb("sub_half", [P, HV])

        def w(name):
            a, b = WCOLS[name]
            return wt[:, a:b]

        def wch(name, j):
            a, _ = WCOLS[name]
            return wt[:, a + j * P:a + (j + 1) * P]

        def col(name):
            return cols[:, COLS[name]:COLS[name] + 1]

        def row(name):
            a, b = ROWS[name]
            return rows[:, a:b]

        def per_stream(name, shape, dt=F32):
            return [sb(f"{name}{s}", shape, dt) for s in range(STREAMS)]

        x = per_stream("x", [P, NT, D])
        xn = per_stream("xn", [P, NT, D])
        xT = per_stream("xT", [P, T])
        bst = per_stream("bst", [P, NT, 6])
        mv = per_stream("mv", [P, NT, 2])
        rstd = per_stream("rstd", [P, NT])
        veps = per_stream("veps", [P, NT])
        big = per_stream("big", [P, 4, T])
        big2 = per_stream("big2", [P, 4, T])
        ctxT = per_stream("ctxT", [P, HG, CTX])
        key_blocks = [per_stream(f"key_blocks{l}", [P, HG, CTX]) for l in range(2)]
        val_blocks = [per_stream(f"val_blocks{l}", [P, NG, HG * XD]) for l in range(2)]
        m0 = per_stream("m0", [P, T], U8)
        m1 = per_stream("m1", [P, T], I32)
        cap = [per_stream(f"cap{l}", [P, T]) for l in range(2)]
        qT = per_stream("qT", [P, T])
        zT = per_stream("zT", [P, T])
        oT = per_stream("oT", [P, T])
        cT = per_stream("cT", [P, T])
        mx = per_stream("mx", [P, NG, T // 32])
        rz = per_stream("rz", [P, NT, NG, HG])
        sg = per_stream("sg", [P, NT, EXPERTS])
        top = per_stream("top", [P, NT, EXPERTS])
        cmpa = per_stream("cmpa", [P, NT, EXPERTS, EXPERTS])
        cmpb = per_stream("cmpb", [P, NT, EXPERTS, EXPERTS])
        rank = per_stream("rank", [P, NT, EXPERTS])
        wsum = per_stream("wsum", [P, NT])
        cpart = per_stream("cpart", [P, NT, 3, EXPERTS], BF16)
        cres = per_stream("cres", [P, NT, EXPERTS])
        combT = per_stream("combT", [3 * EXPERTS, T], BF16)
        ss = per_stream("ss", [P, NT, 4 * AH])
        qpart = per_stream("qpart", [P, 3, T], BF16)
        kpart = per_stream("kpart", [P, 3, T], BF16)
        qstack = per_stream("qstack", [P, AH, T], BF16)
        kstack = per_stream("kstack", [P, AH, T], BF16)
        vals = per_stream("vals", [P, NT, AH, 32])
        on = per_stream("on", [P, NT, AH * MAPS, 32])
        qkn = [o[:, 0:2, :, :].rearrange("p a h c -> p (a h c)").rearrange("p (t c) -> p t c", t=NT) for o in on]
        rzo = per_stream("rzo", [P, NT * AH, MAPS])
        ms = per_stream("ms", [P, NT * AH])
        peak = per_stream("peak", [P, 4, NT * AH])
        gate_t = sb("gate_t", [P, 2, 2, T])
        logit = [b[:, :, :].rearrange("p (h m) t -> p h m t", h=2) for b in big2]
        prob = [b[:, :, :].rearrange("p (h m) t -> p h m t", h=2) for b in big]

        parts_dram = nc.dram_tensor("parts", (STREAMS, 2, MAPS, 3, AH * AD, T), BF16, kind="Internal").ap()

        bank = [ctx.enter_context(nc.psum_tensor(f"bank{i}", [P, T], F32)) for i in range(2)]
        quad = ctx.enter_context(nc.psum_tensor("quad", [P, 2, MAPS, T], F32))
        pair = ctx.enter_context(nc.psum_tensor("pair", [P, 2, T], F32))

        def bk(s, i):
            return [[bank[0][:, :], quad[:, 0, 0, :], quad[:, 0, 1, :], pair[:, 0, :]],
                    [bank[1][:, :], quad[:, 1, 0, :], quad[:, 1, 1, :], pair[:, 1, :]]][s][i]

        def turn(k, s):
            return STREAMS * k + s + 1

        WSECT = [("w_lru", "bt1", "dt"), ("w_ffn1", "f1w1", "f1w2"), ("w_x0", "x0q", "x0o"),
                 ("w_ffn0", "gate", "wd"), ("w_attn", "aqkv", "ao"), ("w_x1", "x1q", "x1o")]

        tab_c, tab_s, tmp = big[0][:, 0, :], big[0][:, 1, :], big[0][:, 2, :]
        small = sb("small", [P, 64])
        smalli = sb("smalli", [P, 4], I32)
        expt = sb("expt", [P, 3, 4])
        expi = sb("expi", [P, 4], I32)
        zc = sb("zc", [P, 10])
        zs = sb("zs", [P, 10])
        ones_sq = sb("ones_sq", [P, P])

        def prologue():
            with nc.Block() as block:
                @block.sync
                def _(sp):
                    sp.dma_start(cols[:, :], cols_in).then_inc(sig("cols_loaded"), 16)
                    for name, a, b in WSECT[:3]:
                        c0, c1 = WCOLS[a][0], WCOLS[b][1]
                        sp.dma_start(wt[:, c0:c1], w_in[:, c0:c1]).then_inc(sig(name), 16)

                @block.scalar
                def _(act):
                    act.dma_start(rows[:, :], rows_in.partition_broadcast(P)).then_inc(sig("rows_loaded"), 16)
                    for name, a, b in WSECT[3:]:
                        c0, c1 = WCOLS[a][0], WCOLS[b][1]
                        act.dma_start(wt[:, c0:c1], w_in[:, c0:c1]).then_inc(sig(name), 16)
                    act.wait_ge(sig("rows_loaded"), 16)
                    act.activation(small[:, 20:21], row("raw"), ACT.Exp, scale=-1.0).then_inc(sig("raw_exp"), 1)
                    act.wait_ge(sig("lambda_sums"), 2)
                    act.activation(small[:, 24:26], small[:, 22:24], ACT.Exp).then_inc(sig("lambda_exp"), 1)
                    act.wait_ge(sig("head_delta"), 1)
                    act.activation(small[:, 32:40], small[:, 40:48], ACT.Tanh).then_inc(sig("head_tanh"), 1)
                    act.wait_ge(sig("angles"), 1)
                    act.activation(small[:, 10:12], small[:, 8:10], ACT.Sin).then_inc(sig("sincos"), 1)

                @block.tensor
                def _(pe):
                    pe.wait_ge(sig("ones"), 1)
                    pe.wait_ge(sig("abs_sums"), 1)
                    pe.matmul(bank[0][:, 0:2], ones_sq[:, :], small[:, 50:52], start=True, stop=True) \
                        .then_inc(sig("abs_total"), 1)

                @block.gpsimd
                def _(pool):
                    n = [0]

                    def link(ins):
                        n[0] += 1
                        ins.then_inc(sig("pool_link0"), 1)
                        pool.wait_ge(sig("pool_link0"), n[0])

                    pool.memset(ones_sq[:, :], 1.0).then_inc(sig("ones"), 1)
                    link(pool.memset(ident[:, :], 0.0))
                    link(pool.affine_select(out=ident[:, :], in_=ident[:, :], compare_op=ALU.not_equal,
                                            fill=1.0, base=0, pattern=[[-1, P]], channel_multiplier=1))
                    link(pool.tensor_copy(identb[:, :], ident[:, :]))
                    link(pool.memset(neg_half[:, :], -0.5))
                    link(pool.memset(mask_k[:, :, :], 1.0))
                    for g in range(NG):
                        m = mask_k[32 * g:32 * g + 32, :, :]
                        link(pool.affine_select(out=m, in_=m, compare_op=ALU.is_ge, fill=0.0, base=0,
                                                pattern=[[-XD, HG], [0, CTX]], channel_multiplier=1))
                        link(pool.affine_select(out=m, in_=m, compare_op=ALU.is_ge, fill=0.0, base=XD - 1,
                                                pattern=[[XD, HG], [0, CTX]], channel_multiplier=-1))
                    link(pool.memset(mask_v[:, :, :, :], 0.0))
                    link(pool.memset(head_sum[:, :], 0.0))
                    for h in range(HG):
                        link(pool.memset(mask_v[32 * h:32 * h + 32, :, h, :], 1.0))
                        link(pool.memset(head_sum[32 * h:32 * h + 32, h:h + 1], 1.0))
                    link(pool.memset(expert_rows[:, :, :], 0.0))
                    er = expert_rows[:, :, :].rearrange("r j (e i) -> r j e i", e=EPC)
                    for p in range(3):
                        link(pool.affine_select(out=er, in_=er, compare_op=ALU.not_equal, fill=1.0,
                                                base=-EXPERTS * p, pattern=[[-EPC, RCH], [-1, EPC], [0, EI]],
                                                channel_multiplier=1))
                    link(pool.memset(lower[:, :, :, :], 1.0))
                    link(pool.affine_select(out=lower[:, :, :, :], in_=lower[:, :, :, :], compare_op=ALU.is_gt,
                                            fill=0.0, base=0, pattern=[[0, NT], [1, EXPERTS], [-1, EXPERTS]],
                                            channel_multiplier=0))
                    for s in range(STREAMS):
                        link(pool.memset(vals[s][:, :, :, HV:32], 1.0))
                        link(pool.memset(qstack[s][32:64, :, :], 0.0))
                        link(pool.memset(kstack[s][32:64, :, :], 0.0))

                @block.vector
                def _(dve):
                    n = [0]

                    def link(ins):
                        n[0] += 1
                        ins.then_inc(sig("dve_link0"), 1)
                        dve.wait_ge(sig("dve_link0"), n[0])

                    def exp(dst, src, width, negate):
                        z, q, r = (expt[:, a, 0:width] for a in range(3))
                        sign = -1.0 if negate else 1.0
                        link(dve.tensor_scalar(z, src, sign * float(np.log2(np.e)), 127.0, ALU.mult, ALU.min))
                        link(dve.tensor_scalar(z, z, -126.0, None, ALU.max))
                        link(dve.tensor_copy(expi[:, 0:width], z))
                        link(dve.tensor_copy(z, expi[:, 0:width]))
                        link(dve.tensor_scalar(r, src, sign, None, ALU.mult))
                        for part in (0.693359375, -2.12194440e-4):
                            link(dve.scalar_tensor_tensor(r, z, -part, r, ALU.mult, ALU.add))
                        link(dve.tensor_scalar(q, r, 1.0 / 5040, None, ALU.mult))
                        for c in (720, 120, 24, 6, 2, 1):
                            link(dve.scalar_tensor_tensor(q, q, 1.0 / c, r, ALU.add, ALU.mult))
                        link(dve.tensor_scalar(z, z, 127.0, float(1 << 23), ALU.add, ALU.mult))
                        link(dve.tensor_copy(expi[:, 0:width], z))
                        link(dve.scalar_tensor_tensor(dst, q, 1.0, expi[:, 0:width].bitcast(F32), ALU.add, ALU.mult))

                    dve.wait_ge(sig("cols_loaded"), 16)
                    a = COLS["nu"]
                    exp(small[:, 0:3], cols[:, a:a + 3], 3, False)
                    exp(decay[:, :], small[:, 0:1], 1, True)
                    link(dve.tensor_scalar(small[:, 3:4], small[:, 1:2], float(1 / (2 * np.pi)), None, ALU.mult))
                    link(dve.tensor_copy(smalli[:, 0:1], small[:, 3:4]))
                    link(dve.tensor_copy(small[:, 4:5], smalli[:, 0:1]))
                    c1 = 6.28125
                    c2 = float(np.float32(2 * np.pi - c1))
                    link(dve.scalar_tensor_tensor(small[:, 5:6], small[:, 4:5], -c1, small[:, 1:2], ALU.mult, ALU.add))
                    link(dve.scalar_tensor_tensor(small[:, 5:6], small[:, 4:5], -c2, small[:, 5:6], ALU.mult, ALU.add))
                    pi = float(np.float32(np.pi))
                    for op, lim, step in ((ALU.is_gt, pi, -2 * np.pi), (ALU.is_lt, -pi, 2 * np.pi)):
                        link(dve.tensor_scalar(small[:, 6:7], small[:, 5:6], lim, float(step), op, ALU.mult))
                        link(dve.tensor_tensor(small[:, 5:6], small[:, 5:6], small[:, 6:7], ALU.add))
                    below = float(np.nextafter(np.float32(np.pi), np.float32(0)))
                    link(dve.tensor_scalar(small[:, 8:9], small[:, 5:6], below, -below, ALU.min, ALU.max))
                    link(dve.tensor_scalar(small[:, 6:7], small[:, 8:9], -1.0, None, ALU.mult))
                    link(dve.tensor_tensor(small[:, 6:7], small[:, 6:7], small[:, 8:9], ALU.max))
                    dve.tensor_scalar(small[:, 9:10], small[:, 6:7], -1.0, float(np.pi / 2), ALU.mult, ALU.add) \
                        .then_inc(sig("angles"), 1)
                    dve.wait_ge(sig("rows_loaded"), 16)
                    for i, (a, b) in enumerate((("lq1", "lk1"), ("lq2", "lk2"))):
                        link(dve.tensor_tensor(tmp[:, i * AD:(i + 1) * AD], row(a), row(b), ALU.mult))
                        dve.tensor_reduce(small[:, 22 + i:23 + i], tmp[:, i * AD:(i + 1) * AD], AX.X, ALU.add) \
                            .then_inc(sig("lambda_sums"), 1)
                    link(dve.tensor_reduce(small[:, 31:32], row("head_delta"), AX.X, ALU.add))
                    link(dve.tensor_scalar(small[:, 31:32], small[:, 31:32], 1.0 / AH, None, ALU.mult))
                    dve.tensor_scalar(small[:, 40:48], row("head_delta"), small[:, 31:32], None, ALU.subtract) \
                        .then_inc(sig("head_delta"), 1)
                    dve.wait_ge(sig("lambda_exp"), 1)
                    link(dve.tensor_tensor(lam[:, :], small[:, 24:25], small[:, 25:26], ALU.subtract))
                    link(dve.tensor_scalar(lam[:, :], lam[:, :], 0.5, None, ALU.add))
                    dve.wait_ge(sig("raw_exp"), 1)
                    link(dve.tensor_scalar(small[:, 21:22], small[:, 20:21], 1.0, None, ALU.add))
                    link(dve.reciprocal(small[:, 20:21], small[:, 21:22]))
                    link(dve.tensor_scalar(small[:, 21:22], small[:, 20:21], 15.0, None, ALU.mult))
                    dve.wait_ge(sig("head_tanh"), 1)
                    link(dve.tensor_scalar(small[:, 32:40], small[:, 32:40], 0.5, 1.0, ALU.mult, ALU.add))
                    dve.tensor_scalar(qscale[:, 0, :], small[:, 32:40], small[:, 21:22], None, ALU.mult)
                    dve.tensor_scalar(qscale[:, 1, :], small[:, 32:40], small[:, 21:22], -1.0, ALU.mult, ALU.mult)
                    dve.tensor_scalar(sub_half[:, :], row("subln"), 0.5, None, ALU.mult)
                    for l in range(2):
                        dve.tensor_scalar(bq_scaled[:, l:l + 1], col(f"bq{l}"), XSCALE, None, ALU.mult)
                    dve.wait_ge(sig("w_ffn1"), 16)
                    dve.tensor_reduce(small[:, 50:51], w("f1w1"), AX.X, ALU.add, apply_absolute_value=True)
                    dve.tensor_reduce(small[:, 51:52], w("f1w2"), AX.X, ALU.add, apply_absolute_value=True) \
                        .then_inc(sig("abs_sums"), 1)
                    dve.memset(tab_c[:, 0:1], 1.0)
                    link(dve.memset(tab_s[:, 0:1], 0.0))
                    dve.wait_ge(sig("sincos"), 1)
                    dve.tensor_copy(zs[:, 0:1], small[:, 10:11])
                    link(dve.tensor_copy(zc[:, 0:1], small[:, 11:12]))
                    steps = T.bit_length() - 1
                    for k in range(steps):
                        m = 1 << k
                        c, sn = zc[:, k:k + 1], zs[:, k:k + 1]
                        dve.tensor_scalar(tmp[:, 0:m], tab_s[:, 0:m], sn, None, ALU.mult)
                        if k < steps - 1:
                            dve.tensor_tensor(small[:, 12:13], sn, sn, ALU.mult)
                            dve.scalar_tensor_tensor(zs[:, k + 1:k + 2], c, 2.0, sn, ALU.mult, ALU.mult)
                        link(dve.tensor_scalar(tmp[:, 256:256 + m], tab_s[:, 0:m], c, None, ALU.mult))
                        dve.scalar_tensor_tensor(tab_c[:, m:2 * m], tab_c[:, 0:m], c, tmp[:, 0:m], ALU.mult, ALU.subtract)
                        if k < steps - 1:
                            dve.scalar_tensor_tensor(zc[:, k + 1:k + 2], c, c, small[:, 12:13], ALU.mult, ALU.subtract)
                        link(dve.scalar_tensor_tensor(tab_s[:, m:2 * m], tab_c[:, 0:m], sn, tmp[:, 256:256 + m],
                                                      ALU.mult, ALU.add))
                    lo, hi = slice(0, NSTATE), slice(NSTATE, P)
                    dve.tensor_scalar(rot_in_c[:, :], tab_c[:, :], small[:, 2:3], None, ALU.mult)
                    dve.tensor_scalar(rot_in_s[lo, :], tab_s[lo, :], small[lo, 2:3], None, ALU.mult)
                    dve.tensor_scalar(rot_in_s[hi, :], tab_s[hi, :], small[hi, 2:3], -1.0, ALU.mult, ALU.mult)
                    dve.tensor_copy(rot_out_c[lo, :], tab_c[lo, :])
                    dve.tensor_scalar(rot_out_c[hi, :], tab_c[hi, :], -1.0, None, ALU.mult)
                    dve.tensor_scalar(rot_out_s[:, :], tab_s[:, :], -1.0, None, ALU.mult)
                    dve.wait_ge(sig("abs_total"), 1)
                    inv = 1.0 / (4 * P * P)
                    link(dve.tensor_scalar(small[:, 52:54], bank[0][:, 0:2], inv, 1e-5, ALU.mult, ALU.add))
                    link(dve.tensor_scalar(small[:, 54:56], small[:, 52:54], 0.5, None, ALU.mult))
                    link(dve.tensor_scalar(small[:, 56:58], small[:, 54:56], -1.0, None, ALU.mult))
                    for i, name in enumerate(("f1w1", "f1w2")):
                        link(dve.tensor_scalar(tmp[:, :], w(name), small[:, 56 + i:57 + i], None, ALU.is_lt))
                        link(dve.scalar_tensor_tensor(w(name), w(name), small[:, 54 + i:55 + i], tmp[:, :],
                                                      ALU.is_gt, ALU.subtract))

        prologue()
        keep = set(sems)
        outer_count = {}

        def body(i):
            with nc.Block() as block:
                def spill(queue, s, which):
                    name = ("q", "k")[which]
                    queue.wait_ge(sig(f"{name}parts"), s + 1)
                    for m in range(MAPS):
                        queue.dma_start(parts_dram[s, which, m].rearrange("c r t -> r c t"),
                                        (qpart, kpart)[which][s][AH * AD * m:AH * AD * (m + 1), :, :]) \
                            .then_inc(sig(f"{name}_spilled{s}"), 16)

                def restack(queue, s, which):
                    stack, part = ((qstack, QPART), (kstack, KPART))[which]
                    queue.wait_ge(sig(f"{('q', 'k')[which]}_spilled{s}"), 16 * MAPS)
                    for m in range(MAPS):
                        src = parts_dram[s, which, m].rearrange("c (r h) t -> c r (h t)", h=AH)
                        for c, n in RUNS:
                            run = src[0:n] if which else src[part[c]:part[c] + 1].broadcast_to([n, AD, AH * T])
                            to = MAP2 * m + AD * c
                            queue.dma_start(stack[s][to:to + AD * n, :, :], run) \
                                .then_inc(sig(f"stacked{s}"), 16)

                @block.sync
                def _(sp):
                    for s in range(STREAMS):
                        b = bass.ds(i * STREAMS + s, 1)
                        sp.dma_start(x[s][:, :, :], x_in[b].rearrange("b (t p) d -> p (b t) d", p=P)) \
                            .then_inc(sig(f"x_loaded{s}"), 16)
                    for s in range(STREAMS):
                        b = bass.ds(i * STREAMS + s, 1)
                        for h in range(HG):
                            r = slice(32 * h, 32 * h + 32)
                            sp.dma_start(ctxT[s][:, h, :], ctx_in[b].rearrange("b d k -> d (b k)")) \
                                .then_inc(sig(f"ctx_loaded{s}"), 16)
                            sp.dma_start(m0[s][r, :], m0_in[b].rearrange("b k q -> k (b q)")) \
                                .then_inc(sig(f"masks_loaded{s}"), 16)
                            sp.dma_start(m1[s][r, :], m1_in[b].rearrange("b k q -> k (b q)")) \
                                .then_inc(sig(f"masks_loaded{s}"), 16)
                    for s in range(STREAMS):
                        for which in range(2):
                            spill(sp, s, which)
                        for which in range(2 if s else 1):
                            restack(sp, s, which)
                    for s in range(STREAMS):
                        sp.wait_ge(sig("x_done"), turn(5, s))
                        b = bass.ds(i * STREAMS + s, 1)
                        sp.dma_start(out[b].rearrange("b (t p) d -> p (b t) d", p=P), x[s][:, :, :]) \
                            .then_inc(sig("stored"), 16)
                    sp.wait_ge(sig("stored"), 16 * STREAMS)

                @block.gpsimd
                def _(pool):
                    n = [0]

                    def link(ins):
                        n[0] += 1
                        ins.then_inc(sig("pool_link"), 1)
                        pool.wait_ge(sig("pool_link"), n[0])

                    def rstds(k):
                        for s in range(STREAMS):
                            pool.wait_ge(sig("moments"), turn(k, s))
                            link(pool.tensor_scalar(veps[s][:, :], mv[s][:, :, 1], LN_EPS, None, ALU.add))
                            pool.tensor_tensor(rstd[s][:, :], veps[s][:, :], neg_half[:, 0:NT], ALU.pow) \
                                .then_inc(sig("rstd_ready"), 1)

                    def biases(k, bias):
                        for s in range(STREAMS):
                            pool.wait_ge(sig("xn_ready"), turn(k, s))
                            pool.tensor_tensor(x[s][:, :, :], x[s][:, :, :],
                                               row(bias).unsqueeze(1).broadcast_to([P, NT, D]), ALU.add) \
                                .then_inc(sig(f"biased{k}"), 1)

                    def recurrence():
                        for s in range(STREAMS):
                            pool.wait_ge(sig("rotated_in"), s + 1)
                            pool.tensor_tensor(big[s][:, 0, :], big[s][:, 0, :], big[s][:, 1, :], ALU.add) \
                                .then_inc(sig("scan_input"), 1)
                        for s in range(STREAMS):
                            pool.wait_ge(sig("scanned"), s + 1)
                            pool.tensor_tensor(big2[s][:, 1, :], big[s][:, 2, :], rot_out_s[:, :], ALU.mult) \
                                .then_inc(sig("rotated_out_s"), 1)

                    def caps0(s):
                        pool.wait_ge(sig(f"masks_loaded{s}"), 16 * 2 * HG)
                        pool.tensor_scalar(cap[0][s][:, :], m0[s][:, :], 0.0, BIG, ALU.is_equal, ALU.mult)
                        link(pool.tensor_scalar(zT[s][:, :], m0[s][:, :], -1.0e18, None, ALU.mult))
                        pool.tensor_tensor(cap[0][s][:, :], cap[0][s][:, :], zT[s][:, :], ALU.add) \
                            .then_inc(sig("caps0"), 1)

                    def caps1(s):
                        link(pool.tensor_scalar(cap[1][s][:, :], m1[s][:, :], 0.0, -BIG, ALU.is_equal, ALU.mult))
                        pool.tensor_scalar(cap[1][s][:, :], cap[1][s][:, :], 100.0, None, ALU.add) \
                            .then_inc(sig("caps1"), 1)

                    def cross(l):
                        for g in range(NG):
                            for s in range(STREAMS):
                                pool.wait_ge(sig("max_spread"), (l * NG + g) * STREAMS + s + 1)
                                pool.tensor_tensor(big[s][:, g, :], big[s][:, g, :], big2[s][:, g, :],
                                                   ALU.subtract).then_inc(sig("shifted"), 1)

                    def experts():
                        for s in range(STREAMS):
                            pool.wait_ge(sig("compared"), s + 1)
                            link(pool.tensor_tensor(cmpb[s][:, :, :, :], cmpb[s][:, :, :, :], lower[:, :, :, :], ALU.mult))
                            pool.tensor_tensor(cmpa[s][:, :, :, :], cmpa[s][:, :, :, :], cmpb[s][:, :, :, :], ALU.add) \
                                .then_inc(sig("beaten_by"), 1)

                    def attention_end(s):
                        pool.wait_ge(sig("mean_square"), s + 1)
                        pool.tensor_tensor(rzo[s][:, :, 0], ms[s][:, :], neg_half[:, 0:NT * AH], ALU.pow) \
                            .then_inc(sig("head_rstd"), 1)

                    rstds(0)
                    for s in range(STREAMS):
                        caps0(s)
                    recurrence()
                    rstds(1)
                    biases(1, "bo_x0")
                    cross(0)
                    rstds(2)
                    experts()
                    rstds(3)
                    biases(3, "bo_a")
                    for s in range(STREAMS):
                        caps1(s)
                    for s in range(STREAMS):
                        attention_end(s)
                    rstds(4)
                    biases(4, "bo_x1")
                    cross(1)
                    rstds(5)
                    biases(5, "b2")

                @block.scalar
                def _(act):
                    def turn_out(k, s):
                        act.wait_ge(sig("xn_turned"), turn(k, s))
                        act.activation(xT[s][:, :], bk(s, 0), ACT.Copy).then_inc(sig("xT_ready"), 1)

                    def cross(l):
                        for s in range(STREAMS):
                            act.wait_ge(sig("q_made"), turn(l, s))
                            act.activation(qT[s][:, :], bk(s, 1), ACT.Identity, scale=XSCALE,
                                           bias=bq_scaled[:, l:l + 1]).then_inc(sig("q_ready"), 1)
                        for g in range(NG):
                            for s in range(STREAMS):
                                act.wait_ge(sig("shifted"), (l * NG + g) * STREAMS + s + 1)
                                act.activation(big[s][:, g, :], big[s][:, g, :], ACT.Exp).then_inc(sig("weights"), 1)
                        for s in range(STREAMS):
                            act.wait_ge(sig("weighed"), turn(l, s))
                            act.activation(zT[s][:, :], bk(s, 0), ACT.Copy).then_inc(sig("z_out"), 1)
                            act.activation(oT[s][:, :], bk(s, 1), ACT.Copy).then_inc(sig("o_out"), 1)
                        for s in range(STREAMS):
                            act.wait_ge(sig("rz_ready"), turn(l, s))
                            act.activation(zT[s][:, :].rearrange("p (h d) -> p h d", d=XD),
                                           rz[s][:, :, :, :].rearrange("p t g h -> p (t g h)").unsqueeze(2)
                                           .broadcast_to([P, NT * XH, XD]), ACT.Copy).then_inc(sig("rz_wide"), 1)

                    for s in range(STREAMS):
                        turn_out(0, s)
                    for s in range(STREAMS):
                        turn_out(1, s)
                    cross(0)
                    for s in range(STREAMS):
                        turn_out(2, s)
                    for s in range(STREAMS):
                        act.wait_ge(sig("gate_logits"), s + 1)
                        act.activation(sg[s][:, :, :], bk(s, 1)[:, 0:NT * EXPERTS].rearrange("p (t e) -> p t e", t=NT),
                                       ACT.Exp, scale=-1.0).then_inc(sig("gate_exp"), 1)
                    for s in range(STREAMS):
                        act.wait_ge(sig("comb_turned"), s + 1)
                        act.activation(combT[s][:, :], bk(s, 3).bitcast(BF16)[0:3 * EXPERTS, 0:T], ACT.Copy) \
                            .then_inc(sig("combT_ready"), 1)
                    for j in range(FCH):
                        for s in range(STREAMS):
                            act.wait_ge(sig("gated"), turn(j, s))
                            if j >= 2:
                                act.wait_ge(sig("hidden"), turn(j - 2, s))
                            act.activation(big[s][:, j % 2, :], bk(s, 1), ACT.Tanh, scale=0.5) \
                                .then_inc(sig("gate_tanh"), 1)
                    for s in range(STREAMS):
                        turn_out(3, s)
                    for s in range(STREAMS):
                        for t in range(NT):
                            act.wait_ge(sig("qkv_made"), s * NT + t + 1)
                            act.activation(big[s][:, t // 2, 256 * (t % 2):256 * (t % 2) + 256], bk(s, t)[:, 0:256],
                                           ACT.Square).then_inc(sig("squares"), 1)
                            act.activation(vals[s][:, t, :, 0:HV],
                                           bk(s, t)[:, 256:384].rearrange("p (h d) -> p h d", h=AH),
                                           ACT.Copy).then_inc(sig("vals_ready"), 1)
                    for s in range(STREAMS):
                        act.wait_ge(sig("square_sums"), s + 1)
                        act.activation(ss[s][:, :, :], ss[s][:, :, :], ACT.Sqrt).then_inc(sig("lengths"), 1)
                    for s in range(STREAMS):
                        for name, part, b, got in (("q1", qpart, 1, "q_turned"), ("k1", kpart, 2, "k_turned")):
                            act.wait_ge(sig(got), s + 1)
                            act.activation(part[s][:, 0, :], bk(s, b), ACT.Copy).then_inc(sig(name), 1)
                        for name, part, a in (("q", qpart, 0), ("k", kpart, 1)):
                            act.wait_ge(sig(f"{name}_rest"), s + 1)
                            act.activation(part[s][:, 1, :], big2[s][:, a, :], ACT.Copy).then_inc(sig(f"{name}2"), 1)
                    restack(act, 0, 1)

                    def difference(s, u):
                        n = s * 16 + u
                        hp = u // 4
                        for hh in range(2):
                            act.wait_ge(sig("diff_made"), 2 * n + hh + 1)
                            if n >= 2:
                                act.wait_ge(sig("logits_made"), 2 * (n - 2) + hh + 1)
                            h = 2 * hp + hh
                            a, _ = ROWS["gain"]
                            act.activation(gate_t[:, n % 2, hh, :], pair[:, hh, :], ACT.Tanh,
                                           scale=rows[:, a + h:a + h + 1]).then_inc(sig("gate_ready"), 1)

                    def exps(s, u):
                        n = s * 16 + u
                        act.wait_ge(sig("logits_made"), 2 * n + 2)
                        if n >= 2:
                            act.wait_ge(sig("unit_used"), n - 1)
                        for m in range(MAPS):
                            act.activation(prob[n % 2][:, :, m, :], logit[n % 2][:, :, m, :], ACT.Exp,
                                           scale=1.0 if m == 0 else -1.0).then_inc(sig("prob_ready"), 1)

                    def heads_out(s, hp):
                        act.wait_ge(sig("unit_used"), s * 16 + 4 * hp + 4)
                        if s * 4 + hp >= 1:
                            act.wait_ge(sig("heads_turned"), s * 4 + hp)
                        act.activation(oT[0][:, :], bank[0][:, :], ACT.Copy).then_inc(sig("heads_out"), 1)

                    def heads_in(s, hp):
                        act.wait_ge(sig("heads_turned"), s * 4 + hp + 1)
                        act.activation(on[s][:, :, 4 * hp:4 * hp + 4, :].rearrange("p t h d -> p t (h d)"),
                                       bank[1][:, :].rearrange("p (t c) -> p t c", t=NT),
                                       ACT.Copy).then_inc(sig("heads_in"), 1)

                    for s in range(STREAMS):
                        for u in range(16):
                            if u == 0:
                                difference(s, 0)
                            if u < 15:
                                difference(s, u + 1)
                            exps(s, u)
                            if u % 4 == 0 and u:
                                heads_out(s, u // 4 - 1)
                            if u % 4 == 2 and u > 4:
                                heads_in(s, u // 4 - 1)
                        heads_out(s, 3)
                        heads_in(s, 3)
                    for s in range(STREAMS):
                        act.wait_ge(sig("y_turned"), s + 1)
                        act.activation(cT[s][:, :], bk(s, 1), ACT.Copy).then_inc(sig("y_ready"), 1)

                    for s in range(STREAMS):
                        turn_out(4, s)
                    cross(1)
                    for s in range(STREAMS):
                        turn_out(5, s)
                    for j in range(F1CH):
                        for s in range(STREAMS):
                            act.wait_ge(sig("f1_made"), turn(j, s))
                            act.activation(big[s][:, j, :], bk(s, 1 + j % 2), ACT.Relu, bias=col(f"b1_{j}")) \
                                .then_inc(sig("f1_hidden"), 1)

                @block.vector
                def _(dve):
                    n = [0]

                    def link(ins):
                        n[0] += 1
                        ins.then_inc(sig("dve_link"), 1)
                        dve.wait_ge(sig("dve_link"), n[0])

                    def moments(k, s):
                        if k == 0:
                            dve.wait_ge(sig(f"x_loaded{s}"), 16)
                        else:
                            dve.wait_ge(sig("x_done"), turn(k - 1, s))
                        for t in range(NT):
                            ins = dve.bn_stats(bst[s][:, t, :], x[s][:, t, :])
                        link(ins)
                        for t in range(NT):
                            ins = dve.bn_aggr(mv[s][:, t, :], bst[s][:, t, :])
                        ins.then_inc(sig("moments"), 1)

                    def normed(k):
                        for s in range(STREAMS):
                            dve.wait_ge(sig("rstd_ready"), turn(k, s))
                            if k:
                                dve.wait_ge(sig("xn_turned"), turn(k - 1, s))
                            for t in range(NT):
                                ins = dve.tensor_scalar(xn[s][:, t, :], x[s][:, t, :], mv[s][:, t, 0:1],
                                                        rstd[s][:, t:t + 1], ALU.subtract, ALU.mult)
                            ins.then_inc(sig("xn_ready"), 1)

                    def residual(k, s, b, made):
                        dve.wait_ge(sig(made), s + 1)
                        if k in (1, 3, 4, 5):
                            dve.wait_ge(sig(f"biased{k}"), s + 1)
                        dve.tensor_tensor(x[s][:, :, :], bk(s, b).rearrange("p (t d) -> p t d", t=NT),
                                          x[s][:, :, :], ALU.add).then_inc(sig("x_done"), 1)

                    def cross_blocks(l, s):
                        dve.wait_ge(sig("kv_made"), turn(l, s))
                        dve.scalar_tensor_tensor(key_blocks[l][s][:, :, :].rearrange("p h k -> p (h k)"),
                                                 bk(s, 2)[:, 0:P], col(f"bk{l}"),
                                                 mask_k[:, :, :].rearrange("p h k -> p (h k)"), ALU.add, ALU.mult)
                        vb = val_blocks[l][s][:, :, :].rearrange("p g c -> p (g c)")
                        link(dve.tensor_tensor(vb, bk(s, 3)[:, 0:P], row(f"bv{l}"), ALU.add))
                        dve.tensor_tensor(vb, vb, mask_v[:, :, :, :].rearrange("p g h d -> p (g h d)"), ALU.mult) \
                            .then_inc(sig("kv_blocks"), 1)

                    def cross(l):
                        low = -BIG if l == 0 else -100.0
                        for s in range(STREAMS):
                            cross_blocks(l, s)
                        for g in range(NG):
                            for s in range(STREAMS):
                                if g == 0:
                                    dve.wait_ge(sig(f"caps{l}"), s + 1)
                                dve.wait_ge(sig("scores_made"), (l * NG + g) * STREAMS + s + 1)
                                dve.scalar_tensor_tensor(big[s][:, g, :], bk(s, 2 + g % 2), low, cap[l][s][:, :],
                                                         ALU.max, ALU.min).then_inc(sig("capped"), 1)
                            for s in range(STREAMS):
                                dve.wait_ge(sig("capped"), (l * NG + g) * STREAMS + s + 1)
                                dve.tensor_reduce(mx[s][:, g, :], big[s][:, g, :].rearrange("p (j k) -> p j k", k=32),
                                                  AX.X, ALU.max, apply_transpose=True).then_inc(sig("max_found"), 1)
                            for s in range(STREAMS):
                                dve.wait_ge(sig("max_found"), (l * NG + g) * STREAMS + s + 1)
                                dve.transpose(big2[s][:, g, :].rearrange("p (j k) -> p j k", k=32),
                                              mx[s][:, g, :].unsqueeze(2).broadcast_to([P, T // 32, 32])) \
                                    .then_inc(sig("max_spread"), 1)

                    def cross_end(l, k):
                        for s in range(STREAMS):
                            dve.wait_ge(sig("z_turned"), turn(l, s))
                            dve.reciprocal(rz[s][:, :, :, :],
                                           bk(s, 2).rearrange("p (t g c) -> p t g c", t=NT, g=NG)[:, :, :, 0:HG]) \
                                .then_inc(sig("rz_ready"), 1)
                        for s in range(STREAMS):
                            dve.wait_ge(sig("rz_turned"), turn(l, s))
                            dve.wait_ge(sig("o_out"), turn(l, s))
                            dve.tensor_tensor(cT[s][:, :], bk(s, 3), oT[s][:, :], ALU.mult).then_inc(sig("ctx_ready"), 1)
                        for s in range(STREAMS):
                            residual(k, s, 1, f"cross_out{l}")

                    for s in range(STREAMS):
                        moments(0, s)
                    normed(0)
                    for s in range(STREAMS):
                        dve.wait_ge(sig("states_in"), s + 1)
                        dve.tensor_tensor(big[s][:, 0, :], bk(s, 1), rot_in_c[:, :], ALU.mult)
                        dve.tensor_tensor(big[s][:, 1, :], bk(s, 2), rot_in_s[:, :], ALU.mult) \
                            .then_inc(sig("rotated_in"), 1)
                    for s in range(STREAMS):
                        dve.wait_ge(sig("scan_input"), s + 1)
                        dve.tensor_tensor_scan(big[s][:, 2, :], decay[:, 0:1].broadcast_to([P, T]), big[s][:, 0, :],
                                               0.0, ALU.mult, ALU.add).then_inc(sig("scanned"), 1)
                    for s in range(STREAMS):
                        dve.wait_ge(sig("scanned"), s + 1)
                        dve.tensor_tensor(big2[s][:, 0, :], big[s][:, 2, :], rot_out_c[:, :], ALU.mult) \
                            .then_inc(sig("rotated_out_c"), 1)
                    for s in range(STREAMS):
                        residual(0, s, 3, "lru_out")
                        moments(1, s)
                    normed(1)
                    cross(0)
                    cross_end(0, 1)
                    for s in range(STREAMS):
                        moments(2, s)
                    normed(2)
                    for s in range(STREAMS):
                        dve.wait_ge(sig("gate_exp"), s + 1)
                        link(dve.tensor_scalar(sg[s][:, :, :], sg[s][:, :, :], 1.0, None, ALU.add))
                        dve.reciprocal(sg[s][:, :, :], sg[s][:, :, :]).then_inc(sig("gate_scores"), 1)
                    for s in range(STREAMS):
                        dve.wait_ge(sig("gate_scores"), s + 1)
                        sj = sg[s][:, :, :].unsqueeze(2).broadcast_to([P, NT, EXPERTS, EXPERTS])
                        se = sg[s][:, :, :].unsqueeze(3).broadcast_to([P, NT, EXPERTS, EXPERTS])
                        dve.tensor_tensor(cmpa[s][:, :, :, :], sj, se, ALU.is_gt)
                        dve.tensor_tensor(cmpb[s][:, :, :, :], sj, se, ALU.is_equal).then_inc(sig("compared"), 1)
                        for t in range(NT):
                            ins = dve.max(top[s][:, t, :], sg[s][:, t, :])
                        link(ins)
                        link(dve.scalar_tensor_tensor(wsum[s][:, :], top[s][:, :, 0], 1e-20, top[s][:, :, 1],
                                                      ALU.add, ALU.add))
                        link(dve.reciprocal(wsum[s][:, :], wsum[s][:, :]))
                        dve.wait_ge(sig("beaten_by"), s + 1)
                        link(dve.tensor_reduce(rank[s][:, :, :], cmpa[s][:, :, :, :], AX.X, ALU.add))
                        link(dve.tensor_scalar(rank[s][:, :, :], rank[s][:, :, :], 1.5, 0.5 * ROUTE_SCALE, ALU.is_lt, ALU.mult))
                        link(dve.tensor_tensor(cres[s][:, :, :], sg[s][:, :, :], rank[s][:, :, :], ALU.mult))
                        link(dve.tensor_tensor(cres[s][:, :, :], cres[s][:, :, :],
                                               wsum[s][:, :].unsqueeze(2).broadcast_to([P, NT, EXPERTS]), ALU.mult))
                        for p in range(3):
                            link(dve.tensor_copy(cpart[s][:, :, p, :], cres[s][:, :, :]))
                            if p < 2:
                                link(dve.tensor_tensor(cres[s][:, :, :], cres[s][:, :, :], cpart[s][:, :, p, :], ALU.subtract))
                        dve.tensor_copy(rank[s][:, 0, 0:1], wsum[s][:, 0:1]).then_inc(sig("comb_ready"), 1)
                    for j in range(FCH):
                        for s in range(STREAMS):
                            th, hid = big[s][:, j % 2, :], big2[s][:, j % 2, :]
                            dve.wait_ge(sig("gate_tanh"), turn(j, s))
                            if j >= 2:
                                dve.wait_ge(sig("down"), turn(j - 2, s))
                            link(dve.scalar_tensor_tensor(hid, th, 1.0, bk(s, 1), ALU.add, ALU.mult))
                            dve.wait_ge(sig("upped"), turn(j, s))
                            if j < RCH:
                                link(dve.tensor_tensor(hid, hid, bk(s, 2), ALU.mult))
                                dve.tensor_tensor(hid, hid, bk(s, 3), ALU.mult).then_inc(sig("hidden"), 1)
                            else:
                                dve.scalar_tensor_tensor(hid, hid, 0.5, bk(s, 2), ALU.mult, ALU.mult) \
                                    .then_inc(sig("hidden"), 1)
                    for s in range(STREAMS):
                        residual(2, s, 0, "ffn0_out")
                        moments(3, s)
                    normed(3)
                    for s in range(STREAMS):
                        dve.wait_ge(sig("squares"), NT * (s + 1))
                        dve.tensor_reduce(ss[s][:, :, :].rearrange("p t (b h) -> p (t b) h", h=AH),
                                          big[s][:, 0:2, :].rearrange("p a (b d h) -> p (a b) h d", d=AD, h=AH), AX.X, ALU.add) \
                            .then_inc(sig("square_sums"), 1)
                    for s in range(STREAMS):
                        dve.wait_ge(sig("lengths"), s + 1)
                        link(dve.tensor_scalar(ss[s][:, :, :], ss[s][:, :, :], 1e-6, None, ALU.max))
                        link(dve.reciprocal(ss[s][:, :, :], ss[s][:, :, :]))
                        link(dve.tensor_tensor(ss[s][:, :, 0:2 * AH], ss[s][:, :, 0:2 * AH],
                                               qscale[:, :, :].rearrange("p m h -> p (m h)").unsqueeze(1)
                                               .broadcast_to([P, NT, 2 * AH]), ALU.mult))
                        for t in range(NT):
                            split = "p (b d h) -> p b d h"
                            ins = dve.tensor_tensor(qkn[s][:, t, :].rearrange(split, d=AD, h=AH),
                                                    bk(s, t)[:, 0:256].rearrange(split, d=AD, h=AH),
                                                    ss[s][:, t, :].rearrange("p (b h) -> p b h", h=AH).unsqueeze(2)
                                                    .broadcast_to([P, 2 * MAPS, AD, AH]), ALU.mult)
                        ins.then_inc(sig("unit_vectors"), 1)
                    for s in range(STREAMS):
                        for src, part, b, got, gives in ((0, qpart, 1, "q1", "q_rest"), (1, kpart, 2, "k1", "k_rest")):
                            dve.wait_ge(sig(got), s + 1)
                            dve.tensor_tensor(big2[s][:, src, :], bk(s, b), part[s][:, 0, :], ALU.subtract) \
                                .then_inc(sig(gives), 1)
                        for name, part, a in (("q", qpart, 0), ("k", kpart, 1)):
                            dve.wait_ge(sig(f"{name}2"), s + 1)
                            dve.tensor_tensor(part[s][:, 2, :], big2[s][:, a, :], part[s][:, 1, :], ALU.subtract) \
                                .then_inc(sig(f"{name}parts"), 1)

                    def logits(s, u):
                        n = s * 16 + u
                        if n == 0:
                            dve.wait_ge(sig("kparts"), STREAMS)
                        for hh in range(2):
                            dve.wait_ge(sig("gate_ready"), 2 * n + hh + 1)
                            dve.wait_ge(sig("scores_ready"), 2 * n + hh + 1)
                            if n >= 2:
                                dve.wait_ge(sig("prob_ready"), 2 * (n - 1))
                            dve.tensor_tensor(logit[n % 2][:, hh, :, :], quad[:, hh, :, :],
                                              gate_t[:, n % 2, hh, :].unsqueeze(1).broadcast_to([P, MAPS, T]), ALU.add) \
                                .then_inc(sig("logits_made"), 1)

                    def heads_end(s):
                        dve.wait_ge(sig("heads_in"), 4 * (s + 1))
                        o = on[s][:, :, :, :].rearrange("p t (h m) c -> p (t h) m c", m=MAPS)
                        link(dve.reciprocal(rzo[s][:, :, :], o[:, :, :, HV]))
                        link(dve.tensor_scalar(rzo[s][:, :, 1], rzo[s][:, :, 1], lam[:, 0:1], None, ALU.mult))
                        shape = [P, NT * AH, HV]
                        y1 = qT[s][:, :].rearrange("p (h d) -> p h d", d=HV)
                        y2 = cT[s][:, :].rearrange("p (h d) -> p h d", d=HV)
                        y = xn[s][:, :, :].rearrange("p t (h d) -> p (t h) d", d=HV)
                        dve.tensor_tensor(y1, o[:, :, 0, 0:HV], rzo[s][:, :, 0].unsqueeze(2).broadcast_to(shape), ALU.mult)
                        link(dve.tensor_tensor(y2, o[:, :, 1, 0:HV], rzo[s][:, :, 1].unsqueeze(2).broadcast_to(shape), ALU.mult))
                        link(dve.tensor_tensor(y1, y1, y2, ALU.subtract))
                        pk = [peak[s][:, a, :] for a in range(4)]
                        link(dve.tensor_reduce(pk[0], y1, AX.X, ALU.max, apply_absolute_value=True))
                        link(dve.tensor_scalar(pk[0], pk[0], 1e-15, None, ALU.max))
                        link(dve.reciprocal(pk[1], pk[0]))
                        dve.tensor_scalar(pk[2], pk[0], 2.0 ** -64, 1.0e3, ALU.mult, ALU.min)
                        link(dve.tensor_tensor(y1, y1, pk[1].unsqueeze(2).broadcast_to(shape), ALU.mult))
                        link(dve.tensor_tensor(y2, y1, y1, ALU.mult))
                        dve.scalar_tensor_tensor(pk[3], pk[1], RMS_EPS, pk[1], ALU.mult, ALU.mult)
                        link(dve.tensor_reduce(pk[0], y2, AX.X, ALU.add))
                        dve.scalar_tensor_tensor(ms[s][:, :], pk[0], 1.0 / HV, pk[3], ALU.mult, ALU.add) \
                            .then_inc(sig("mean_square"), 1)
                        link(dve.tensor_tensor(pk[2], pk[2], pk[2], ALU.mult))
                        link(dve.tensor_tensor(pk[2], pk[2], pk[0], ALU.mult))
                        link(dve.tensor_scalar(pk[2], pk[2], 1.0, None, ALU.is_lt))
                        dve.wait_ge(sig("head_rstd"), s + 1)
                        link(dve.tensor_tensor(pk[2], pk[2], rzo[s][:, :, 0], ALU.mult))
                        link(dve.tensor_tensor(y1, y1, pk[2].unsqueeze(2).broadcast_to(shape), ALU.mult))
                        dve.tensor_tensor(y, y1, sub_half[:, :].unsqueeze(1).broadcast_to(shape), ALU.mult) \
                            .then_inc(sig("y_made"), 1)

                    for s in range(STREAMS):
                        for u in range(16):
                            logits(s, u)
                        heads_end(s)
                    for s in range(STREAMS):
                        residual(3, s, 2, "attn_out")
                        moments(4, s)
                    normed(4)
                    cross(1)
                    cross_end(1, 4)
                    for s in range(STREAMS):
                        moments(5, s)
                    normed(5)
                    for s in range(STREAMS):
                        residual(5, s, 3, "ffn1_out")

                @block.tensor
                def _(pe):
                    def turn_in(k, s):
                        pe.wait_ge(sig("xn_ready"), turn(k, s))
                        if k:
                            pe.wait_ge(sig("x_done"), turn(k - 1, s))
                        for t in range(NT):
                            ins = pe.transpose(bk(s, 0)[:, t * P:(t + 1) * P], xn[s][:, t, :], ident[:, :])
                        ins.then_inc(sig("xn_turned"), 1)

                    def to_tokens(dst, pairs, done):
                        for t in range(NT):
                            for a, (lhs, rhs) in enumerate(pairs):
                                ins = pe.matmul(dst[:, t * P:(t + 1) * P], lhs[:, t * P:(t + 1) * P], rhs,
                                                start=(a == 0), stop=(a == len(pairs) - 1))
                        ins.then_inc(sig(done), 1)

                    def cross(l, k):
                        pe.wait_ge(sig(f"w_x{l}"), 16)
                        for s in range(STREAMS):
                            if l == 0:
                                pe.wait_ge(sig(f"ctx_loaded{s}"), 16 * HG)
                            pe.wait_ge(sig("x_done"), turn(k - 1, s))
                            c4 = ctxT[s][:, :, :].rearrange("p h k -> p (h k)")
                            pe.matmul(bk(s, 2)[:, 0:P], w(f"x{l}k"), c4, start=True, stop=True)
                            pe.matmul(bk(s, 3)[:, 0:P], c4, w(f"x{l}v"), start=True, stop=True) \
                                .then_inc(sig("kv_made"), 1)
                        for s in range(STREAMS):
                            turn_in(k, s)
                        for s in range(STREAMS):
                            pe.wait_ge(sig("xT_ready"), turn(k, s))
                            pe.matmul(bk(s, 1), w(f"x{l}q"), xT[s][:, :], start=True, stop=True) \
                                .then_inc(sig("q_made"), 1)
                        for g in range(NG):
                            for s in range(STREAMS):
                                pe.wait_ge(sig("q_ready"), turn(l, s))
                                pe.wait_ge(sig("kv_blocks"), turn(l, s))
                                if g >= 2:
                                    pe.wait_ge(sig("capped"), (l * NG + g - 2) * STREAMS + s + 1)
                                r = slice(32 * g, 32 * g + 32)
                                pe.matmul(bk(s, 2 + g % 2), key_blocks[l][s][r, :, :].rearrange("p h k -> p (h k)"),
                                          qT[s][r, :], start=True, stop=True).then_inc(sig("scores_made"), 1)
                        for s in range(STREAMS):
                            pe.wait_ge(sig("weights"), (l * NG + NG - 1) * STREAMS + s + 1)
                            for g in range(NG):
                                pe.matmul(bk(s, 1)[32 * g:32 * g + 32, :], val_blocks[l][s][:, g, :], big[s][:, g, :],
                                          start=True, stop=True)
                            for g in range(NG):
                                ins = pe.matmul(bk(s, 0)[32 * g:32 * g + 32, :], head_sum[:, :], big[s][:, g, :],
                                                start=True, stop=True)
                            ins.then_inc(sig("weighed"), 1)
                        for s in range(STREAMS):
                            pe.wait_ge(sig("z_out"), turn(l, s))
                            for t in range(NT):
                                ins = pe.transpose(bk(s, 2)[:, t * P:(t + 1) * P], zT[s][:, t * P:(t + 1) * P], ident[:, :])
                            ins.then_inc(sig("z_turned"), 1)
                        for s in range(STREAMS):
                            pe.wait_ge(sig("rz_wide"), turn(l, s))
                            for t in range(NT):
                                ins = pe.transpose(bk(s, 3)[:, t * P:(t + 1) * P], zT[s][:, t * P:(t + 1) * P], ident[:, :])
                            ins.then_inc(sig("rz_turned"), 1)
                        for s in range(STREAMS):
                            pe.wait_ge(sig("ctx_ready"), turn(l, s))
                            to_tokens(bk(s, 1), [(cT[s], w(f"x{l}o"))], f"cross_out{l}")

                    pe.wait_ge(sig("w_lru"), 16)
                    for s in range(STREAMS):
                        turn_in(0, s)
                    for s in range(STREAMS):
                        pe.wait_ge(sig("xT_ready"), s + 1)
                        pe.matmul(bk(s, 1), w("bt1"), xT[s][:, :], start=True, stop=True)
                        pe.matmul(bk(s, 2), w("bt2"), xT[s][:, :], start=True, stop=True).then_inc(sig("states_in"), 1)
                    for s in range(STREAMS):
                        pe.wait_ge(sig("rotated_out_c"), s + 1)
                        pe.wait_ge(sig("rotated_out_s"), s + 1)
                        to_tokens(bk(s, 3), [(big2[s][:, 0, :], w("wc1")), (big2[s][:, 1, :], w("wc2")),
                                             (xT[s], w("dt"))], "lru_out")
                    cross(0, 1)

                    pe.wait_ge(sig("w_ffn0"), 16)
                    for s in range(STREAMS):
                        turn_in(2, s)
                    for s in range(STREAMS):
                        pe.wait_ge(sig("xT_ready"), turn(2, s))
                        for t in range(NT):
                            ins = pe.matmul(bk(s, 1)[:, t * EXPERTS:(t + 1) * EXPERTS], xT[s][:, t * P:(t + 1) * P],
                                            w("gate"), start=True, stop=True)
                        ins.then_inc(sig("gate_logits"), 1)
                    for s in range(STREAMS):
                        pe.wait_ge(sig("comb_ready"), s + 1)
                        for t in range(NT):
                            ins = pe.transpose(bk(s, 3).bitcast(BF16)[0:3 * EXPERTS, t * P:(t + 1) * P],
                                               cpart[s][:, t, :, :].rearrange("p a e -> p (a e)"), identb[:, :])
                        ins.then_inc(sig("comb_turned"), 1)

                    def up(j, s):
                        if j == 0:
                            pe.wait_ge(sig("gate_exp"), s + 1)
                            pe.wait_ge(sig("combT_ready"), s + 1)
                        else:
                            pe.wait_ge(sig("hidden"), turn(j - 1, s))
                        pe.matmul(bk(s, 1), wch("wg", j), xT[s][:, :], start=True, stop=True).then_inc(sig("gated"), 1)
                        ins = pe.matmul(bk(s, 2), wch("wu", j), xT[s][:, :], start=True, stop=True)
                        if j < RCH:
                            ins = pe.matmul(bk(s, 3), expert_rows[:, j, :], combT[s][:, :], start=True, stop=True)
                        ins.then_inc(sig("upped"), 1)

                    def down(j, s):
                        pe.wait_ge(sig("hidden"), turn(j, s))
                        for t in range(NT):
                            ins = pe.matmul(bk(s, 0)[:, t * P:(t + 1) * P], big2[s][:, j % 2, t * P:(t + 1) * P],
                                            wch("wd", j), start=(j == 0 and t == 0), stop=(j == FCH - 1),
                                            skip_group_check=True)
                        ins.then_inc(sig("down" if j < FCH - 1 else "ffn0_out"), 1)

                    for j in range(FCH):
                        for s in range(STREAMS):
                            up(j, s)
                            if j:
                                down(j - 1, s)
                    for s in range(STREAMS):
                        down(FCH - 1, s)

                    pe.wait_ge(sig("w_attn"), 16)
                    for s in range(STREAMS):
                        turn_in(3, s)
                    for s in range(STREAMS):
                        pe.wait_ge(sig("xT_ready"), turn(3, s))
                        for t in range(NT):
                            pe.matmul(bk(s, t)[:, 0:384], xT[s][:, t * P:(t + 1) * P], w("aqkv"),
                                      start=True, stop=True).then_inc(sig("qkv_made"), 1)
                    for s in range(STREAMS):
                        pe.wait_ge(sig("unit_vectors"), s + 1)
                        pe.wait_ge(sig("vals_ready"), NT * (s + 1))
                        for a, got in ((0, "q_turned"), (1, "k_turned")):
                            for t in range(NT):
                                ins = pe.transpose(bk(s, 1 + a)[:, t * P:(t + 1) * P],
                                                   qkn[s][:, t, a * P:(a + 1) * P], ident[:, :])
                            ins.then_inc(sig(got), 1)

                    pe.wait_ge(sig("k_rest"), STREAMS)
                    for _ in range(WARM_UP):
                        pe.matmul(bank[1][:, :], identb[:, :], kpart[0][:, 0, :], start=True, stop=True)

                    def scores(s, u):
                        n = s * 16 + u
                        hp, c = u // 4, u % 4
                        kc = slice(c * P, (c + 1) * P)
                        if n == 0:
                            pe.wait_ge(sig("k_rest"), STREAMS)
                            pe.wait_ge(sig("q_rest"), STREAMS)
                        if u == 0:
                            pe.wait_ge(sig(f"stacked{s}"), 16 * 2 * MAPS * len(RUNS))
                        for hh in range(2):
                            h = 2 * hp + hh
                            if n >= 1:
                                pe.wait_ge(sig("gate_ready"), 2 * (n - 1) + hh + 1)
                            pe.matmul(pair[:, hh, :], kstack[s][0:MAP2 + KROWS, h, kc], qstack[s][0:MAP2 + KROWS, h, :],
                                      start=True, stop=True).then_inc(sig("diff_made"), 1)
                        for hh in range(2):
                            h = 2 * hp + hh
                            if n >= 1:
                                pe.wait_ge(sig("logits_made"), 2 * (n - 1) + hh + 1)
                            for m in range(MAPS):
                                r = slice(MAP2 * m, MAP2 * m + KROWS)
                                ins = pe.matmul(quad[:, hh, m, :], kstack[s][r, h, kc], qstack[s][r, h, :],
                                                start=True, stop=True)
                            ins.then_inc(sig("scores_ready"), 1)

                    def weigh(s, u):
                        n = s * 16 + u
                        hp, c = u // 4, u % 4
                        pe.wait_ge(sig("prob_ready"), 2 * n + 2)
                        if c == 0 and s * 4 + hp >= 1:
                            pe.wait_ge(sig("heads_out"), s * 4 + hp)
                        for hh in range(2):
                            for m in range(MAPS):
                                q = 32 * (2 * hh + m)
                                ins = pe.matmul(bank[0][q:q + 32, :], vals[s][:, c, 2 * hp + hh, :],
                                                prob[n % 2][:, hh, m, :], start=(c == 0), stop=(c == 3),
                                                skip_group_check=True)
                        ins.then_inc(sig("unit_used"), 1)

                    def heads_turn(s, hp):
                        pe.wait_ge(sig("heads_out"), s * 4 + hp + 1)
                        if s * 4 + hp >= 1:
                            pe.wait_ge(sig("heads_in"), s * 4 + hp)
                        for t in range(NT):
                            ins = pe.transpose(bank[1][:, t * P:(t + 1) * P], oT[0][:, t * P:(t + 1) * P], ident[:, :])
                        ins.then_inc(sig("heads_turned"), 1)

                    for s in range(STREAMS):
                        for u in range(16):
                            scores(s, u)
                            if u >= 1:
                                weigh(s, u - 1)
                            if u % 4 == 2 and u > 4:
                                heads_turn(s, u // 4 - 1)
                        weigh(s, 15)
                        heads_turn(s, 3)
                    for s in range(STREAMS):
                        pe.wait_ge(sig("y_made"), s + 1)
                        pe.wait_ge(sig("logits_made"), 2 * 16 * STREAMS)
                        for t in range(NT):
                            ins = pe.transpose(bk(s, 1)[:, t * P:(t + 1) * P], xn[s][:, t, :], ident[:, :])
                        ins.then_inc(sig("y_turned"), 1)
                    pe.wait_ge(sig("gate_ready"), 2 * 16 * STREAMS)
                    for s in range(STREAMS):
                        pe.wait_ge(sig("y_ready"), s + 1)
                        to_tokens(bk(s, 2), [(cT[s], w("ao"))], "attn_out")
                    cross(1, 4)
                    for s in range(STREAMS):
                        turn_in(5, s)
                    for j in range(F1CH):
                        for s in range(STREAMS):
                            pe.wait_ge(sig("xT_ready"), turn(5, s))
                            if j >= 2:
                                pe.wait_ge(sig("f1_hidden"), turn(j - 2, s))
                            pe.matmul(bk(s, 1 + j % 2), wch("f1w1", j), xT[s][:, :], start=True, stop=True) \
                                .then_inc(sig("f1_made"), 1)
                    for s in range(STREAMS):
                        pe.wait_ge(sig("f1_hidden"), turn(F1CH - 1, s))
                        to_tokens(bk(s, 3), [(big[s][:, j, :], wch("f1w2", j)) for j in range(F1CH)], "ffn1_out")

        with nc.Fori(0, B // STREAMS) as i:
            body(i)
            for name in sems:
                if name not in keep:
                    nc.gpsimd.sem_clear(sems[name])
            nc.all_engine_barrier()


def kernel(**inputs):
    import concourse.bacc as bacc
    from concourse.bass_utils import run_bass_kernel_spmd as run

    v = {k: np.asarray(a) for k, a in inputs.items()}
    t = lambda n: v[n].T
    routed = lambda n: v[n].reshape(EXPERTS * EI, D).T
    maps_first = lambda n: v[n].reshape(AH, MAPS, AD, D).transpose(1, 2, 0, 3).reshape(D, D).T
    down = v["L0_ffn_w_down"].transpose(0, 2, 1).reshape(RCH, P, D).transpose(1, 0, 2).reshape(P, RCH * D)
    w2 = v["L1_ffn_W2"].T.reshape(F1CH, P, D).transpose(1, 0, 2).reshape(P, F1CH * D)
    w = np.concatenate([
        t("L0_attn_B_re"), t("L0_attn_B_im"), t("L0_attn_B_im"), t("L0_attn_B_re"),
        np.concatenate([t("L0_attn_C_re"), t("L0_attn_C_im")]),
        np.concatenate([t("L0_attn_C_im"), t("L0_attn_C_re")]), t("L0_attn_D"),
        t("L1_ffn_W1"), w2,
        t("L0_xattn_Wq"), t("L0_xattn_Wk"), t("L0_xattn_Wv"), t("L0_xattn_Wo"),
        t("L0_ffn_gate_weight"), routed("L0_ffn_w_gate"), t("L0_ffn_ws_gate"),
        routed("L0_ffn_w_up"), t("L0_ffn_ws_up"), down, t("L0_ffn_ws_down"),
        maps_first("L1_attn_Wq"), maps_first("L1_attn_Wk"), t("L1_attn_Wv"), t("L1_attn_Wo"),
        t("L1_xattn_wq"), t("L1_xattn_wk"), t("L1_xattn_wv"), t("L1_xattn_wo")], axis=1)
    twice = lambda n: np.concatenate([v[n], v[n]])
    cols = np.stack([twice("L0_attn_nu_log"), twice("L0_attn_theta_log"), twice("L0_attn_gamma_log"),
                     v["L0_xattn_bq"], v["L0_xattn_bk"], v["L1_xattn_bq"], v["L1_xattn_bk"],
                     *v["L1_ffn_b1"].reshape(F1CH, P)], axis=1)
    rows = np.concatenate([v["L0_xattn_bv"], v["L1_xattn_bv"], v["L0_xattn_bo"], v["L1_attn_bo"],
                           v["L1_xattn_bo"], v["L1_ffn_b2"], v["L1_attn_delta_gain"], v["L1_attn_cos_head_delta"],
                           v["L1_attn_cos_logit_scale_raw"].reshape(1), v["L1_attn_lambda_q1"],
                           v["L1_attn_lambda_k1"], v["L1_attn_lambda_q2"], v["L1_attn_lambda_k2"],
                           v["L1_attn_subln_weight"]])
    assert w.shape == (P, WTOTAL) and cols.shape == (P, len(COLS)) and rows.shape == (RTOTAL,)
    arrays = {"x": v["x"], "ctx": v["ctx_1024"].transpose(0, 2, 1),
              "mask0": v["mask_BxSxS2_bf0"].transpose(0, 2, 1),
              "mask1": v["mask_Bx1xSxS2_ik1"][:, 0].transpose(0, 2, 1), "w": w, "cols": cols, "rows": rows}
    arrays = {k: np.ascontiguousarray(a) for k, a in arrays.items()}
    nc = bacc.Bacc("TRN2", target_bir_lowering=False, num_devices=1)
    args = [nc.dram_tensor(f"{k}_in", a.shape, mybir.dt.from_np(a.dtype), kind="ExternalInput").ap()
            for k, a in arrays.items()]
    args.append(nc.dram_tensor("out", (B, T, D), F32, kind="ExternalOutput").ap())
    build(nc, *args)
    r = run(nc, [{f"{k}_in": a for k, a in arrays.items()}], core_ids=[0])
    return r.results[0]["out"]
```

```python
import numpy as np
import concourse.bass as bass
from concourse import mybir
from contextlib import ExitStack

F32 = mybir.dt.float32
BF16 = mybir.dt.bfloat16
I32 = mybir.dt.int32
U8 = mybir.dt.uint8
ALU = mybir.AluOpType
ACT = mybir.ActivationFunctionType
AX = mybir.AxisListType

B, T, D = 4, 512, 128
P = 128
NT = T // P
STREAMS = 2
NSTATE = 64
CTX = 32
XH, XD = 16, 8
HG = P // CTX
NG = XH // HG
XSCALE = 1.0 / float(np.sqrt(XD))
EXPERTS, EI = 8, 64
EPC = P // EI
RCH = EXPERTS // EPC
FCH = RCH + 1
FFN_ORDER = (RCH, *range(RCH))
ROUTE_SCALE = 2.5
AH, AD = 8, 8
MAPS = 2
HV = 2 * AD
F1CH = 4
LN_EPS = 1e-5
RMS_EPS = 1e-5
HALF = T // 2
KC = T // P
PAIRS = AH // 2
GROUPS = STREAMS * PAIRS
UNITS = GROUPS * KC
WARM_UP = 40
WARM_UP_NORM = 12
BIG = 3.0e38

WCOLS, _at = {}, 0
for _name, _n in [("bt1", 128), ("bt2", 128), ("wc1", 128), ("wc2", 128), ("dt", 128),
                  ("f1w1", 512), ("f1w2", 512),
                  ("x0q", 128), ("x0k", 128), ("x0v", 128), ("x0o", 128),
                  ("gate", EXPERTS), ("wg", FCH * P), ("wu", FCH * P), ("wd", FCH * P),
                  ("aqkv", 384), ("ao", 128),
                  ("x1q", 128), ("x1k", 128), ("x1v", 128), ("x1o", 128)]:
    WCOLS[_name] = (_at, _at + _n)
    _at += _n
WTOTAL = _at
COLS = {n: i for i, n in enumerate(["nu", "theta", "gamma", "bq0", "bk0", "bq1", "bk1",
                                    "b1_0", "b1_1", "b1_2", "b1_3"])}
ROWS, _at = {}, 0
for _name, _n in [("bv0", 128), ("bv1", 128), ("bo_x0", 128), ("bo_a", 128), ("bo_x1", 128), ("b2", 128),
                  ("gain", AH), ("head_delta", AH), ("raw", 1), ("lq1", AD), ("lk1", AD), ("lq2", AD),
                  ("lk2", AD), ("subln", HV)]:
    ROWS[_name] = (_at, _at + _n)
    _at += _n
RTOTAL = _at
QGROUPS = ((0, 3, 1), (3, 5, 1), (5, 6, 1))
KGROUPS = ((1, 6, 2), (2, 5, 2), (0, 1, 1))
PRODUCTS = 6
KROWS = PRODUCTS * AD
MAP2 = 64


def build(nc, x_in, ctx_in, m0_in, m1_in, w_in, cols_in, rows_in, out):
    ctx = ExitStack()
    with ctx:
        def sb(name, shape, dt=F32):
            return ctx.enter_context(nc.sbuf_tensor(name, shape, dt))

        sems = {}

        def sig(name):
            if name not in sems:
                sems[name] = ctx.enter_context(nc.semaphore(name))
            return sems[name]

        wt = sb("wt", [P, WTOTAL])
        cols = sb("cols", [P, len(COLS)])
        rows = sb("rows", [P, RTOTAL])
        ident = sb("ident", [P, P])
        identb = sb("identb", [P, P], BF16)
        mask_k = sb("mask_k", [P, XH, CTX])
        mask_v = sb("mask_v", [P, NG, HG, XD])
        expert_rows = sb("expert_rows", [3 * EXPERTS, RCH, P], BF16)
        lower = sb("lower", [P, NT, EXPERTS, EXPERTS])
        neg_half = sb("neg_half", [P, 32])
        rot_in_c = sb("rot_in_c", [P, T])
        rot_in_s = sb("rot_in_s", [P, T])
        rot_out_c = sb("rot_out_c", [P, T])
        rot_out_s = sb("rot_out_s", [P, T])
        decay = sb("decay", [P, 1])
        bq_scaled = sb("bq_scaled", [P, 2])
        lam = sb("lam", [P, 1])
        qscale = sb("qscale", [P, MAPS, AH])
        sub_half = sb("sub_half", [P, HV])

        def w(name):
            a, b = WCOLS[name]
            return wt[:, a:b]

        def wch(name, j):
            a, _ = WCOLS[name]
            return wt[:, a + j * P:a + (j + 1) * P]

        def col(name):
            return cols[:, COLS[name]:COLS[name] + 1]

        def row(name):
            a, b = ROWS[name]
            return rows[:, a:b]

        def per_stream(name, shape, dt=F32):
            return [sb(f"{name}{s}", shape, dt) for s in range(STREAMS)]

        x = per_stream("x", [P, NT, D])
        xn = per_stream("xn", [P, NT, D])
        xT = per_stream("xT", [P, T])
        bst = per_stream("bst", [P, NT, 6])
        mv = per_stream("mv", [P, NT, 2])
        rstd = per_stream("rstd", [P, NT])
        veps = per_stream("veps", [P, NT])
        big = per_stream("big", [P, 4, T])
        big2 = per_stream("big2", [P, 4, T])
        ctxT = per_stream("ctxT", [P, HG, CTX])
        key_blocks = per_stream("key_blocks", [P, XH, CTX])
        val_blocks = per_stream("val_blocks", [P, NG, HG * XD])
        m0 = per_stream("m0", [P, NT, CTX], U8)
        m1 = per_stream("m1", [P, NT, CTX], I32)
        cap = [per_stream(f"cap{l}", [P, NT, CTX]) for l in range(2)]
        cap_part = per_stream("cap_part", [P, NT, CTX])
        qT = per_stream("qT", [P, T])
        accT = sb("accT", [P, T])
        cT = per_stream("cT", [P, T])
        mx = per_stream("mx", [P, NT, XH])
        sg = per_stream("sg", [P, NT, EXPERTS])
        top = per_stream("top", [P, NT, EXPERTS])
        cmpa = per_stream("cmpa", [P, NT, EXPERTS, EXPERTS])
        cmpb = per_stream("cmpb", [P, NT, EXPERTS, EXPERTS])
        rank = per_stream("rank", [P, NT, EXPERTS])
        wsum = per_stream("wsum", [P, NT])
        cpart = per_stream("cpart", [P, NT, 3, EXPERTS], BF16)
        cres = per_stream("cres", [P, NT, EXPERTS])
        combT = per_stream("combT", [3 * EXPERTS, T], BF16)
        ss = per_stream("ss", [P, NT, 4 * AH])
        qpart = per_stream("qpart", [P, 3, T], BF16)
        kpart = per_stream("kpart", [P, 3, T], BF16)
        qstack = per_stream("qstack", [P, AH, T], BF16)
        kstack = per_stream("kstack", [P, AH, T], BF16)
        vals = per_stream("vals", [P, NT, AH, 32])
        on = per_stream("on", [P, NT, AH * MAPS, 32])
        qkn = [o[:, 0:2, :, :].rearrange("p a h c -> p (a h c)").rearrange("p (t c) -> p t c", t=NT) for o in on]
        rzo = per_stream("rzo", [P, NT * AH, MAPS])
        ms = per_stream("ms", [P, NT * AH])
        peak = per_stream("peak", [P, 4, NT * AH])
        gate_t = sb("gate_t", [P, 2, 2, T])
        logit = [b[:, :, :].rearrange("p (h m) t -> p h m t", h=2) for b in big2]
        prob = [b[:, :, :].rearrange("p (h m) t -> p h m t", h=2) for b in big]

        parts_dram = nc.dram_tensor("parts", (STREAMS, 2, PRODUCTS, P, T), BF16, kind="Internal").ap()

        bank = [ctx.enter_context(nc.psum_tensor(f"bank{i}", [P, T], F32)) for i in range(2)]
        quad = ctx.enter_context(nc.psum_tensor("quad", [P, 2, MAPS, T], F32))
        pair = ctx.enter_context(nc.psum_tensor("pair", [P, 2, T], F32))

        def bk(s, i):
            return [[bank[0][:, :], quad[:, 0, 0, :], quad[:, 0, 1, :], pair[:, 0, :]],
                    [bank[1][:, :], quad[:, 1, 0, :], quad[:, 1, 1, :], pair[:, 1, :]]][s][i]

        def turn(k, s):
            return STREAMS * k + s + 1

        WSECT = [("w_lru", "bt1", "dt"), ("w_ffn1", "f1w1", "f1w2"), ("w_x0", "x0q", "x0o"),
                 ("w_ffn0", "gate", "wd"), ("w_attn", "aqkv", "ao"), ("w_x1", "x1q", "x1o")]

        def unit(n):
            return n // (PAIRS * KC), n // KC % PAIRS, n % KC

        tab_c, tab_s, tmp = big[0][:, 0, :], big[0][:, 1, :], big[0][:, 2, :]
        small = sb("small", [P, 64])
        smalli = sb("smalli", [P, 4], I32)
        expt = sb("expt", [P, 3, 4])
        expi = sb("expi", [P, 4], I32)
        zc = sb("zc", [P, 10])
        zs = sb("zs", [P, 10])
        ones_sq = sb("ones_sq", [P, P])
        warm_rhs = sb("warm_rhs", [P, T], BF16)
        zeros = sb("zeros", [MAP2 - KROWS, T], BF16)

        def prologue():
            with nc.Block() as block:
                @block.sync
                def _(sp):
                    sp.dma_start(cols[:, :], cols_in).then_inc(sig("cols_loaded"), 16)
                    for name, a, b in WSECT[:3]:
                        c0, c1 = WCOLS[a][0], WCOLS[b][1]
                        sp.dma_start(wt[:, c0:c1], w_in[:, c0:c1]).then_inc(sig(name), 16)
                    sp.wait_ge(sig("zeros"), 1)
                    for s in range(STREAMS):
                        for stack in (qstack, kstack):
                            for m in range(MAPS):
                                sp.dma_start(stack[s][MAP2 * m + KROWS:MAP2 * (m + 1), :, :],
                                             zeros[:, :].unsqueeze(1).broadcast_to([MAP2 - KROWS, AH, T])) \
                                    .then_inc(sig("rows_zeroed"), 16)

                @block.scalar
                def _(act):
                    act.dma_start(rows[:, :], rows_in.partition_broadcast(P)).then_inc(sig("rows_loaded"), 16)
                    for name, a, b in WSECT[3:]:
                        c0, c1 = WCOLS[a][0], WCOLS[b][1]
                        act.dma_start(wt[:, c0:c1], w_in[:, c0:c1]).then_inc(sig(name), 16)
                    act.wait_ge(sig("rows_loaded"), 16)
                    act.activation(small[:, 20:21], row("raw"), ACT.Exp, scale=-1.0).then_inc(sig("raw_exp"), 1)
                    act.wait_ge(sig("lambda_sums"), 2)
                    act.activation(small[:, 24:26], small[:, 22:24], ACT.Exp).then_inc(sig("lambda_exp"), 1)
                    act.wait_ge(sig("head_delta"), 1)
                    act.activation(small[:, 32:40], small[:, 40:48], ACT.Tanh).then_inc(sig("head_tanh"), 1)
                    act.wait_ge(sig("angles"), 1)
                    act.activation(small[:, 10:12], small[:, 8:10], ACT.Sin).then_inc(sig("sincos"), 1)

                @block.tensor
                def _(pe):
                    pe.wait_ge(sig("ones"), 1)
                    pe.wait_ge(sig("abs_sums"), 1)
                    pe.matmul(bank[0][:, 0:2], ones_sq[:, :], small[:, 50:52], start=True, stop=True) \
                        .then_inc(sig("abs_total"), 1)

                @block.gpsimd
                def _(pool):
                    links = [0]

                    def link(ins):
                        links[0] += 1
                        ins.then_inc(sig("pool_link0"), 1)
                        pool.wait_ge(sig("pool_link0"), links[0])

                    pool.memset(zeros[:, :], 0.0).then_inc(sig("zeros"), 1)
                    pool.memset(warm_rhs[:, :], 1.0)
                    pool.memset(ones_sq[:, :], 1.0).then_inc(sig("ones"), 1)
                    link(pool.memset(ident[:, :], 0.0))
                    link(pool.affine_select(out=ident[:, :], in_=ident[:, :], compare_op=ALU.not_equal,
                                            fill=1.0, base=0, pattern=[[-1, P]], channel_multiplier=1))
                    link(pool.tensor_copy(identb[:, :], ident[:, :]))
                    link(pool.memset(neg_half[:, :], -0.5))
                    link(pool.memset(mask_k[:, :, :], 1.0))
                    link(pool.affine_select(out=mask_k[:, :, :], in_=mask_k[:, :, :], compare_op=ALU.is_ge, fill=0.0,
                                            base=0, pattern=[[-XD, XH], [0, CTX]], channel_multiplier=1))
                    link(pool.affine_select(out=mask_k[:, :, :], in_=mask_k[:, :, :], compare_op=ALU.is_ge, fill=0.0,
                                            base=XD - 1, pattern=[[XD, XH], [0, CTX]], channel_multiplier=-1))
                    link(pool.memset(mask_v[:, :, :, :], 0.0))
                    for h in range(HG):
                        link(pool.memset(mask_v[CTX * h:CTX * h + CTX, :, h, :], 1.0))
                    link(pool.memset(expert_rows[:, :, :], 0.0))
                    er = expert_rows[:, :, :].rearrange("r j (e i) -> r j e i", e=EPC)
                    for p in range(3):
                        link(pool.affine_select(out=er, in_=er, compare_op=ALU.not_equal, fill=1.0,
                                                base=-EXPERTS * p, pattern=[[-EPC, RCH], [-1, EPC], [0, EI]],
                                                channel_multiplier=1))
                    link(pool.memset(lower[:, :, :, :], 1.0))
                    link(pool.affine_select(out=lower[:, :, :, :], in_=lower[:, :, :, :], compare_op=ALU.is_gt,
                                            fill=0.0, base=0, pattern=[[0, NT], [1, EXPERTS], [-1, EXPERTS]],
                                            channel_multiplier=0))
                    for s in range(STREAMS):
                        link(pool.memset(vals[s][:, :, :, HV:32], 1.0))

                @block.vector
                def _(dve):
                    links = [0]

                    def link(ins):
                        links[0] += 1
                        ins.then_inc(sig("dve_link0"), 1)
                        dve.wait_ge(sig("dve_link0"), links[0])

                    def exp(dst, src, width, negate):
                        z, q, r = (expt[:, a, 0:width] for a in range(3))
                        sign = -1.0 if negate else 1.0
                        link(dve.tensor_scalar(z, src, sign * float(np.log2(np.e)), 127.0, ALU.mult, ALU.min))
                        link(dve.tensor_scalar(z, z, -126.0, None, ALU.max))
                        link(dve.tensor_copy(expi[:, 0:width], z))
                        link(dve.tensor_copy(z, expi[:, 0:width]))
                        link(dve.tensor_scalar(r, src, sign, None, ALU.mult))
                        for part in (0.693359375, -2.12194440e-4):
                            link(dve.scalar_tensor_tensor(r, z, -part, r, ALU.mult, ALU.add))
                        link(dve.tensor_scalar(q, r, 1.0 / 5040, None, ALU.mult))
                        for c in (720, 120, 24, 6, 2, 1):
                            link(dve.scalar_tensor_tensor(q, q, 1.0 / c, r, ALU.add, ALU.mult))
                        link(dve.tensor_scalar(z, z, 127.0, float(1 << 23), ALU.add, ALU.mult))
                        link(dve.tensor_copy(expi[:, 0:width], z))
                        link(dve.scalar_tensor_tensor(dst, q, 1.0, expi[:, 0:width].bitcast(F32), ALU.add, ALU.mult))

                    dve.wait_ge(sig("cols_loaded"), 16)
                    a = COLS["nu"]
                    exp(small[:, 0:3], cols[:, a:a + 3], 3, False)
                    exp(decay[:, :], small[:, 0:1], 1, True)
                    link(dve.tensor_scalar(small[:, 3:4], small[:, 1:2], float(1 / (2 * np.pi)), None, ALU.mult))
                    link(dve.tensor_copy(smalli[:, 0:1], small[:, 3:4]))
                    link(dve.tensor_copy(small[:, 4:5], smalli[:, 0:1]))
                    c1 = 6.28125
                    c2 = float(np.float32(2 * np.pi - c1))
                    link(dve.scalar_tensor_tensor(small[:, 5:6], small[:, 4:5], -c1, small[:, 1:2], ALU.mult, ALU.add))
                    link(dve.scalar_tensor_tensor(small[:, 5:6], small[:, 4:5], -c2, small[:, 5:6], ALU.mult, ALU.add))
                    pi = float(np.float32(np.pi))
                    for op, lim, step in ((ALU.is_gt, pi, -2 * np.pi), (ALU.is_lt, -pi, 2 * np.pi)):
                        link(dve.tensor_scalar(small[:, 6:7], small[:, 5:6], lim, float(step), op, ALU.mult))
                        link(dve.tensor_tensor(small[:, 5:6], small[:, 5:6], small[:, 6:7], ALU.add))
                    below = float(np.nextafter(np.float32(np.pi), np.float32(0)))
                    link(dve.tensor_scalar(small[:, 8:9], small[:, 5:6], below, -below, ALU.min, ALU.max))
                    link(dve.tensor_scalar(small[:, 6:7], small[:, 8:9], -1.0, None, ALU.mult))
                    link(dve.tensor_tensor(small[:, 6:7], small[:, 6:7], small[:, 8:9], ALU.max))
                    dve.tensor_scalar(small[:, 9:10], small[:, 6:7], -1.0, float(np.pi / 2), ALU.mult, ALU.add) \
                        .then_inc(sig("angles"), 1)
                    dve.wait_ge(sig("rows_loaded"), 16)
                    for i, (a, b) in enumerate((("lq1", "lk1"), ("lq2", "lk2"))):
                        link(dve.tensor_tensor(tmp[:, i * AD:(i + 1) * AD], row(a), row(b), ALU.mult))
                        dve.tensor_reduce(small[:, 22 + i:23 + i], tmp[:, i * AD:(i + 1) * AD], AX.X, ALU.add) \
                            .then_inc(sig("lambda_sums"), 1)
                    link(dve.tensor_reduce(small[:, 31:32], row("head_delta"), AX.X, ALU.add))
                    link(dve.tensor_scalar(small[:, 31:32], small[:, 31:32], 1.0 / AH, None, ALU.mult))
                    dve.tensor_scalar(small[:, 40:48], row("head_delta"), small[:, 31:32], None, ALU.subtract) \
                        .then_inc(sig("head_delta"), 1)
                    dve.wait_ge(sig("lambda_exp"), 1)
                    link(dve.tensor_tensor(lam[:, :], small[:, 24:25], small[:, 25:26], ALU.subtract))
                    link(dve.tensor_scalar(lam[:, :], lam[:, :], 0.5, None, ALU.add))
                    dve.wait_ge(sig("raw_exp"), 1)
                    link(dve.tensor_scalar(small[:, 21:22], small[:, 20:21], 1.0, None, ALU.add))
                    link(dve.reciprocal(small[:, 20:21], small[:, 21:22]))
                    link(dve.tensor_scalar(small[:, 21:22], small[:, 20:21], 15.0, None, ALU.mult))
                    dve.wait_ge(sig("head_tanh"), 1)
                    link(dve.tensor_scalar(small[:, 32:40], small[:, 32:40], 0.5, 1.0, ALU.mult, ALU.add))
                    dve.tensor_scalar(qscale[:, 0, :], small[:, 32:40], small[:, 21:22], None, ALU.mult)
                    dve.tensor_scalar(qscale[:, 1, :], small[:, 32:40], small[:, 21:22], -1.0, ALU.mult, ALU.mult)
                    dve.tensor_scalar(sub_half[:, :], row("subln"), 0.5, None, ALU.mult)
                    for l in range(2):
                        dve.tensor_scalar(bq_scaled[:, l:l + 1], col(f"bq{l}"), XSCALE, None, ALU.mult)
                    dve.wait_ge(sig("w_ffn1"), 16)
                    dve.tensor_reduce(small[:, 50:51], w("f1w1"), AX.X, ALU.add, apply_absolute_value=True)
                    dve.tensor_reduce(small[:, 51:52], w("f1w2"), AX.X, ALU.add, apply_absolute_value=True) \
                        .then_inc(sig("abs_sums"), 1)
                    dve.memset(tab_c[:, 0:1], 1.0)
                    link(dve.memset(tab_s[:, 0:1], 0.0))
                    dve.wait_ge(sig("sincos"), 1)
                    dve.tensor_copy(zs[:, 0:1], small[:, 10:11])
                    link(dve.tensor_copy(zc[:, 0:1], small[:, 11:12]))
                    steps = T.bit_length() - 1
                    for k in range(steps):
                        m = 1 << k
                        c, sn = zc[:, k:k + 1], zs[:, k:k + 1]
                        dve.tensor_scalar(tmp[:, 0:m], tab_s[:, 0:m], sn, None, ALU.mult)
                        if k < steps - 1:
                            dve.tensor_tensor(small[:, 12:13], sn, sn, ALU.mult)
                            dve.scalar_tensor_tensor(zs[:, k + 1:k + 2], c, 2.0, sn, ALU.mult, ALU.mult)
                        link(dve.tensor_scalar(tmp[:, 256:256 + m], tab_s[:, 0:m], c, None, ALU.mult))
                        dve.scalar_tensor_tensor(tab_c[:, m:2 * m], tab_c[:, 0:m], c, tmp[:, 0:m], ALU.mult, ALU.subtract)
                        if k < steps - 1:
                            dve.scalar_tensor_tensor(zc[:, k + 1:k + 2], c, c, small[:, 12:13], ALU.mult, ALU.subtract)
                        link(dve.scalar_tensor_tensor(tab_s[:, m:2 * m], tab_c[:, 0:m], sn, tmp[:, 256:256 + m],
                                                      ALU.mult, ALU.add))
                    lo, hi = slice(0, NSTATE), slice(NSTATE, P)
                    dve.tensor_scalar(rot_in_c[:, :], tab_c[:, :], small[:, 2:3], None, ALU.mult)
                    dve.tensor_scalar(rot_in_s[lo, :], tab_s[lo, :], small[lo, 2:3], None, ALU.mult)
                    dve.tensor_scalar(rot_in_s[hi, :], tab_s[hi, :], small[hi, 2:3], -1.0, ALU.mult, ALU.mult)
                    dve.tensor_copy(rot_out_c[lo, :], tab_c[lo, :])
                    dve.tensor_scalar(rot_out_c[hi, :], tab_c[hi, :], -1.0, None, ALU.mult)
                    dve.tensor_scalar(rot_out_s[:, :], tab_s[:, :], -1.0, None, ALU.mult)
                    dve.wait_ge(sig("abs_total"), 1)
                    inv = 1.0 / (4 * P * P)
                    link(dve.tensor_scalar(small[:, 52:54], bank[0][:, 0:2], inv, 1e-5, ALU.mult, ALU.add))
                    link(dve.tensor_scalar(small[:, 54:56], small[:, 52:54], 0.5, None, ALU.mult))
                    link(dve.tensor_scalar(small[:, 56:58], small[:, 54:56], -1.0, None, ALU.mult))
                    for i, name in enumerate(("f1w1", "f1w2")):
                        link(dve.tensor_scalar(tmp[:, :], w(name), small[:, 56 + i:57 + i], None, ALU.is_lt))
                        link(dve.scalar_tensor_tensor(w(name), w(name), small[:, 54 + i:55 + i], tmp[:, :],
                                                      ALU.is_gt, ALU.subtract))

        prologue()
        keep = set(sems)
        def body(i):
            with nc.Block() as block:
                def spill(queue, s, which, part):
                    name = ("q", "k")[which]
                    queue.wait_ge(sig(f"{name}part{part}"), s + 1)
                    a, b, step = (QGROUPS, KGROUPS)[which][part]
                    queue.dma_start(parts_dram[s, which, a:b:step].rearrange("c r t -> r c t"),
                                    (qpart, kpart)[which][s][:, part:part + 1, :]
                                    .broadcast_to([P, len(range(a, b, step)), T])) \
                        .then_inc(sig(f"{name}_spilled{s}"), 16)

                def restack(queue, s, which):
                    stack = (qstack, kstack)[which]
                    queue.wait_ge(sig(f"{('q', 'k')[which]}_spilled{s}"), 16 * 3)
                    for m in range(MAPS):
                        queue.dma_start(stack[s][MAP2 * m:MAP2 * m + KROWS, :, :],
                                        parts_dram[s, which][:, AH * AD * m:AH * AD * (m + 1), :]
                                        .rearrange("c (r h) t -> c r (h t)", h=AH)).then_inc(sig(f"stacked{s}"), 16)

                @block.sync
                def _(sp):
                    for s in range(STREAMS):
                        b = bass.ds(i * STREAMS + s, 1)
                        sp.dma_start(x[s][:, :, :], x_in[b].rearrange("b (t p) d -> p (b t) d", p=P)) \
                            .then_inc(sig(f"x_loaded{s}"), 16)
                    for s in range(STREAMS):
                        b = bass.ds(i * STREAMS + s, 1)
                        sp.dma_start(ctxT[s][:, :, :],
                                     ctx_in[b].rearrange("b d k -> d b k").broadcast_to([D, HG, CTX])) \
                            .then_inc(sig(f"ctx_loaded{s}"), 16)
                        sp.dma_start(m0[s][:, :, :], m0_in[b].rearrange("b p t k -> p (b t) k")) \
                            .then_inc(sig(f"masks_loaded{s}"), 16)
                        sp.dma_start(m1[s][:, :, :], m1_in[b].rearrange("b p t k -> p (b t) k")) \
                            .then_inc(sig(f"masks_loaded{s}"), 16)
                    for s in range(STREAMS):
                        for part in range(3):
                            for which in range(2):
                                spill(sp, s, which, part)
                        for which in range(2):
                            restack(sp, s, which)
                    for s in range(STREAMS):
                        sp.wait_ge(sig("x_done"), turn(5, s))
                        b = bass.ds(i * STREAMS + s, 1)
                        sp.dma_start(out[b].rearrange("b (t p) d -> p (b t) d", p=P), x[s][:, :, :]) \
                            .then_inc(sig("stored"), 16)
                    sp.wait_ge(sig("stored"), 16 * STREAMS)

                @block.gpsimd
                def _(pool):
                    links = [0]

                    def link(ins):
                        links[0] += 1
                        ins.then_inc(sig("pool_link"), 1)
                        pool.wait_ge(sig("pool_link"), links[0])

                    def rstds(k):
                        for s in range(STREAMS):
                            pool.wait_ge(sig("moments"), turn(k, s))
                            link(pool.tensor_scalar(veps[s][:, :], mv[s][:, :, 1], LN_EPS, None, ALU.add))
                            pool.tensor_tensor(rstd[s][:, :], veps[s][:, :], neg_half[:, 0:NT], ALU.pow) \
                                .then_inc(sig("rstd_ready"), 1)

                    def biases(k, bias):
                        for s in range(STREAMS):
                            pool.wait_ge(sig("xn_ready"), turn(k, s))
                            pool.tensor_tensor(x[s][:, :, :], x[s][:, :, :],
                                               row(bias).unsqueeze(1).broadcast_to([P, NT, D]), ALU.add) \
                                .then_inc(sig(f"biased{k}"), 1)

                    def recurrence():
                        for s in range(STREAMS):
                            pool.wait_ge(sig("scanned"), s + 1)
                            pool.tensor_tensor(big2[s][:, 1, :], big[s][:, 2, :], rot_out_s[:, :], ALU.mult) \
                                .then_inc(sig("rotated_out_s"), 1)

                    def caps0(s):
                        pool.wait_ge(sig(f"masks_loaded{s}"), 16 * 2)
                        pool.tensor_scalar(cap[0][s][:, :, :], m0[s][:, :, :], 0.0, BIG, ALU.is_equal, ALU.mult)
                        link(pool.tensor_scalar(cap_part[s][:, :, :], m0[s][:, :, :], -1.0e18, None, ALU.mult))
                        pool.tensor_tensor(cap[0][s][:, :, :], cap[0][s][:, :, :], cap_part[s][:, :, :], ALU.add) \
                            .then_inc(sig("caps0"), 1)

                    def caps1(s):
                        link(pool.tensor_scalar(cap[1][s][:, :, :], m1[s][:, :, :], 0.0, -BIG, ALU.is_equal, ALU.mult))
                        pool.tensor_scalar(cap[1][s][:, :, :], cap[1][s][:, :, :], 100.0, None, ALU.add) \
                            .then_inc(sig("caps1"), 1)

                    def cross(l):
                        for t in range(NT):
                            for s in range(STREAMS):
                                pool.wait_ge(sig("max_found"), (l * NT + t) * STREAMS + s + 1)
                                a = big[s][:, t, :].rearrange("p (h k) -> p h k", k=CTX)
                                pool.tensor_tensor(a, a, mx[s][:, t, :].unsqueeze(2).broadcast_to([P, XH, CTX]),
                                                   ALU.subtract).then_inc(sig("shifted"), 1)

                    def experts():
                        for s in range(STREAMS):
                            pool.wait_ge(sig("compared"), s + 1)
                            link(pool.tensor_tensor(cmpb[s][:, :, :, :], cmpb[s][:, :, :, :], lower[:, :, :, :], ALU.mult))
                            pool.tensor_tensor(cmpa[s][:, :, :, :], cmpa[s][:, :, :, :], cmpb[s][:, :, :, :], ALU.add) \
                                .then_inc(sig("beaten_by"), 1)

                    def attention_end(s):
                        pool.wait_ge(sig("mean_square"), s + 1)
                        pool.tensor_tensor(rzo[s][:, :, 0], ms[s][:, :], neg_half[:, 0:NT * AH], ALU.pow) \
                            .then_inc(sig("head_rstd"), 1)

                    rstds(0)
                    for s in range(STREAMS):
                        caps0(s)
                    recurrence()
                    rstds(1)
                    biases(1, "bo_x0")
                    cross(0)
                    rstds(2)
                    experts()
                    rstds(3)
                    biases(3, "bo_a")
                    for s in range(STREAMS):
                        caps1(s)
                    for s in range(STREAMS):
                        attention_end(s)
                    rstds(4)
                    biases(4, "bo_x1")
                    cross(1)
                    rstds(5)
                    biases(5, "b2")

                @block.scalar
                def _(act):
                    def turn_out(k, s):
                        act.wait_ge(sig("xn_turned"), turn(k, s))
                        act.activation(xT[s][:, :], bk(s, 0), ACT.Copy).then_inc(sig("xT_ready"), 1)

                    def cross(l):
                        for s in range(STREAMS):
                            act.wait_ge(sig("q_made"), turn(l, s))
                            act.activation(qT[s][:, :], bk(s, 1), ACT.Identity, scale=XSCALE,
                                           bias=bq_scaled[:, l:l + 1]).then_inc(sig("q_ready"), 1)
                        for t in range(NT + 1):
                            for s in range(STREAMS):
                                if t < NT:
                                    act.wait_ge(sig("shifted"), (l * NT + t) * STREAMS + s + 1)
                                    act.activation(big[s][:, t, :], big[s][:, t, :], ACT.Exp) \
                                        .then_inc(sig("weights"), 1)
                            for s in range(STREAMS):
                                if t:
                                    act.wait_ge(sig("weights_turned"), (l * NT + t - 1) * STREAMS + s + 1)
                                    act.activation(big2[s][:, t - 1, :], bk(s, (t - 1) % 2), ACT.Copy) \
                                        .then_inc(sig("weightsT_ready"), 1)

                    for s in range(STREAMS):
                        turn_out(0, s)
                    for s in range(STREAMS):
                        turn_out(1, s)
                    cross(0)
                    for s in range(STREAMS):
                        turn_out(2, s)
                    for s in range(STREAMS):
                        act.wait_ge(sig("gate_logits"), s + 1)
                        act.activation(sg[s][:, :, :], bk(s, 3)[:, 0:NT * EXPERTS].rearrange("p (t e) -> p t e", t=NT),
                                       ACT.Exp, scale=-1.0).then_inc(sig("gate_exp"), 1)
                    for j in range(FCH):
                        if j == 2:
                            for s in range(STREAMS):
                                act.wait_ge(sig("comb_turned"), s + 1)
                                act.activation(combT[s][:, :], bk(s, 3).bitcast(BF16)[0:3 * EXPERTS, 0:T], ACT.Copy) \
                                    .then_inc(sig("combT_ready"), 1)
                        for s in range(STREAMS):
                            act.wait_ge(sig("gated"), turn(j, s))
                            if j >= 2:
                                act.wait_ge(sig("hidden"), turn(j - 2, s))
                            act.activation(big[s][:, j % 2, :], bk(s, 1), ACT.Tanh, scale=0.5) \
                                .then_inc(sig("gate_tanh"), 1)
                    for s in range(STREAMS):
                        turn_out(3, s)
                    for s in range(STREAMS):
                        for t in range(NT):
                            act.wait_ge(sig("qkv_made"), s * NT + t + 1)
                            act.activation(big[s][:, t // 2, 256 * (t % 2):256 * (t % 2) + 256], bk(s, t)[:, 0:256],
                                           ACT.Square).then_inc(sig("squares"), 1)
                            act.activation(vals[s][:, t, :, 0:HV],
                                           bk(s, t)[:, 256:384].rearrange("p (h d) -> p h d", h=AH),
                                           ACT.Copy).then_inc(sig("vals_ready"), 1)
                    for s in range(STREAMS):
                        act.wait_ge(sig("square_sums"), s + 1)
                        act.activation(ss[s][:, :, :], ss[s][:, :, :], ACT.Sqrt).then_inc(sig("lengths"), 1)
                    for s in range(STREAMS):
                        for name, part, b, got in (("q", qpart, 1, "q_turned"), ("k", kpart, 2, "k_turned")):
                            act.wait_ge(sig(got), s + 1)
                            act.activation(part[s][:, 0, :], bk(s, b), ACT.Copy).then_inc(sig(f"{name}part0"), 1)
                        for name, part, a in (("q", qpart, 0), ("k", kpart, 1)):
                            act.wait_ge(sig(f"{name}_rest"), s + 1)
                            act.activation(part[s][:, 1, :], big2[s][:, a, :], ACT.Copy).then_inc(sig(f"{name}part1"), 1)

                    def difference(n):
                        s, hp, c = unit(n)
                        a, _ = ROWS["gain"]
                        for hh in range(2):
                            h = 2 * hp + hh
                            act.wait_ge(sig("diff_made"), 2 * n + hh + 1)
                            if n >= 2:
                                act.wait_ge(sig("logits_made"), 2 * (n - 2) + hh + 1)
                            act.activation(gate_t[:, n % 2, hh, :], pair[:, hh, :], ACT.Tanh,
                                           scale=rows[:, a + h:a + h + 1]).then_inc(sig("gate_ready"), 1)

                    def exps(n):
                        act.wait_ge(sig("logits_made"), 2 * n + 2)
                        if n >= 2:
                            act.wait_ge(sig("unit_used"), n - 1)
                        for m in range(MAPS):
                            act.activation(prob[n % 2][:, :, m, :], logit[n % 2][:, :, m, :], ACT.Exp,
                                           scale=1.0 if m == 0 else -1.0).then_inc(sig("prob_ready"), 1)

                    difference(0)
                    for n in range(UNITS):
                        if n + 1 < UNITS:
                            difference(n + 1)
                        exps(n)
                    for s in range(STREAMS):
                        act.wait_ge(sig("y_turned"), s + 1)
                        act.activation(cT[s][:, :], bk(s, 1), ACT.Copy).then_inc(sig("y_ready"), 1)

                    for s in range(STREAMS):
                        turn_out(4, s)
                    cross(1)
                    for s in range(STREAMS):
                        turn_out(5, s)
                    for j in range(F1CH):
                        for s in range(STREAMS):
                            act.wait_ge(sig("f1_made"), turn(j, s))
                            act.activation(big[s][:, j, :], bk(s, 1 + j % 2), ACT.Relu, bias=col(f"b1_{j}")) \
                                .then_inc(sig("f1_hidden"), 1)

                @block.vector
                def _(dve):
                    links = [0]

                    def link(ins):
                        links[0] += 1
                        ins.then_inc(sig("dve_link"), 1)
                        dve.wait_ge(sig("dve_link"), links[0])

                    def moments(k, s):
                        if k == 0:
                            dve.wait_ge(sig(f"x_loaded{s}"), 16)
                        else:
                            dve.wait_ge(sig("x_done"), turn(k - 1, s))
                        for t in range(NT):
                            ins = dve.bn_stats(bst[s][:, t, :], x[s][:, t, :])
                        link(ins)
                        for t in range(NT):
                            ins = dve.bn_aggr(mv[s][:, t, :], bst[s][:, t, :])
                        ins.then_inc(sig("moments"), 1)

                    def normed(k):
                        for s in range(STREAMS):
                            dve.wait_ge(sig("rstd_ready"), turn(k, s))
                            if k:
                                dve.wait_ge(sig("xn_turned"), turn(k - 1, s))
                            for t in range(NT):
                                ins = dve.tensor_scalar(xn[s][:, t, :], x[s][:, t, :], mv[s][:, t, 0:1],
                                                        rstd[s][:, t:t + 1], ALU.subtract, ALU.mult)
                            ins.then_inc(sig("xn_ready"), 1)

                    def residual(k, s, b, made):
                        dve.wait_ge(sig(made), s + 1)
                        if k in (1, 3, 4, 5):
                            dve.wait_ge(sig(f"biased{k}"), s + 1)
                        dve.tensor_tensor(x[s][:, :, :], bk(s, b).rearrange("p (t d) -> p t d", t=NT),
                                          x[s][:, :, :], ALU.add).then_inc(sig("x_done"), 1)

                    def cross_blocks(l, s):
                        dve.wait_ge(sig("kv_made"), turn(l, s))
                        dve.scalar_tensor_tensor(key_blocks[s][:, :, :],
                                                 bk(s, 2)[:, 0:CTX].unsqueeze(1).broadcast_to([P, XH, CTX]),
                                                 col(f"bk{l}"), mask_k[:, :, :], ALU.add, ALU.mult)
                        vb = val_blocks[s][:, :, :]
                        link(dve.tensor_tensor(vb, bk(s, 3)[:, 0:P].rearrange("p (g c) -> p g c", g=NG),
                                               row(f"bv{l}").rearrange("p (g c) -> p g c", g=NG), ALU.add))
                        dve.tensor_tensor(vb, vb, mask_v[:, :, :, :].rearrange("p g h d -> p g (h d)"), ALU.mult) \
                            .then_inc(sig("kv_blocks"), 1)

                    def cross(l):
                        low = -BIG if l == 0 else -100.0
                        for s in range(STREAMS):
                            cross_blocks(l, s)
                        for t in range(NT):
                            for s in range(STREAMS):
                                if t == 0:
                                    dve.wait_ge(sig(f"caps{l}"), s + 1)
                                dve.wait_ge(sig("scores_made"), (l * NT + t) * STREAMS + s + 1)
                                dve.scalar_tensor_tensor(big[s][:, t, :].rearrange("p (h k) -> p h k", k=CTX),
                                                         bk(s, 2 + t % 2).rearrange("p (h k) -> p h k", k=CTX), low,
                                                         cap[l][s][:, t, :].unsqueeze(1).broadcast_to([P, XH, CTX]),
                                                         ALU.max, ALU.min).then_inc(sig("capped"), 1)
                            for s in range(STREAMS):
                                dve.wait_ge(sig("capped"), (l * NT + t) * STREAMS + s + 1)
                                dve.tensor_reduce(mx[s][:, t, :], big[s][:, t, :].rearrange("p (h k) -> p h k", k=CTX),
                                                  AX.X, ALU.max).then_inc(sig("max_found"), 1)

                    def cross_end(l, k):
                        for a in range(2):
                            for s in range(STREAMS):
                                dve.wait_ge(sig("weighed"), 4 * l + 2 * a + s + 1)
                                sums_over = xn[s][:, :, :].rearrange("p t d -> p (t d)")[:, a * HALF:(a + 1) * HALF]
                                link(dve.reciprocal(sums_over, bk(s, 2 + a)[:, HALF:T]))
                                dve.tensor_tensor(cT[s][:, a * HALF:(a + 1) * HALF], bk(s, 2 + a)[:, 0:HALF], sums_over,
                                                  ALU.mult).then_inc(sig("ctx_ready"), 1)
                        for s in range(STREAMS):
                            residual(k, s, 1, f"cross_out{l}")

                    for s in range(STREAMS):
                        moments(0, s)
                    normed(0)
                    for s in range(STREAMS):
                        dve.wait_ge(sig("states_in"), s + 1)
                        dve.tensor_tensor(big[s][:, 0, :], bk(s, 1), rot_in_c[:, :], ALU.mult)
                        dve.tensor_tensor(big[s][:, 1, :], bk(s, 2), rot_in_s[:, :], ALU.mult) \
                            .then_inc(sig("rotated_in"), 1)
                    for s in range(STREAMS):
                        dve.wait_ge(sig("rotated_in"), s + 1)
                        dve.tensor_tensor(big[s][:, 0, :], big[s][:, 0, :], big[s][:, 1, :], ALU.add) \
                            .then_inc(sig("scan_input"), 1)
                    for s in range(STREAMS):
                        dve.wait_ge(sig("scan_input"), s + 1)
                        dve.tensor_tensor_scan(big[s][:, 2, :], decay[:, 0:1].broadcast_to([P, T]), big[s][:, 0, :],
                                               0.0, ALU.mult, ALU.add).then_inc(sig("scanned"), 1)
                    for s in range(STREAMS):
                        dve.wait_ge(sig("scanned"), s + 1)
                        dve.tensor_tensor(big2[s][:, 0, :], big[s][:, 2, :], rot_out_c[:, :], ALU.mult) \
                            .then_inc(sig("rotated_out_c"), 1)
                    for s in range(STREAMS):
                        residual(0, s, 3, "lru_out")
                        moments(1, s)
                    normed(1)
                    cross(0)
                    cross_end(0, 1)
                    for s in range(STREAMS):
                        moments(2, s)
                    normed(2)
                    def hidden(j, s):
                        th, hid = big[s][:, j % 2, :], big2[s][:, j % 2, :]
                        dve.wait_ge(sig("gate_tanh"), turn(j, s))
                        if j >= 2:
                            dve.wait_ge(sig("down"), turn(j - 2, s))
                        link(dve.scalar_tensor_tensor(hid, th, 1.0, bk(s, 1), ALU.add, ALU.mult))
                        dve.wait_ge(sig("upped"), turn(j, s))
                        if FFN_ORDER[j] < RCH:
                            link(dve.tensor_tensor(hid, hid, bk(s, 2), ALU.mult))
                            dve.wait_ge(sig("comb_spread"), turn(j - 1, s))
                            dve.tensor_tensor(hid, hid, bk(s, 3), ALU.mult).then_inc(sig("hidden"), 1)
                        else:
                            dve.scalar_tensor_tensor(hid, hid, 0.5, bk(s, 2), ALU.mult, ALU.mult) \
                                .then_inc(sig("hidden"), 1)

                    for s in range(STREAMS):
                        dve.wait_ge(sig("gate_exp"), s + 1)
                        link(dve.tensor_scalar(sg[s][:, :, :], sg[s][:, :, :], 1.0, None, ALU.add))
                        dve.reciprocal(sg[s][:, :, :], sg[s][:, :, :]).then_inc(sig("gate_scores"), 1)
                    for s in range(STREAMS):
                        dve.wait_ge(sig("gate_scores"), s + 1)
                        sj = sg[s][:, :, :].unsqueeze(2).broadcast_to([P, NT, EXPERTS, EXPERTS])
                        se = sg[s][:, :, :].unsqueeze(3).broadcast_to([P, NT, EXPERTS, EXPERTS])
                        dve.tensor_tensor(cmpa[s][:, :, :, :], sj, se, ALU.is_gt)
                        dve.tensor_tensor(cmpb[s][:, :, :, :], sj, se, ALU.is_equal).then_inc(sig("compared"), 1)
                    for s in range(STREAMS):
                        for t in range(NT):
                            ins = dve.max(top[s][:, t, :], sg[s][:, t, :])
                    link(ins)
                    for s in range(STREAMS):
                        ins = dve.scalar_tensor_tensor(wsum[s][:, :], top[s][:, :, 0], 1e-20, top[s][:, :, 1],
                                                       ALU.add, ALU.add)
                    link(ins)
                    for s in range(STREAMS):
                        ins = dve.reciprocal(wsum[s][:, :], wsum[s][:, :])
                    link(ins)
                    for s in range(STREAMS):
                        dve.wait_ge(sig("beaten_by"), s + 1)
                        ins = dve.tensor_reduce(rank[s][:, :, :], cmpa[s][:, :, :, :], AX.X, ALU.add)
                    link(ins)
                    for s in range(STREAMS):
                        ins = dve.tensor_scalar(rank[s][:, :, :], rank[s][:, :, :], 1.5, 0.5 * ROUTE_SCALE,
                                                ALU.is_lt, ALU.mult)
                    link(ins)
                    for s in range(STREAMS):
                        ins = dve.tensor_tensor(cres[s][:, :, :], sg[s][:, :, :], rank[s][:, :, :], ALU.mult)
                    link(ins)
                    for s in range(STREAMS):
                        ins = dve.tensor_tensor(cres[s][:, :, :], cres[s][:, :, :],
                                                wsum[s][:, :].unsqueeze(2).broadcast_to([P, NT, EXPERTS]), ALU.mult)
                    link(ins)
                    for p in range(2):
                        for s in range(STREAMS):
                            ins = dve.tensor_copy(cpart[s][:, :, p, :], cres[s][:, :, :])
                        link(ins)
                        for s in range(STREAMS):
                            ins = dve.tensor_tensor(cres[s][:, :, :], cres[s][:, :, :], cpart[s][:, :, p, :], ALU.subtract)
                        link(ins)
                    for s in range(STREAMS):
                        dve.tensor_copy(cpart[s][:, :, 2, :], cres[s][:, :, :]).then_inc(sig("comb_ready"), 1)
                    for j in range(FCH):
                        for s in range(STREAMS):
                            hidden(j, s)
                    for s in range(STREAMS):
                        residual(2, s, 0, "ffn0_out")
                        moments(3, s)
                    normed(3)
                    for s in range(STREAMS):
                        dve.wait_ge(sig("squares"), NT * (s + 1))
                        dve.tensor_reduce(ss[s][:, :, :].rearrange("p t (b h) -> p (t b) h", h=AH),
                                          big[s][:, 0:2, :].rearrange("p a (b d h) -> p (a b) h d", d=AD, h=AH), AX.X, ALU.add) \
                            .then_inc(sig("square_sums"), 1)
                    for s in range(STREAMS):
                        dve.wait_ge(sig("lengths"), s + 1)
                        link(dve.tensor_scalar(ss[s][:, :, :], ss[s][:, :, :], 1e-6, None, ALU.max))
                        link(dve.reciprocal(ss[s][:, :, :], ss[s][:, :, :]))
                        link(dve.tensor_tensor(ss[s][:, :, 0:2 * AH], ss[s][:, :, 0:2 * AH],
                                               qscale[:, :, :].rearrange("p m h -> p (m h)").unsqueeze(1)
                                               .broadcast_to([P, NT, 2 * AH]), ALU.mult))
                        for t in range(NT):
                            split = "p (b d h) -> p b d h"
                            ins = dve.tensor_tensor(qkn[s][:, t, :].rearrange(split, d=AD, h=AH),
                                                    bk(s, t)[:, 0:256].rearrange(split, d=AD, h=AH),
                                                    ss[s][:, t, :].rearrange("p (b h) -> p b h", h=AH).unsqueeze(2)
                                                    .broadcast_to([P, 2 * MAPS, AD, AH]), ALU.mult)
                        ins.then_inc(sig("unit_vectors"), 1)
                    for s in range(STREAMS):
                        for a, part, b, got, gives in ((0, qpart, 1, "qpart0", "q_rest"), (1, kpart, 2, "kpart0", "k_rest")):
                            dve.wait_ge(sig(got), s + 1)
                            dve.tensor_tensor(big2[s][:, a, :], bk(s, b), part[s][:, 0, :], ALU.subtract) \
                                .then_inc(sig(gives), 1)
                        for name, part, a in (("q", qpart, 0), ("k", kpart, 1)):
                            dve.wait_ge(sig(f"{name}part1"), s + 1)
                            dve.tensor_tensor(part[s][:, 2, :], big2[s][:, a, :], part[s][:, 1, :], ALU.subtract) \
                                .then_inc(sig(f"{name}part2"), 1)

                    def logits(n):
                        if n == 0:
                            dve.wait_ge(sig("kpart2"), STREAMS)
                        for hh in range(2):
                            dve.wait_ge(sig("gate_ready"), 2 * n + hh + 1)
                            dve.wait_ge(sig("scores_ready"), 2 * n + hh + 1)
                            if n >= 2:
                                dve.wait_ge(sig("prob_ready"), 2 * (n - 1))
                            dve.tensor_tensor(logit[n % 2][:, hh, :, :], quad[:, hh, :, :],
                                              gate_t[:, n % 2, hh, :].unsqueeze(1).broadcast_to([P, MAPS, T]), ALU.add) \
                                .then_inc(sig("logits_made"), 1)

                    def heads_out(g):
                        dve.wait_ge(sig("unit_used"), KC * (g + 1))
                        if g >= 1:
                            dve.wait_ge(sig("heads_turned"), g)
                        dve.tensor_copy(accT[:, :], bank[0][:, :]).then_inc(sig("heads_out"), 1)

                    def heads_in(g):
                        s, hp = g // PAIRS, g % PAIRS
                        dve.wait_ge(sig("heads_turned"), g + 1)
                        dve.tensor_copy(on[s][:, :, 4 * hp:4 * hp + 4, :].rearrange("p t h d -> p t (h d)"),
                                        bank[1][:, :].rearrange("p (t c) -> p t c", t=NT)).then_inc(sig("heads_in"), 1)

                    shape = [P, NT * AH, HV]

                    def head_views(s):
                        o = on[s][:, :, :, :].rearrange("p t (h m) c -> p (t h) m c", m=MAPS)
                        y1 = qT[s][:, :].rearrange("p (h d) -> p h d", d=HV)
                        y2 = cT[s][:, :].rearrange("p (h d) -> p h d", d=HV)
                        return o, y1, y2, [peak[s][:, a, :] for a in range(4)]

                    def heads_over_sums(s):
                        o, y1, y2, pk = head_views(s)
                        dve.wait_ge(sig("heads_in"), 4 * (s + 1))
                        link(dve.reciprocal(rzo[s][:, :, :], o[:, :, :, HV]))
                        link(dve.tensor_scalar(rzo[s][:, :, 1], rzo[s][:, :, 1], lam[:, 0:1], None, ALU.mult))
                        dve.tensor_tensor(y1, o[:, :, 0, 0:HV], rzo[s][:, :, 0].unsqueeze(2).broadcast_to(shape), ALU.mult)
                        link(dve.tensor_tensor(y2, o[:, :, 1, 0:HV], rzo[s][:, :, 1].unsqueeze(2).broadcast_to(shape), ALU.mult))

                    def heads_difference(s):
                        o, y1, y2, pk = head_views(s)
                        link(dve.tensor_tensor(y1, y1, y2, ALU.subtract))
                        link(dve.tensor_reduce(pk[0], y1, AX.X, ALU.max, apply_absolute_value=True))

                    def heads_scaled(s):
                        o, y1, y2, pk = head_views(s)
                        link(dve.tensor_scalar(pk[0], pk[0], 1e-15, None, ALU.max))
                        link(dve.reciprocal(pk[1], pk[0]))
                        dve.tensor_scalar(pk[2], pk[0], 2.0 ** -64, 1.0e3, ALU.mult, ALU.min)
                        link(dve.tensor_tensor(y1, y1, pk[1].unsqueeze(2).broadcast_to(shape), ALU.mult))

                    def heads_squares(s):
                        o, y1, y2, pk = head_views(s)
                        link(dve.tensor_tensor(y2, y1, y1, ALU.mult))
                        dve.scalar_tensor_tensor(pk[3], pk[1], RMS_EPS, pk[1], ALU.mult, ALU.mult)
                        link(dve.tensor_reduce(pk[0], y2, AX.X, ALU.add))
                        dve.scalar_tensor_tensor(ms[s][:, :], pk[0], 1.0 / HV, pk[3], ALU.mult, ALU.add) \
                            .then_inc(sig("mean_square"), 1)

                    def heads_guard(s):
                        o, y1, y2, pk = head_views(s)
                        link(dve.tensor_tensor(pk[2], pk[2], pk[2], ALU.mult))
                        link(dve.tensor_tensor(pk[2], pk[2], pk[0], ALU.mult))
                        link(dve.tensor_scalar(pk[2], pk[2], 1.0, None, ALU.is_lt))

                    def heads_normed(s):
                        o, y1, y2, pk = head_views(s)
                        y = xn[s][:, :, :].rearrange("p t (h d) -> p (t h) d", d=HV)
                        dve.wait_ge(sig("head_rstd"), s + 1)
                        link(dve.tensor_tensor(pk[2], pk[2], rzo[s][:, :, 0], ALU.mult))
                        link(dve.tensor_tensor(y1, y1, pk[2].unsqueeze(2).broadcast_to(shape), ALU.mult))
                        dve.tensor_tensor(y, y1, sub_half[:, :].unsqueeze(1).broadcast_to(shape), ALU.mult) \
                            .then_inc(sig("y_made"), 1)

                    HEADS_END = (heads_over_sums, heads_difference, heads_scaled, heads_squares, heads_guard,
                                 heads_normed)

                    for n in range(UNITS):
                        logits(n)
                        g, c = n // KC - 1, n % KC
                        if g >= 0 and c == 1:
                            heads_out(g)
                        if g >= 0 and c == 3:
                            heads_in(g)
                        a = (n - (PAIRS + 1) * KC) // 2
                        if c % 2 == 0 and 0 <= a < len(HEADS_END):
                            HEADS_END[a](0)
                    heads_out(GROUPS - 1)
                    heads_in(GROUPS - 1)
                    for step in HEADS_END[0:3]:
                        step(1)
                    residual(3, 0, 2, "attn_out")
                    moments(4, 0)
                    for step in HEADS_END[3:]:
                        step(1)
                    residual(3, 1, 2, "attn_out")
                    moments(4, 1)
                    normed(4)
                    cross(1)
                    cross_end(1, 4)
                    for s in range(STREAMS):
                        moments(5, s)
                    normed(5)
                    for s in range(STREAMS):
                        residual(5, s, 3, "ffn1_out")

                @block.tensor
                def _(pe):
                    def keep_warm(dst, count):
                        for _ in range(count):
                            pe.matmul(dst, identb[:, :], warm_rhs[:, :], start=True, stop=True)

                    def turn_in(k, s):
                        if k:
                            pe.wait_ge(sig("x_done"), turn(k - 1, s))
                            if s == 0:
                                keep_warm(bk(0, 0), WARM_UP_NORM)
                        pe.wait_ge(sig("xn_ready"), turn(k, s))
                        for t in range(NT):
                            ins = pe.transpose(bk(s, 0)[:, t * P:(t + 1) * P], xn[s][:, t, :], ident[:, :])
                        ins.then_inc(sig("xn_turned"), 1)

                    def to_tokens(dst, pairs, done):
                        for t in range(NT):
                            for a, (lhs, rhs) in enumerate(pairs):
                                ins = pe.matmul(dst[:, t * P:(t + 1) * P], lhs[:, t * P:(t + 1) * P], rhs,
                                                start=(a == 0), stop=(a == len(pairs) - 1))
                        ins.then_inc(sig(done), 1)

                    def cross(l, k):
                        pe.wait_ge(sig(f"w_x{l}"), 16)
                        for s in range(STREAMS):
                            if l == 0:
                                pe.wait_ge(sig(f"ctx_loaded{s}"), 16)
                            pe.wait_ge(sig("x_done"), turn(k - 1, s))
                            c4 = ctxT[s][:, :, :].rearrange("p h k -> p (h k)")
                            pe.matmul(bk(s, 2)[:, 0:CTX], w(f"x{l}k"), ctxT[s][:, 0, :], start=True, stop=True)
                            pe.matmul(bk(s, 3)[:, 0:P], c4, w(f"x{l}v"), start=True, stop=True) \
                                .then_inc(sig("kv_made"), 1)
                        for s in range(STREAMS):
                            turn_in(k, s)
                        for s in range(STREAMS):
                            pe.wait_ge(sig("xT_ready"), turn(k, s))
                            pe.matmul(bk(s, 1), w(f"x{l}q"), xT[s][:, :], start=True, stop=True) \
                                .then_inc(sig("q_made"), 1)
                        for t in range(NT):
                            for s in range(STREAMS):
                                pe.wait_ge(sig("q_ready"), turn(l, s))
                                pe.wait_ge(sig("kv_blocks"), turn(l, s))
                                if t >= 2:
                                    pe.wait_ge(sig("capped"), (l * NT + t - 2) * STREAMS + s + 1)
                                pe.matmul(bk(s, 2 + t % 2), qT[s][:, t * P:(t + 1) * P],
                                          key_blocks[s][:, :, :].rearrange("p h k -> p (h k)"),
                                          start=True, stop=True).then_inc(sig("scores_made"), 1)
                        def weigh_keys(a):
                            for s in range(STREAMS):
                                pe.wait_ge(sig("weightsT_ready"), (l * NT + 2 * a + 1) * STREAMS + s + 1)
                                for half, lhs in ((0, None), (1, mask_v[:, 0, :, :].rearrange("p h d -> p (h d)"))):
                                    for g in range(NG):
                                        ins = pe.matmul(bk(s, 2 + a)[32 * g:32 * g + 32, half * HALF:(half + 1) * HALF],
                                                        val_blocks[s][:, g, :] if lhs is None else lhs,
                                                        big2[s][:, 2 * a:2 * a + 2, g * P:(g + 1) * P],
                                                        start=True, stop=True)
                                ins.then_inc(sig("weighed"), 1)

                        for t in range(NT):
                            for s in range(STREAMS):
                                pe.wait_ge(sig("weights"), (l * NT + t) * STREAMS + s + 1)
                                if t >= 2:
                                    pe.wait_ge(sig("weightsT_ready"), (l * NT + t - 2) * STREAMS + s + 1)
                                for g in range(NG):
                                    ins = pe.transpose(bk(s, t % 2)[:, g * P:(g + 1) * P],
                                                       big[s][:, t, g * P:(g + 1) * P], ident[:, :])
                                ins.then_inc(sig("weights_turned"), 1)
                            if t == 2:
                                weigh_keys(0)
                        weigh_keys(1)
                        for a in range(2):
                            for s in range(STREAMS):
                                pe.wait_ge(sig("ctx_ready"), 4 * l + 2 * a + s + 1)
                                if a == 0:
                                    pe.wait_ge(sig("weightsT_ready"), (l * NT + NT - 1) * STREAMS + s + 1)
                                for t in (2 * a, 2 * a + 1):
                                    ins = pe.matmul(bk(s, 1)[:, t * P:(t + 1) * P], cT[s][:, t * P:(t + 1) * P],
                                                    w(f"x{l}o"), start=True, stop=True)
                                if a == 1:
                                    ins.then_inc(sig(f"cross_out{l}"), 1)

                    pe.wait_ge(sig("w_lru"), 16)
                    for s in range(STREAMS):
                        turn_in(0, s)
                    for s in range(STREAMS):
                        pe.wait_ge(sig("xT_ready"), s + 1)
                        pe.matmul(bk(s, 1), w("bt1"), xT[s][:, :], start=True, stop=True)
                        pe.matmul(bk(s, 2), w("bt2"), xT[s][:, :], start=True, stop=True).then_inc(sig("states_in"), 1)
                    for s in range(STREAMS):
                        pe.wait_ge(sig("rotated_out_c"), s + 1)
                        pe.wait_ge(sig("rotated_out_s"), s + 1)
                        to_tokens(bk(s, 3), [(big2[s][:, 0, :], w("wc1")), (big2[s][:, 1, :], w("wc2")),
                                             (xT[s], w("dt"))], "lru_out")
                    cross(0, 1)

                    pe.wait_ge(sig("w_ffn0"), 16)
                    for s in range(STREAMS):
                        turn_in(2, s)
                    for s in range(STREAMS):
                        pe.wait_ge(sig("xT_ready"), turn(2, s))
                        for t in range(NT):
                            ins = pe.matmul(bk(s, 3)[:, t * EXPERTS:(t + 1) * EXPERTS], xT[s][:, t * P:(t + 1) * P],
                                            w("gate"), start=True, stop=True)
                        ins.then_inc(sig("gate_logits"), 1)

                    def turn_comb(s):
                        pe.wait_ge(sig("gate_exp"), s + 1)
                        pe.wait_ge(sig("comb_ready"), s + 1)
                        for t in range(NT):
                            ins = pe.transpose(bk(s, 3).bitcast(BF16)[0:3 * EXPERTS, t * P:(t + 1) * P],
                                               cpart[s][:, t, :, :].rearrange("p a e -> p (a e)"), identb[:, :])
                        ins.then_inc(sig("comb_turned"), 1)

                    def up(j, s):
                        if j:
                            pe.wait_ge(sig("hidden"), turn(j - 1, s))
                        c = FFN_ORDER[j]
                        pe.matmul(bk(s, 1), wch("wg", c), xT[s][:, :], start=True, stop=True).then_inc(sig("gated"), 1)
                        pe.matmul(bk(s, 2), wch("wu", c), xT[s][:, :], start=True, stop=True).then_inc(sig("upped"), 1)

                    def spread_comb(j, s):
                        pe.wait_ge(sig("combT_ready"), s + 1)
                        pe.matmul(bk(s, 3), expert_rows[:, FFN_ORDER[j], :], combT[s][:, :], start=True, stop=True) \
                            .then_inc(sig("comb_spread"), 1)

                    def down(j, s):
                        pe.wait_ge(sig("hidden"), turn(j, s))
                        for t in range(NT):
                            ins = pe.matmul(bk(s, 0)[:, t * P:(t + 1) * P], big2[s][:, j % 2, t * P:(t + 1) * P],
                                            wch("wd", FFN_ORDER[j]), start=(j == 0 and t == 0), stop=(j == FCH - 1),
                                            skip_group_check=True)
                        ins.then_inc(sig("down" if j < FCH - 1 else "ffn0_out"), 1)

                    for j in range(FCH):
                        for s in range(STREAMS):
                            up(j, s)
                            if j >= 2:
                                spread_comb(j, s)
                            if j:
                                down(j - 1, s)
                        if j == 1:
                            for s in range(STREAMS):
                                turn_comb(s)
                            for s in range(STREAMS):
                                spread_comb(1, s)
                    for s in range(STREAMS):
                        down(FCH - 1, s)

                    pe.wait_ge(sig("w_attn"), 16)
                    for s in range(STREAMS):
                        turn_in(3, s)
                    for s in range(STREAMS):
                        pe.wait_ge(sig("xT_ready"), turn(3, s))
                        for t in range(NT):
                            pe.matmul(bk(s, t)[:, 0:384], xT[s][:, t * P:(t + 1) * P], w("aqkv"),
                                      start=True, stop=True).then_inc(sig("qkv_made"), 1)
                    for s in range(STREAMS):
                        pe.wait_ge(sig("unit_vectors"), s + 1)
                        pe.wait_ge(sig("vals_ready"), NT * (s + 1))
                        for a, got in ((0, "q_turned"), (1, "k_turned")):
                            for t in range(NT):
                                ins = pe.transpose(bk(s, 1 + a)[:, t * P:(t + 1) * P],
                                                   qkn[s][:, t, a * P:(a + 1) * P], ident[:, :])
                            ins.then_inc(sig(got), 1)

                    pe.wait_ge(sig("k_rest"), STREAMS)
                    keep_warm(bank[1][:, :], WARM_UP)

                    def differences(n):
                        s, hp, c = unit(n)
                        kc = slice(c * P, (c + 1) * P)
                        if n == 0:
                            pe.wait_ge(sig("k_rest"), STREAMS)
                            pe.wait_ge(sig("q_rest"), STREAMS)
                            pe.wait_ge(sig("rows_zeroed"), 16 * 2 * MAPS * STREAMS)
                        if hp == 0 and c == 0:
                            pe.wait_ge(sig(f"stacked{s}"), 16 * 2 * MAPS)
                        for hh in range(2):
                            h = 2 * hp + hh
                            if n >= 1:
                                pe.wait_ge(sig("gate_ready"), 2 * (n - 1) + hh + 1)
                            pe.matmul(pair[:, hh, :], kstack[s][:, h, kc], qstack[s][:, h, :],
                                      start=True, stop=True).then_inc(sig("diff_made"), 1)

                    def scores(n):
                        s, hp, c = unit(n)
                        kc = slice(c * P, (c + 1) * P)
                        for hh in range(2):
                            h = 2 * hp + hh
                            if n >= 1:
                                pe.wait_ge(sig("logits_made"), 2 * (n - 1) + hh + 1)
                            for m in range(MAPS):
                                r = slice(MAP2 * m, MAP2 * m + MAP2)
                                ins = pe.matmul(quad[:, hh, m, :], kstack[s][r, h, kc], qstack[s][r, h, :],
                                                start=True, stop=True)
                            ins.then_inc(sig("scores_ready"), 1)

                    def weigh(n):
                        s, hp, c = unit(n)
                        g = n // KC
                        pe.wait_ge(sig("prob_ready"), 2 * n + 2)
                        if c == 0 and g >= 1:
                            pe.wait_ge(sig("heads_out"), g)
                        for hh in range(2):
                            for m in range(MAPS):
                                q = 32 * (2 * hh + m)
                                ins = pe.matmul(bank[0][q:q + 32, :], vals[s][:, c, 2 * hp + hh, :],
                                                prob[n % 2][:, hh, m, :], start=(c == 0), stop=(c == KC - 1),
                                                skip_group_check=True)
                        ins.then_inc(sig("unit_used"), 1)

                    def heads_turn(g):
                        pe.wait_ge(sig("heads_out"), g + 1)
                        if g >= 1:
                            pe.wait_ge(sig("heads_in"), g)
                        for t in range(NT):
                            ins = pe.transpose(bank[1][:, t * P:(t + 1) * P], accT[:, t * P:(t + 1) * P], ident[:, :])
                        ins.then_inc(sig("heads_turned"), 1)

                    LAG = 3
                    for n in range(UNITS + LAG):
                        if n < UNITS:
                            differences(n)
                        if n >= LAG:
                            weigh(n - LAG)
                            if n >= KC + LAG and (n - LAG) % KC == 0:
                                heads_turn((n - LAG) // KC - 1)
                        if n < UNITS:
                            scores(n)
                    heads_turn(GROUPS - 1)
                    for s in range(STREAMS):
                        pe.wait_ge(sig("y_made"), s + 1)
                        pe.wait_ge(sig("logits_made"), 2 * UNITS)
                        for t in range(NT):
                            ins = pe.transpose(bk(s, 1)[:, t * P:(t + 1) * P], xn[s][:, t, :], ident[:, :])
                        ins.then_inc(sig("y_turned"), 1)
                        if s == 0:
                            pe.wait_ge(sig("gate_ready"), 2 * UNITS)
                        pe.wait_ge(sig("y_ready"), s + 1)
                        to_tokens(bk(s, 2), [(cT[s], w("ao"))], "attn_out")
                    cross(1, 4)
                    for s in range(STREAMS):
                        turn_in(5, s)
                    for j in range(F1CH):
                        for s in range(STREAMS):
                            pe.wait_ge(sig("xT_ready"), turn(5, s))
                            if j >= 2:
                                pe.wait_ge(sig("f1_hidden"), turn(j - 2, s))
                            pe.matmul(bk(s, 1 + j % 2), wch("f1w1", j), xT[s][:, :], start=True, stop=True) \
                                .then_inc(sig("f1_made"), 1)
                    for s in range(STREAMS):
                        pe.wait_ge(sig("f1_hidden"), turn(F1CH - 1, s))
                        to_tokens(bk(s, 3), [(big[s][:, j, :], wch("f1w2", j)) for j in range(F1CH)], "ffn1_out")

        with nc.Fori(0, B // STREAMS) as i:
            body(i)
            engines = [nc.gpsimd, nc.sync, nc.scalar, nc.vector, nc.tensor]
            for j, name in enumerate(n for n in sems if n not in keep):
                engines[j % len(engines)].sem_clear(sems[name])
            nc.all_engine_barrier()


def kernel(**inputs):
    import concourse.bacc as bacc
    from concourse.bass_utils import run_bass_kernel_spmd as run

    v = {k: np.asarray(a) for k, a in inputs.items()}
    t = lambda n: v[n].T
    routed = lambda n: v[n].reshape(EXPERTS * EI, D).T
    maps_first = lambda n: v[n].reshape(AH, MAPS, AD, D).transpose(1, 2, 0, 3).reshape(D, D).T
    down = v["L0_ffn_w_down"].transpose(0, 2, 1).reshape(RCH, P, D).transpose(1, 0, 2).reshape(P, RCH * D)
    w2 = v["L1_ffn_W2"].T.reshape(F1CH, P, D).transpose(1, 0, 2).reshape(P, F1CH * D)
    w = np.concatenate([
        t("L0_attn_B_re"), t("L0_attn_B_im"), t("L0_attn_B_im"), t("L0_attn_B_re"),
        np.concatenate([t("L0_attn_C_re"), t("L0_attn_C_im")]),
        np.concatenate([t("L0_attn_C_im"), t("L0_attn_C_re")]), t("L0_attn_D"),
        t("L1_ffn_W1"), w2,
        t("L0_xattn_Wq"), t("L0_xattn_Wk"), t("L0_xattn_Wv"), t("L0_xattn_Wo"),
        t("L0_ffn_gate_weight"), routed("L0_ffn_w_gate"), t("L0_ffn_ws_gate"),
        routed("L0_ffn_w_up"), t("L0_ffn_ws_up"), down, t("L0_ffn_ws_down"),
        maps_first("L1_attn_Wq"), maps_first("L1_attn_Wk"), t("L1_attn_Wv"), t("L1_attn_Wo"),
        t("L1_xattn_wq"), t("L1_xattn_wk"), t("L1_xattn_wv"), t("L1_xattn_wo")], axis=1)
    by_tile = lambda m: m.reshape(B, NT, P, CTX).transpose(0, 2, 1, 3)
    twice = lambda n: np.concatenate([v[n], v[n]])
    cols = np.stack([twice("L0_attn_nu_log"), twice("L0_attn_theta_log"), twice("L0_attn_gamma_log"),
                     v["L0_xattn_bq"], v["L0_xattn_bk"], v["L1_xattn_bq"], v["L1_xattn_bk"],
                     *v["L1_ffn_b1"].reshape(F1CH, P)], axis=1)
    rows = np.concatenate([v["L0_xattn_bv"], v["L1_xattn_bv"], v["L0_xattn_bo"], v["L1_attn_bo"],
                           v["L1_xattn_bo"], v["L1_ffn_b2"], v["L1_attn_delta_gain"], v["L1_attn_cos_head_delta"],
                           v["L1_attn_cos_logit_scale_raw"].reshape(1), v["L1_attn_lambda_q1"],
                           v["L1_attn_lambda_k1"], v["L1_attn_lambda_q2"], v["L1_attn_lambda_k2"],
                           v["L1_attn_subln_weight"]])
    assert w.shape == (P, WTOTAL) and cols.shape == (P, len(COLS)) and rows.shape == (RTOTAL,)
    arrays = {"x": v["x"], "ctx": v["ctx_1024"].transpose(0, 2, 1),
              "mask0": by_tile(v["mask_BxSxS2_bf0"]), "mask1": by_tile(v["mask_Bx1xSxS2_ik1"]), "w": w, "cols": cols, "rows": rows}
    arrays = {k: np.ascontiguousarray(a) for k, a in arrays.items()}
    nc = bacc.Bacc("TRN2", target_bir_lowering=False, num_devices=1)
    args = [nc.dram_tensor(f"{k}_in", a.shape, mybir.dt.from_np(a.dtype), kind="ExternalInput").ap()
            for k, a in arrays.items()]
    args.append(nc.dram_tensor("out", (B, T, D), F32, kind="ExternalOutput").ap())
    build(nc, *args)
    r = run(nc, [{f"{k}_in": a for k, a in arrays.items()}], core_ids=[0])
    return r.results[0]["out"]
```

```python
import numpy as np
import concourse.bass as bass
from concourse import mybir
from contextlib import ExitStack

F32 = mybir.dt.float32
BF16 = mybir.dt.bfloat16
I32 = mybir.dt.int32
U8 = mybir.dt.uint8
ALU = mybir.AluOpType
ACT = mybir.ActivationFunctionType
AX = mybir.AxisListType

B, T, D = 4, 512, 128
P = 128
NT = T // P
STREAMS = 2
TURNS = B // STREAMS
NSTATE = 64
CTX = 32
XH, XD = 16, 8
HG = P // CTX
NG = XH // HG
XSCALE = 1.0 / float(np.sqrt(XD))
EXPERTS, EI = 8, 64
EPC = P // EI
RCH = EXPERTS // EPC
FCH = RCH + 1
FFN_ORDER = (RCH, *range(RCH))
ROUTE_SCALE = 2.5
AH, AD = 8, 8
MAPS = 2
HV = 2 * AD
F1CH = 4
LN_EPS = 1e-5
RMS_EPS = 1e-5
HALF = T // 2
KC = T // P
PAIRS = AH // 2
GROUPS = STREAMS * PAIRS
UNITS = GROUPS * KC
WARM_UP = 6
WARM_UP_NORM = 14
WARM_UP_HEADS = 14
WARM_UP_SCAN = 12
BIG = 3.0e38

WCOLS, _at = {}, 0
for _name, _n in [("bt1", 128), ("bt2", 128), ("wc1", 128), ("wc2", 128), ("dt", 128),
                  ("f1w1", 512), ("f1w2", 512),
                  ("x0q", 128), ("x0k", 128), ("x0v", 128), ("x0o", 128),
                  ("gate", EXPERTS), ("wg", FCH * P), ("wu", FCH * P), ("wd", FCH * P),
                  ("aqkv", 384), ("ao", 128),
                  ("x1q", 128), ("x1k", 128), ("x1v", 128), ("x1o", 128)]:
    WCOLS[_name] = (_at, _at + _n)
    _at += _n
WTOTAL = _at
COLS = {n: i for i, n in enumerate(["nu", "theta", "gamma", "bq0", "bk0", "bq1", "bk1",
                                    "b1_0", "b1_1", "b1_2", "b1_3"])}
ROWS, _at = {}, 0
for _name, _n in [("bv0", 128), ("bv1", 128), ("bo_x0", 128), ("bo_a", 128), ("bo_x1", 128), ("b2", 128),
                  ("gain", AH), ("head_delta", AH), ("raw", 1), ("lq1", AD), ("lk1", AD), ("lq2", AD),
                  ("lk2", AD), ("subln", HV)]:
    ROWS[_name] = (_at, _at + _n)
    _at += _n
RTOTAL = _at
QGROUPS = ((0, 3, 1), (3, 5, 1), (5, 6, 1))
KGROUPS = ((1, 6, 2), (2, 5, 2), (0, 1, 1))
PRODUCTS = 6
KROWS = PRODUCTS * AD
MAP2 = 64


def build(nc, x_in, ctx_in, m0_in, m1_in, w_in, cols_in, rows_in, out):
    ctx = ExitStack()
    with ctx:
        def sb(name, shape, dt=F32):
            return ctx.enter_context(nc.sbuf_tensor(name, shape, dt))

        sems = {}

        def sig(name):
            if name not in sems:
                sems[name] = ctx.enter_context(nc.semaphore(name))
            return sems[name]

        wt = sb("wt", [P, WTOTAL])
        cols = sb("cols", [P, len(COLS)])
        rows = sb("rows", [P, RTOTAL])
        ident = sb("ident", [P, P])
        identb = sb("identb", [P, P], BF16)
        mask_k = sb("mask_k", [P, XH, CTX])
        mask_v = sb("mask_v", [P, NG, HG, XD])
        expert_rows = sb("expert_rows", [3 * EXPERTS, RCH, P], BF16)
        lower = sb("lower", [P, NT, EXPERTS, EXPERTS])
        neg_half = sb("neg_half", [P, 32])
        rot_in_c = sb("rot_in_c", [P, T])
        rot_in_s = sb("rot_in_s", [P, T])
        rot_out_c = sb("rot_out_c", [P, T])
        rot_out_s = sb("rot_out_s", [P, T])
        decay = sb("decay", [P, 1])
        bq_scaled = sb("bq_scaled", [P, 2])
        lam = sb("lam", [P, 1])
        qscale = sb("qscale", [P, MAPS, AH])
        sub_half = sb("sub_half", [P, HV])

        def w(name):
            a, b = WCOLS[name]
            return wt[:, a:b]

        def wch(name, j):
            a, _ = WCOLS[name]
            return wt[:, a + j * P:a + (j + 1) * P]

        def col(name):
            return cols[:, COLS[name]:COLS[name] + 1]

        def row(name):
            a, b = ROWS[name]
            return rows[:, a:b]

        def per_stream(name, shape, dt=F32):
            return [sb(f"{name}{s}", shape, dt) for s in range(STREAMS)]

        x = per_stream("x", [P, NT, D])
        x_next = per_stream("x_next", [P, NT, D])
        xn = per_stream("xn", [P, NT, D])
        xT = per_stream("xT", [P, T])
        bst = per_stream("bst", [P, NT, 6])
        mv = per_stream("mv", [P, NT, 2])
        rstd = per_stream("rstd", [P, NT])
        veps = per_stream("veps", [P, NT])
        big = per_stream("big", [P, 4, T])
        big2 = per_stream("big2", [P, 4, T])
        ctxT = per_stream("ctxT", [P, HG, CTX])
        key_blocks = per_stream("key_blocks", [P, XH, CTX])
        val_blocks = per_stream("val_blocks", [P, NG, HG * XD])
        m0 = per_stream("m0", [P, NT, CTX], U8)
        m1 = per_stream("m1", [P, NT, CTX], I32)
        cap = [per_stream(f"cap{l}", [P, NT, CTX]) for l in range(2)]
        cap_part = per_stream("cap_part", [P, NT, CTX])
        qT = per_stream("qT", [P, T])
        accT = sb("accT", [P, T])
        cT = per_stream("cT", [P, T])
        mx = per_stream("mx", [P, NT, XH])
        sg = per_stream("sg", [P, NT, EXPERTS])
        top = per_stream("top", [P, NT, EXPERTS])
        cmpa, cmpb = ([b[:, 3, a * HALF:(a + 1) * HALF].rearrange("p (t e f) -> p t e f", t=NT, e=EXPERTS)
                       for b in big2] for a in range(2))
        rank = per_stream("rank", [P, NT, EXPERTS])
        wsum = per_stream("wsum", [P, NT])
        cpart = per_stream("cpart", [P, NT, 3, EXPERTS], BF16)
        cres = per_stream("cres", [P, NT, EXPERTS])
        combT = per_stream("combT", [3 * EXPERTS, T], BF16)
        ss = per_stream("ss", [P, NT, 4 * AH])
        qpart = per_stream("qpart", [P, 3, T], BF16)
        kpart = per_stream("kpart", [P, 3, T], BF16)
        qstack = per_stream("qstack", [P, AH, T], BF16)
        kstack = per_stream("kstack", [P, AH, T], BF16)
        vals = per_stream("vals", [P, NT, AH, 32])
        on = per_stream("on", [P, NT, AH * MAPS, 32])
        qkn = [o[:, 0:2, :, :].rearrange("p a h c -> p (a h c)").rearrange("p (t c) -> p t c", t=NT) for o in on]
        rzo = per_stream("rzo", [P, NT * AH, MAPS])
        ms = per_stream("ms", [P, NT * AH])
        peak = per_stream("peak", [P, 4, NT * AH])
        gate_t = sb("gate_t", [P, 2, 2, T])
        logit = [b[:, :, :].rearrange("p (c m) t -> p c m t", c=2) for b in big2]
        more = [sb(f"more{a}", [P, 4, T]) for a in range(2)]
        prob = [b[:, :, :].rearrange("p (c m) t -> p c m t", c=2) for b in (*big, *more)]

        parts_dram = nc.dram_tensor("parts", (STREAMS, 2, PRODUCTS, P, T), BF16, kind="Internal").ap()

        bank = [ctx.enter_context(nc.psum_tensor(f"bank{i}", [P, T], F32)) for i in range(2)]
        quad = ctx.enter_context(nc.psum_tensor("quad", [P, 2, MAPS, T], F32))
        pair = ctx.enter_context(nc.psum_tensor("pair", [P, 2, T], F32))

        def bk(s, i):
            return [[bank[0][:, :], quad[:, 0, 0, :], quad[:, 0, 1, :], pair[:, 0, :]],
                    [bank[1][:, :], quad[:, 1, 0, :], quad[:, 1, 1, :], pair[:, 1, :]]][s][i]

        def turn(k, s):
            return STREAMS * k + s + 1

        WSECT = [("w_lru", "bt1", "dt"), ("w_ffn1", "f1w1", "f1w2"), ("w_x0", "x0q", "x0o"),
                 ("w_ffn0", "gate", "wd"), ("w_attn", "aqkv", "ao"), ("w_x1", "x1q", "x1o")]

        def unit(n):
            return n // (PAIRS * 4), 2 * (n // 4 % PAIRS) + n % 2, 2 * (n // 2 % 2)

        tab_c, tab_s, tmp = big[0][:, 0, :], big[0][:, 1, :], big[0][:, 2, :]
        small = sb("small", [P, 64])
        smalli = sb("smalli", [P, 4], I32)
        expt = sb("expt", [P, 3, 4])
        expi = sb("expi", [P, 4], I32)
        zc = sb("zc", [P, 10])
        zs = sb("zs", [P, 10])
        ones_sq = big[1][:, 2, 0:P]
        scrap = sb("scrap", [P, 1])
        zeros = big[1][0:MAP2 - KROWS, 3, 0:T // 2].bitcast(BF16)

        def load_x(queue, s, batch, done):
            queue.dma_start(x_next[s][:, :, :], x_in[bass.ds(batch, 1)].rearrange("b (t p) d -> p (b t) d", p=P)) \
                .then_inc(sig(done), 16)

        def prologue():
            with nc.Block() as block:
                @block.sync
                def _(sp):
                    sp.dma_start(cols[:, :], cols_in).then_inc(sig("cols_loaded"), 16)
                    for s in range(STREAMS):
                        load_x(sp, s, s, "x_loaded")
                    for name, a, b in WSECT[:3]:
                        c0, c1 = WCOLS[a][0], WCOLS[b][1]
                        sp.dma_start(wt[:, c0:c1], w_in[:, c0:c1]).then_inc(sig(name), 16)
                    sp.wait_ge(sig("zeros"), 1)
                    for s in range(STREAMS):
                        for stack in (qstack, kstack):
                            for m in range(MAPS):
                                sp.dma_start(stack[s][MAP2 * m + KROWS:MAP2 * (m + 1), :, :],
                                             zeros.unsqueeze(1).broadcast_to([MAP2 - KROWS, AH, T])) \
                                    .then_inc(sig("rows_zeroed"), 16)
                    sp.wait_ge(sig("rows_zeroed"), 16 * 2 * MAPS * STREAMS)
                    sp.wait_ge(sig("x_loaded"), 16 * STREAMS)

                @block.scalar
                def _(act):
                    act.dma_start(rows[:, :], rows_in.partition_broadcast(P)).then_inc(sig("rows_loaded"), 16)
                    for name, a, b in WSECT[3:]:
                        c0, c1 = WCOLS[a][0], WCOLS[b][1]
                        act.dma_start(wt[:, c0:c1], w_in[:, c0:c1]).then_inc(sig(name), 16)
                    act.wait_ge(sig("rows_loaded"), 16)
                    act.activation(small[:, 20:21], row("raw"), ACT.Exp, scale=-1.0).then_inc(sig("raw_exp"), 1)
                    act.wait_ge(sig("lambda_sums"), 2)
                    act.activation(small[:, 24:26], small[:, 22:24], ACT.Exp).then_inc(sig("lambda_exp"), 1)
                    act.wait_ge(sig("head_delta"), 1)
                    act.activation(small[:, 32:40], small[:, 40:48], ACT.Tanh).then_inc(sig("head_tanh"), 1)
                    act.wait_ge(sig("angles"), 1)
                    act.activation(small[:, 10:12], small[:, 8:10], ACT.Sin).then_inc(sig("sincos"), 1)
                    act.wait_ge(sig("abs_products"), 1)
                    act.activation(small[:, 58:60], bank[0][:, 0:2], ACT.Copy).then_inc(sig("abs_total"), 1)
                    act.wait_ge(sig("tables"), 1)
                    act.activation(rot_in_c[:, :], tab_c[:, :], ACT.Identity, scale=small[:, 2:3])
                    act.activation(rot_in_s[0:NSTATE, :], tab_s[0:NSTATE, :], ACT.Identity, scale=small[0:NSTATE, 2:3])
                    act.activation(rot_out_s[:, :], tab_s[:, :], ACT.Identity, scale=-1.0)

                @block.tensor
                def _(pe):
                    pe.wait_ge(sig("ones"), 1)
                    pe.wait_ge(sig("abs_sums"), 1)
                    pe.matmul(bank[0][:, 0:2], ones_sq, small[:, 50:52], start=True, stop=True) \
                        .then_inc(sig("abs_products"), 1)

                @block.gpsimd
                def _(pool):
                    links = [0]

                    def link(ins):
                        links[0] += 1
                        ins.then_inc(sig("pool_link0"), 1)
                        pool.wait_ge(sig("pool_link0"), links[0])

                    pool.memset(zeros, 0.0).then_inc(sig("zeros"), 1)
                    pool.memset(ones_sq, 1.0).then_inc(sig("ones"), 1)
                    pool.memset(neg_half[:, :], -0.5).then_inc(sig("x_free"), 16 * STREAMS)
                    link(pool.memset(ident[:, :], 0.0))
                    link(pool.affine_select(out=ident[:, :], in_=ident[:, :], compare_op=ALU.not_equal,
                                            fill=1.0, base=0, pattern=[[-1, P]], channel_multiplier=1))
                    link(pool.tensor_copy(identb[:, :], ident[:, :]))
                    link(pool.memset(mask_k[:, :, :], 1.0))
                    link(pool.affine_select(out=mask_k[:, :, :], in_=mask_k[:, :, :], compare_op=ALU.is_ge, fill=0.0,
                                            base=0, pattern=[[-XD, XH], [0, CTX]], channel_multiplier=1))
                    link(pool.affine_select(out=mask_k[:, :, :], in_=mask_k[:, :, :], compare_op=ALU.is_ge, fill=0.0,
                                            base=XD - 1, pattern=[[XD, XH], [0, CTX]], channel_multiplier=-1))
                    link(pool.memset(mask_v[:, :, :, :], 0.0))
                    for h in range(HG):
                        link(pool.memset(mask_v[CTX * h:CTX * h + CTX, :, h, :], 1.0))
                    link(pool.memset(expert_rows[:, :, :], 0.0))
                    er = expert_rows[:, :, :].rearrange("r j (e i) -> r j e i", e=EPC)
                    for p in range(3):
                        link(pool.affine_select(out=er, in_=er, compare_op=ALU.not_equal, fill=1.0,
                                                base=-EXPERTS * p, pattern=[[-EPC, RCH], [-1, EPC], [0, EI]],
                                                channel_multiplier=1))
                    link(pool.memset(lower[:, :, :, :], 1.0))
                    link(pool.affine_select(out=lower[:, :, :, :], in_=lower[:, :, :, :], compare_op=ALU.is_gt,
                                            fill=0.0, base=0, pattern=[[0, NT], [1, EXPERTS], [-1, EXPERTS]],
                                            channel_multiplier=0))
                    for s in range(STREAMS):
                        link(pool.memset(vals[s][:, :, :, HV:32], 1.0))
                    pool.wait_ge(sig("abs_total"), 1)
                    inv = 1.0 / (4 * P * P)
                    link(pool.tensor_scalar(small[:, 52:54], small[:, 58:60], inv, 1e-5, ALU.mult, ALU.add))
                    link(pool.tensor_scalar(small[:, 54:56], small[:, 52:54], 0.5, None, ALU.mult))
                    link(pool.tensor_scalar(small[:, 56:58], small[:, 54:56], -1.0, None, ALU.mult))
                    below = big[1][:, 0, :]
                    for i, name in enumerate(("f1w1", "f1w2")):
                        pool.tensor_scalar(below, w(name), small[:, 56 + i:57 + i], None, ALU.is_lt)
                        link(pool.tensor_scalar(w(name), w(name), small[:, 54 + i:55 + i], None, ALU.is_gt))
                        link(pool.tensor_tensor(w(name), w(name), below, ALU.subtract))

                @block.vector
                def _(dve):
                    links = [0]

                    def link(ins):
                        links[0] += 1
                        ins.then_inc(sig("dve_link0"), 1)
                        dve.wait_ge(sig("dve_link0"), links[0])

                    def exp(dst, src, width, negate):
                        z, q, r = (expt[:, a, 0:width] for a in range(3))
                        sign = -1.0 if negate else 1.0
                        link(dve.tensor_scalar(z, src, sign * float(np.log2(np.e)), 127.0, ALU.mult, ALU.min))
                        link(dve.tensor_scalar(z, z, -126.0, None, ALU.max))
                        link(dve.tensor_copy(expi[:, 0:width], z))
                        link(dve.tensor_copy(z, expi[:, 0:width]))
                        link(dve.tensor_scalar(r, src, sign, None, ALU.mult))
                        for part in (0.693359375, -2.12194440e-4):
                            link(dve.scalar_tensor_tensor(r, z, -part, r, ALU.mult, ALU.add))
                        link(dve.tensor_scalar(q, r, 1.0 / 5040, None, ALU.mult))
                        for c in (720, 120, 24, 6, 2, 1):
                            link(dve.scalar_tensor_tensor(q, q, 1.0 / c, r, ALU.add, ALU.mult))
                        link(dve.tensor_scalar(z, z, 127.0, float(1 << 23), ALU.add, ALU.mult))
                        link(dve.tensor_copy(expi[:, 0:width], z))
                        link(dve.scalar_tensor_tensor(dst, q, 1.0, expi[:, 0:width].bitcast(F32), ALU.add, ALU.mult))

                    dve.wait_ge(sig("cols_loaded"), 16)
                    a = COLS["nu"]
                    exp(small[:, 0:3], cols[:, a:a + 3], 3, False)
                    exp(decay[:, :], small[:, 0:1], 1, True)
                    link(dve.tensor_scalar(small[:, 3:4], small[:, 1:2], float(1 / (2 * np.pi)), None, ALU.mult))
                    link(dve.tensor_copy(smalli[:, 0:1], small[:, 3:4]))
                    link(dve.tensor_copy(small[:, 4:5], smalli[:, 0:1]))
                    c1 = 6.28125
                    c2 = float(np.float32(2 * np.pi - c1))
                    link(dve.scalar_tensor_tensor(small[:, 5:6], small[:, 4:5], -c1, small[:, 1:2], ALU.mult, ALU.add))
                    link(dve.scalar_tensor_tensor(small[:, 5:6], small[:, 4:5], -c2, small[:, 5:6], ALU.mult, ALU.add))
                    pi = float(np.float32(np.pi))
                    for op, lim, step in ((ALU.is_gt, pi, -2 * np.pi), (ALU.is_lt, -pi, 2 * np.pi)):
                        link(dve.tensor_scalar(small[:, 6:7], small[:, 5:6], lim, float(step), op, ALU.mult))
                        link(dve.tensor_tensor(small[:, 5:6], small[:, 5:6], small[:, 6:7], ALU.add))
                    below = float(np.nextafter(np.float32(np.pi), np.float32(0)))
                    link(dve.tensor_scalar(small[:, 8:9], small[:, 5:6], below, -below, ALU.min, ALU.max))
                    link(dve.tensor_scalar(small[:, 6:7], small[:, 8:9], -1.0, None, ALU.mult))
                    link(dve.tensor_tensor(small[:, 6:7], small[:, 6:7], small[:, 8:9], ALU.max))
                    dve.tensor_scalar(small[:, 9:10], small[:, 6:7], -1.0, float(np.pi / 2), ALU.mult, ALU.add) \
                        .then_inc(sig("angles"), 1)
                    dve.wait_ge(sig("rows_loaded"), 16)
                    for i, (a, b) in enumerate((("lq1", "lk1"), ("lq2", "lk2"))):
                        link(dve.tensor_tensor(tmp[:, i * AD:(i + 1) * AD], row(a), row(b), ALU.mult))
                        dve.tensor_reduce(small[:, 22 + i:23 + i], tmp[:, i * AD:(i + 1) * AD], AX.X, ALU.add) \
                            .then_inc(sig("lambda_sums"), 1)
                    link(dve.tensor_reduce(small[:, 31:32], row("head_delta"), AX.X, ALU.add))
                    link(dve.tensor_scalar(small[:, 31:32], small[:, 31:32], 1.0 / AH, None, ALU.mult))
                    dve.tensor_scalar(small[:, 40:48], row("head_delta"), small[:, 31:32], None, ALU.subtract) \
                        .then_inc(sig("head_delta"), 1)
                    dve.wait_ge(sig("lambda_exp"), 1)
                    link(dve.tensor_tensor(lam[:, :], small[:, 24:25], small[:, 25:26], ALU.subtract))
                    link(dve.tensor_scalar(lam[:, :], lam[:, :], 0.5, None, ALU.add))
                    dve.wait_ge(sig("raw_exp"), 1)
                    link(dve.tensor_scalar(small[:, 21:22], small[:, 20:21], 1.0, None, ALU.add))
                    link(dve.reciprocal(small[:, 20:21], small[:, 21:22]))
                    link(dve.tensor_scalar(small[:, 21:22], small[:, 20:21], 15.0, None, ALU.mult))
                    dve.wait_ge(sig("head_tanh"), 1)
                    link(dve.tensor_scalar(small[:, 32:40], small[:, 32:40], 0.5, 1.0, ALU.mult, ALU.add))
                    dve.tensor_scalar(qscale[:, 0, :], small[:, 32:40], small[:, 21:22], None, ALU.mult)
                    dve.tensor_scalar(qscale[:, 1, :], small[:, 32:40], small[:, 21:22], -1.0, ALU.mult, ALU.mult)
                    dve.tensor_scalar(sub_half[:, :], row("subln"), 0.5, None, ALU.mult)
                    for l in range(2):
                        dve.tensor_scalar(bq_scaled[:, l:l + 1], col(f"bq{l}"), XSCALE, None, ALU.mult)
                    dve.wait_ge(sig("w_ffn1"), 16)
                    dve.tensor_reduce(small[:, 50:51], w("f1w1"), AX.X, ALU.add, apply_absolute_value=True)
                    dve.tensor_reduce(small[:, 51:52], w("f1w2"), AX.X, ALU.add, apply_absolute_value=True) \
                        .then_inc(sig("abs_sums"), 1)
                    dve.memset(tab_c[:, 0:1], 1.0)
                    link(dve.memset(tab_s[:, 0:1], 0.0))
                    dve.wait_ge(sig("sincos"), 1)
                    dve.tensor_copy(zs[:, 0:1], small[:, 10:11])
                    link(dve.tensor_copy(zc[:, 0:1], small[:, 11:12]))
                    steps = T.bit_length() - 1
                    for k in range(steps):
                        m = 1 << k
                        c, sn = zc[:, k:k + 1], zs[:, k:k + 1]
                        dve.tensor_scalar(tmp[:, 0:m], tab_s[:, 0:m], sn, None, ALU.mult)
                        if k < steps - 1:
                            dve.tensor_tensor(small[:, 12:13], sn, sn, ALU.mult)
                            dve.scalar_tensor_tensor(zs[:, k + 1:k + 2], c, 2.0, sn, ALU.mult, ALU.mult)
                        link(dve.tensor_scalar(tmp[:, 256:256 + m], tab_s[:, 0:m], c, None, ALU.mult))
                        dve.scalar_tensor_tensor(tab_c[:, m:2 * m], tab_c[:, 0:m], c, tmp[:, 0:m], ALU.mult, ALU.subtract)
                        if k < steps - 1:
                            dve.scalar_tensor_tensor(zc[:, k + 1:k + 2], c, c, small[:, 12:13], ALU.mult, ALU.subtract)
                        tables = dve.scalar_tensor_tensor(tab_s[:, m:2 * m], tab_c[:, 0:m], sn, tmp[:, 256:256 + m],
                                                          ALU.mult, ALU.add)
                        if k < steps - 1:
                            link(tables)
                    lo, hi = slice(0, NSTATE), slice(NSTATE, P)
                    tables.then_inc(sig("tables"), 1)
                    dve.wait_ge(sig("tables"), 1)
                    dve.tensor_scalar(rot_in_s[hi, :], tab_s[hi, :], small[hi, 2:3], -1.0, ALU.mult, ALU.mult)
                    dve.tensor_copy(rot_out_c[lo, :], tab_c[lo, :])
                    dve.tensor_scalar(rot_out_c[hi, :], tab_c[hi, :], -1.0, None, ALU.mult)

        prologue()
        keep = set(sems)
        def body(i):
            with nc.Block() as block:
                def spill(queue, s, which, part):
                    name = ("q", "k")[which]
                    queue.wait_ge(sig(f"{name}part{part}"), s + 1)
                    a, b, step = (QGROUPS, KGROUPS)[which][part]
                    queue.dma_start(parts_dram[s, which, a:b:step].rearrange("c r t -> r c t"),
                                    (qpart, kpart)[which][s][:, part:part + 1, :]
                                    .broadcast_to([P, len(range(a, b, step)), T])) \
                        .then_inc(sig(f"{name}_spilled{s}"), 16)

                def restack(queue, s, which, half):
                    stack = (qstack, kstack)[which]
                    queue.wait_ge(sig(f"{('q', 'k')[which]}_spilled{s}"), 16 * 3)
                    h = slice(half * AH // 2, (half + 1) * AH // 2)
                    for m in range(MAPS):
                        queue.dma_start(stack[s][MAP2 * m:MAP2 * m + KROWS, h, :],
                                        parts_dram[s, which][:, AH * AD * m:AH * AD * (m + 1), :]
                                        .rearrange("c (r h) t -> c r h t", h=AH)[:, :, h, :]
                                        .rearrange("c r h t -> c r (h t)")).then_inc(sig(f"stacked{s}_{half}"), 16)

                shape = [P, NT * AH, HV]

                def head_views(s):
                    y1 = qT[s][:, :].rearrange("p (h d) -> p h d", d=HV)
                    y2 = cT[s][:, :].rearrange("p (h d) -> p h d", d=HV)
                    y = xn[s][:, :, :].rearrange("p t (h d) -> p (t h) d", d=HV)
                    return y1, y2, y, [peak[s][:, a, :] for a in range(4)]

                def heads_over_sums(engine, link, s):
                    y1, y2, y, pk = head_views(s)
                    o = on[s][:, :, :, :].rearrange("p t (h m) c -> p (t h) m c", m=MAPS)
                    engine.tensor_tensor(y1, o[:, :, 0, 0:HV], rzo[s][:, :, 0].unsqueeze(2).broadcast_to(shape), ALU.mult)
                    link(engine.tensor_tensor(y2, o[:, :, 1, 0:HV], rzo[s][:, :, 1].unsqueeze(2).broadcast_to(shape),
                                              ALU.mult))
                    return engine.tensor_tensor(y1, y1, y2, ALU.subtract)

                def heads_squared(engine, link, s):
                    y1, y2, y, pk = head_views(s)
                    link(engine.tensor_tensor(y1, y1, pk[1].unsqueeze(2).broadcast_to(shape), ALU.mult))
                    return engine.tensor_tensor(y2, y1, y1, ALU.mult)

                def heads_normed(engine, link, s):
                    y1, y2, y, pk = head_views(s)
                    link(engine.tensor_tensor(pk[2], pk[2], rzo[s][:, :, 0], ALU.mult))
                    link(engine.tensor_tensor(y1, y1, pk[2].unsqueeze(2).broadcast_to(shape), ALU.mult))
                    return engine.tensor_tensor(y, y1, sub_half[:, :].unsqueeze(1).broadcast_to(shape), ALU.mult)

                @block.sync
                def _(sp):
                    for s in range(STREAMS):
                        b = bass.ds(i * STREAMS + s, 1)
                        sp.dma_start(ctxT[s][:, :, :],
                                     ctx_in[b].rearrange("b d k -> d b k").broadcast_to([D, HG, CTX])) \
                            .then_inc(sig(f"ctx_loaded{s}"), 16)
                        sp.dma_start(m0[s][:, :, :], m0_in[b].rearrange("b p t k -> p (b t) k")) \
                            .then_inc(sig(f"masks_loaded{s}"), 16)
                        sp.dma_start(m1[s][:, :, :], m1_in[b].rearrange("b p t k -> p (b t) k")) \
                            .then_inc(sig(f"masks_loaded{s}"), 16)
                    for s in range(STREAMS):
                        sp.wait_ge(sig("x_done"), turn(0, s))
                        load_x(sp, s, STREAMS * (TURNS - 1) + s - i * STREAMS, "next_loaded")
                    for s in range(STREAMS):
                        for part in range(3):
                            for which in range(2):
                                spill(sp, s, which, part)
                        for half in range(2):
                            for which in range(2):
                                restack(sp, s, which, half)
                    sp.wait_ge(sig("next_loaded"), 16 * STREAMS)
                    for s in range(STREAMS):
                        sp.wait_ge(sig("x_done"), turn(5, s))
                        b = bass.ds(i * STREAMS + s, 1)
                        sp.dma_start(out[b].rearrange("b (t p) d -> p (b t) d", p=P), x[s][:, :, :]) \
                            .then_inc(sig("x_free"), 16)

                @block.gpsimd
                def _(pool):
                    links = [0]

                    def link(ins):
                        links[0] += 1
                        ins.then_inc(sig("pool_link"), 1)
                        pool.wait_ge(sig("pool_link"), links[0])

                    def rstd_of(k, s):
                        pool.wait_ge(sig("moments"), turn(k, s))
                        link(pool.tensor_scalar(veps[s][:, :], mv[s][:, :, 1], LN_EPS, None, ALU.add))
                        pool.tensor_tensor(rstd[s][:, :], veps[s][:, :], neg_half[:, 0:NT], ALU.pow) \
                            .then_inc(sig("rstd_ready"), 1)

                    def rstds(k):
                        for s in range(STREAMS):
                            rstd_of(k, s)

                    def bias_of(k, s, bias):
                        pool.wait_ge(sig("xn_ready"), turn(k, s))
                        pool.tensor_tensor(x[s][:, :, :], x[s][:, :, :],
                                           row(bias).unsqueeze(1).broadcast_to([P, NT, D]), ALU.add) \
                            .then_inc(sig(f"biased{k}"), 1)

                    def biases(k, bias):
                        for s in range(STREAMS):
                            bias_of(k, s, bias)

                    def recurrence():
                        for s in range(STREAMS):
                            pool.wait_ge(sig("scanned"), s + 1)
                            pool.tensor_tensor(big2[s][:, 1, :], big[s][:, 2, :], rot_out_s[:, :], ALU.mult) \
                                .then_inc(sig("rotated_out_s"), 1)

                    def caps0(s):
                        pool.wait_ge(sig(f"masks_loaded{s}"), 16 * 2)
                        pool.tensor_scalar(cap[0][s][:, :, :], m0[s][:, :, :], 0.0, BIG, ALU.is_equal, ALU.mult)
                        link(pool.tensor_scalar(cap_part[s][:, :, :], m0[s][:, :, :], -1.0e18, None, ALU.mult))
                        pool.tensor_tensor(cap[0][s][:, :, :], cap[0][s][:, :, :], cap_part[s][:, :, :], ALU.add) \
                            .then_inc(sig("caps0"), 1)

                    def caps1(s):
                        link(pool.tensor_scalar(cap[1][s][:, :, :], m1[s][:, :, :], 0.0, -BIG, ALU.is_equal, ALU.mult))
                        pool.tensor_scalar(cap[1][s][:, :, :], cap[1][s][:, :, :], 100.0, None, ALU.add) \
                            .then_inc(sig("caps1"), 1)

                    def shift(l, s, *tiles):
                        for t in tiles:
                            pool.wait_ge(sig(f"max_found{s}"), l * NT + t + 1)
                            a = big[s][:, t, :].rearrange("p (h k) -> p h k", k=CTX)
                            pool.tensor_tensor(a, a, mx[s][:, t, :].unsqueeze(2).broadcast_to([P, XH, CTX]),
                                               ALU.subtract).then_inc(sig(f"shifted{s}"), 1)

                    def first_heads_end():
                        pool.wait_ge(sig("head_sums"), 1)
                        heads_over_sums(pool, link, 0).then_inc(sig("head_difference"), 1)
                        pool.wait_ge(sig("head_peaks"), 1)
                        heads_squared(pool, link, 0).then_inc(sig("head_squares"), 1)
                        pool.wait_ge(sig("mean_square"), 1)
                        link(pool.tensor_tensor(rzo[0][:, :, 0], ms[0][:, :], neg_half[:, 0:NT * AH], ALU.pow))
                        pool.wait_ge(sig("head_guard"), 1)
                        heads_normed(pool, link, 0).then_inc(sig("y_made"), 1)

                    rstds(0)
                    for s in range(STREAMS):
                        caps0(s)
                    recurrence()
                    rstds(1)
                    biases(1, "bo_x0")
                    for t in range(NT):
                        for s in range(STREAMS):
                            shift(0, s, t)
                    rstds(2)
                    rstds(3)
                    biases(3, "bo_a")
                    for s in range(STREAMS):
                        caps1(s)
                    first_heads_end()
                    rstd_of(4, 0)
                    shift(1, 0, 0, 1)
                    rstd_of(4, 1)
                    bias_of(4, 0, "bo_x1")
                    shift(1, 0, 2, 3)
                    bias_of(4, 1, "bo_x1")
                    shift(1, 1, 0, 1)
                    rstd_of(5, 0)
                    shift(1, 1, 2, 3)
                    bias_of(5, 0, "b2")
                    rstd_of(5, 1)
                    bias_of(5, 1, "b2")

                @block.scalar
                def _(act):
                    def turn_out(k, s):
                        act.wait_ge(sig("xn_turned"), turn(k, s))
                        act.activation(xT[s][:, :], bk(s, 0), ACT.Copy).then_inc(sig("xT_ready"), 1)

                    def q_out(l, s):
                        act.wait_ge(sig("q_made"), turn(l, s))
                        act.activation(qT[s][:, :], bk(s, 1), ACT.Identity, scale=XSCALE,
                                       bias=bq_scaled[:, l:l + 1]).then_inc(sig("q_ready"), 1)

                    def weights(l, s, t):
                        act.wait_ge(sig(f"shifted{s}"), l * NT + t + 1)
                        act.activation(big[s][:, t, :], big[s][:, t, :], ACT.Exp).then_inc(sig(f"weights{s}"), 1)

                    def weights_out(l, s, t):
                        act.wait_ge(sig(f"weights_turned{s}"), l * NT + t + 1)
                        act.activation(big2[s][:, t, :], bk(s, t % 2), ACT.Copy).then_inc(sig(f"weightsT_ready{s}"), 1)

                    for s in range(STREAMS):
                        turn_out(0, s)
                    for s in range(STREAMS):
                        turn_out(1, s)
                    for s in range(STREAMS):
                        q_out(0, s)
                    for t in range(NT + 1):
                        for s in range(STREAMS):
                            if t < NT:
                                weights(0, s, t)
                        for s in range(STREAMS):
                            if t:
                                weights_out(0, s, t - 1)
                    for s in range(STREAMS):
                        turn_out(2, s)
                    for s in range(STREAMS):
                        act.wait_ge(sig("gate_logits"), s + 1)
                        act.activation(sg[s][:, :, :], bk(s, 3)[:, 0:NT * EXPERTS].rearrange("p (t e) -> p t e", t=NT),
                                       ACT.Exp, scale=-1.0).then_inc(sig("gate_exp"), 1)
                    for j in range(FCH):
                        if j == 2:
                            for s in range(STREAMS):
                                act.wait_ge(sig("comb_turned"), s + 1)
                                act.activation(combT[s][:, :], bk(s, 3).bitcast(BF16)[0:3 * EXPERTS, 0:T], ACT.Copy) \
                                    .then_inc(sig("combT_ready"), 1)
                        for s in range(STREAMS):
                            act.wait_ge(sig("gated"), turn(j, s))
                            if j >= 2:
                                act.wait_ge(sig("hidden"), turn(j - 2, s))
                            act.activation(big[s][:, j % 2, :], bk(s, 1), ACT.Tanh, scale=0.5) \
                                .then_inc(sig("gate_tanh"), 1)
                    for s in range(STREAMS):
                        turn_out(3, s)
                    act.activation(scrap[:, :], ident[:, 0:1], ACT.Sqrt)
                    def lengths(s):
                        act.wait_ge(sig("square_sums"), s + 1)
                        act.activation(ss[s][:, :, :], ss[s][:, :, :], ACT.Sqrt).then_inc(sig("lengths"), 1)

                    def parts(s):
                        for name, part, b, got in (("q", qpart, 1, "q_turned"), ("k", kpart, 2, "k_turned")):
                            act.wait_ge(sig(got), s + 1)
                            act.activation(part[s][:, 0, :], bk(s, b), ACT.Copy).then_inc(sig(f"{name}part0"), 1)
                        for name, part, a in (("q", qpart, 0), ("k", kpart, 1)):
                            act.wait_ge(sig(f"{name}_rest"), s + 1)
                            act.activation(part[s][:, 1, :], big2[s][:, a, :], ACT.Copy).then_inc(sig(f"{name}part1"), 1)

                    for s in range(STREAMS):
                        for t in range(NT):
                            act.wait_ge(sig("qkv_made"), s * NT + t + 1)
                            act.activation(big[s][:, t // 2, 256 * (t % 2):256 * (t % 2) + 256], bk(s, t)[:, 0:256],
                                           ACT.Square).then_inc(sig("squares"), 1)
                        for t in range(NT):
                            act.activation(vals[s][:, t, :, 0:HV],
                                           bk(s, t)[:, 256:384].rearrange("p (h d) -> p h d", h=AH),
                                           ACT.Copy).then_inc(sig("vals_ready"), 1)
                        if s == 0:
                            lengths(0)
                    parts(0)
                    lengths(1)
                    parts(1)

                    def difference(n):
                        s, h, c = unit(n)
                        a, _ = ROWS["gain"]
                        act.wait_ge(sig("diff_made"), n + 1)
                        if n >= 2:
                            act.wait_ge(sig("logits_made"), 2 * (n - 1))
                        act.activation(gate_t[:, n % 2, :, :], pair[:, :, :], ACT.Tanh,
                                       scale=rows[:, a + h:a + h + 1]).then_inc(sig("gate_ready"), 1)

                    def exps(n):
                        act.wait_ge(sig("logits_made"), 2 * n + 2)
                        if n >= 4:
                            act.wait_ge(sig("pair_used"), n // 2 - 1)
                        for m in range(MAPS):
                            act.activation(prob[n % 4][:, :, m, :], logit[n % 2][:, :, m, :], ACT.Exp,
                                           scale=1.0 if m == 0 else -1.0).then_inc(sig("prob_ready"), 1)

                    difference(0)
                    for n in range(UNITS):
                        if n + 1 < UNITS:
                            difference(n + 1)
                        exps(n)
                    act.activation(scrap[:, :], ident[:, 0:1], ACT.Sqrt)
                    turn_out(4, 0)
                    q_out(1, 0)
                    act.wait_ge(sig("mean_square"), 2)
                    act.activation(ms[1][:, :], ms[1][:, :], ACT.Sqrt).then_inc(sig("head_length"), 1)
                    act.wait_ge(sig("y_turned"), 2)
                    act.activation(cT[1][:, :], bk(1, 1), ACT.Copy).then_inc(sig("y_ready"), 1)
                    for s in range(STREAMS):
                        weights(1, s, 0)
                        weights(1, s, 1)
                        weights_out(1, s, 0)
                        weights_out(1, s, 1)
                        weights(1, s, 2)
                        weights(1, s, 3)
                        turn_out(4 + s, 1 - s)
                        weights_out(1, s, 2)
                        if s == 0:
                            q_out(1, 1)
                        weights_out(1, s, 3)
                    for s in range(STREAMS):
                        if s:
                            turn_out(5, s)
                        for j in range(F1CH):
                            act.wait_ge(sig(f"f1_made{s}"), j + 1)
                            act.activation(big[s][:, j, :], bk(s, 1 + j % 2), ACT.Relu, bias=col(f"b1_{j}")) \
                                .then_inc(sig(f"f1_hidden{s}"), 1)

                @block.vector
                def _(dve):
                    links = [0]

                    def link(ins):
                        links[0] += 1
                        ins.then_inc(sig("dve_link"), 1)
                        dve.wait_ge(sig("dve_link"), links[0])

                    def moments(k, s):
                        if k:
                            dve.wait_ge(sig("x_done"), turn(k - 1, s))
                        for t in range(NT):
                            ins = dve.bn_stats(bst[s][:, t, :], (x if k else x_next)[s][:, t, :])
                        link(ins)
                        for t in range(NT):
                            ins = dve.bn_aggr(mv[s][:, t, :], bst[s][:, t, :])
                        ins.then_inc(sig("moments"), 1)

                    def normed_of(k, s):
                        dve.wait_ge(sig("rstd_ready"), turn(k, s))
                        if k:
                            dve.wait_ge(sig("xn_turned"), turn(k - 1, s))
                        for t in range(NT):
                            ins = dve.tensor_scalar(xn[s][:, t, :], (x if k else x_next)[s][:, t, :], mv[s][:, t, 0:1],
                                                    rstd[s][:, t:t + 1], ALU.subtract, ALU.mult)
                        ins.then_inc(sig("xn_ready"), 1)

                    def normed(k):
                        for s in range(STREAMS):
                            normed_of(k, s)

                    def residual(k, s, b, made):
                        dve.wait_ge(sig(made), s + 1)
                        if k in (1, 3, 4, 5):
                            dve.wait_ge(sig(f"biased{k}"), s + 1)
                        if k == 0 and s == 0:
                            dve.wait_ge(sig("x_free"), 16 * STREAMS)
                            dve.sem_clear(sig("x_free"))
                        dve.tensor_tensor(x[s][:, :, :], bk(s, b).rearrange("p (t d) -> p t d", t=NT),
                                          (x if k else x_next)[s][:, :, :], ALU.add).then_inc(sig("x_done"), 1)

                    def cross_blocks(l, s, b):
                        dve.wait_ge(sig("kv_made"), turn(l, s))
                        dve.scalar_tensor_tensor(key_blocks[s][:, :, :],
                                                 bk(s, b)[:, 0:CTX].unsqueeze(1).broadcast_to([P, XH, CTX]),
                                                 col(f"bk{l}"), mask_k[:, :, :], ALU.add, ALU.mult)
                        vb = val_blocks[s][:, :, :]
                        link(dve.tensor_tensor(vb, bk(s, b)[:, P:2 * P].rearrange("p (g c) -> p g c", g=NG),
                                               row(f"bv{l}").rearrange("p (g c) -> p g c", g=NG), ALU.add))
                        dve.tensor_tensor(vb, vb, mask_v[:, :, :, :].rearrange("p g h d -> p g (h d)"), ALU.mult) \
                            .then_inc(sig("kv_blocks"), 1)

                    def cap_and_max(l, *tiles):
                        for s, t in tiles:
                            if t == 0:
                                dve.wait_ge(sig(f"caps{l}"), s + 1)
                            dve.wait_ge(sig(f"scores_made{s}"), l * NT + t + 1)
                            dve.scalar_tensor_tensor(big[s][:, t, :].rearrange("p (h k) -> p h k", k=CTX),
                                                     bk(s, 2 + t % 2).rearrange("p (h k) -> p h k", k=CTX),
                                                     -BIG if l == 0 else -100.0,
                                                     cap[l][s][:, t, :].unsqueeze(1).broadcast_to([P, XH, CTX]),
                                                     ALU.max, ALU.min).then_inc(sig(f"capped{s}"), 1)
                        for s, t in tiles:
                            dve.wait_ge(sig(f"capped{s}"), l * NT + t + 1)
                            dve.tensor_reduce(mx[s][:, t, :], big[s][:, t, :].rearrange("p (h k) -> p h k", k=CTX),
                                              AX.X, ALU.max).then_inc(sig(f"max_found{s}"), 1)

                    def cross_end(l, s, a):
                        dve.wait_ge(sig(f"weighed{s}"), 2 * l + a + 1)
                        sums_over = xn[s][:, :, :].rearrange("p t d -> p (t d)")[:, a * HALF:(a + 1) * HALF]
                        link(dve.reciprocal(sums_over, bk(s, 2 + a)[:, HALF:T]))
                        dve.tensor_tensor(cT[s][:, a * HALF:(a + 1) * HALF], bk(s, 2 + a)[:, 0:HALF], sums_over,
                                          ALU.mult).then_inc(sig(f"ctx_ready{s}"), 1)

                    for s in range(STREAMS):
                        moments(0, s)
                    normed(0)
                    for s in range(STREAMS):
                        dve.wait_ge(sig("states_in"), s + 1)
                        dve.tensor_tensor(big[s][:, 0, :], bk(s, 1), rot_in_c[:, :], ALU.mult)
                        dve.tensor_tensor(big[s][:, 1, :], bk(s, 2), rot_in_s[:, :], ALU.mult) \
                            .then_inc(sig("rotated_in"), 1)
                    for s in range(STREAMS):
                        dve.wait_ge(sig("rotated_in"), s + 1)
                        dve.tensor_tensor(big[s][:, 0, :], big[s][:, 0, :], big[s][:, 1, :], ALU.add) \
                            .then_inc(sig("scan_input"), 1)
                    for s in range(STREAMS):
                        dve.wait_ge(sig("scan_input"), s + 1)
                        dve.tensor_tensor_scan(big[s][:, 2, :], decay[:, 0:1].broadcast_to([P, T]), big[s][:, 0, :],
                                               0.0, ALU.mult, ALU.add).then_inc(sig("scanned"), 1)
                    for s in range(STREAMS):
                        dve.wait_ge(sig("scanned"), s + 1)
                        dve.tensor_tensor(big2[s][:, 0, :], big[s][:, 2, :], rot_out_c[:, :], ALU.mult) \
                            .then_inc(sig("rotated_out_c"), 1)
                    for s in range(STREAMS):
                        cross_blocks(0, s, 2)
                    for s in range(STREAMS):
                        residual(0, s, 3, "lru_out")
                        moments(1, s)
                    normed(1)
                    for t in range(NT):
                        cap_and_max(0, *((s, t) for s in range(STREAMS)))
                    for a in range(2):
                        for s in range(STREAMS):
                            cross_end(0, s, a)
                    for s in range(STREAMS):
                        residual(1, s, 1, "cross_out0")
                    for s in range(STREAMS):
                        moments(2, s)
                    normed(2)
                    def hidden(j, s):
                        th, hid = big[s][:, j % 2, :], big2[s][:, j % 2, :]
                        dve.wait_ge(sig("gate_tanh"), turn(j, s))
                        if j >= 2:
                            dve.wait_ge(sig("down"), turn(j - 2, s))
                        link(dve.scalar_tensor_tensor(hid, th, 1.0, bk(s, 1), ALU.add, ALU.mult))
                        dve.wait_ge(sig("upped"), turn(j, s))
                        if FFN_ORDER[j] < RCH:
                            link(dve.tensor_tensor(hid, hid, bk(s, 2), ALU.mult))
                            dve.wait_ge(sig("comb_spread"), turn(j - 1, s))
                            dve.tensor_tensor(hid, hid, bk(s, 3), ALU.mult).then_inc(sig("hidden"), 1)
                        else:
                            dve.scalar_tensor_tensor(hid, hid, 0.5, bk(s, 2), ALU.mult, ALU.mult) \
                                .then_inc(sig("hidden"), 1)

                    for s in range(STREAMS):
                        dve.wait_ge(sig("gate_exp"), s + 1)
                        link(dve.tensor_scalar(sg[s][:, :, :], sg[s][:, :, :], 1.0, None, ALU.add))
                        dve.reciprocal(sg[s][:, :, :], sg[s][:, :, :]).then_inc(sig("gate_scores"), 1)
                    for s in range(STREAMS):
                        dve.wait_ge(sig("gate_scores"), s + 1)
                        sj = sg[s][:, :, :].unsqueeze(2).broadcast_to([P, NT, EXPERTS, EXPERTS])
                        se = sg[s][:, :, :].unsqueeze(3).broadcast_to([P, NT, EXPERTS, EXPERTS])
                        dve.tensor_tensor(cmpa[s], sj, se, ALU.is_gt)
                        ins = dve.tensor_tensor(cmpb[s], sj, se, ALU.is_equal)
                    link(ins)
                    for s in range(STREAMS):
                        ins = dve.tensor_tensor(cmpb[s], cmpb[s], lower[:, :, :, :], ALU.mult)
                    link(ins)
                    for s in range(STREAMS):
                        ins = dve.tensor_tensor(cmpa[s], cmpa[s], cmpb[s], ALU.add)
                    for s in range(STREAMS):
                        for t in range(NT):
                            ins = dve.max(top[s][:, t, :], sg[s][:, t, :])
                    link(ins)
                    for s in range(STREAMS):
                        ins = dve.scalar_tensor_tensor(wsum[s][:, :], top[s][:, :, 0], 1e-20, top[s][:, :, 1],
                                                       ALU.add, ALU.add)
                    link(ins)
                    for s in range(STREAMS):
                        ins = dve.reciprocal(wsum[s][:, :], wsum[s][:, :])
                    link(ins)
                    hidden(0, 0)
                    for s in range(STREAMS):
                        ins = dve.tensor_reduce(rank[s][:, :, :], cmpa[s], AX.X, ALU.add)
                    link(ins)
                    for s in range(STREAMS):
                        ins = dve.tensor_scalar(rank[s][:, :, :], rank[s][:, :, :], 1.5, 0.5 * ROUTE_SCALE,
                                                ALU.is_lt, ALU.mult)
                    link(ins)
                    for s in range(STREAMS):
                        ins = dve.tensor_tensor(cres[s][:, :, :], sg[s][:, :, :], rank[s][:, :, :], ALU.mult)
                    link(ins)
                    for s in range(STREAMS):
                        ins = dve.tensor_tensor(cres[s][:, :, :], cres[s][:, :, :],
                                                wsum[s][:, :].unsqueeze(2).broadcast_to([P, NT, EXPERTS]), ALU.mult)
                    link(ins)
                    hidden(0, 1)
                    for p in range(2):
                        for s in range(STREAMS):
                            ins = dve.tensor_copy(cpart[s][:, :, p, :], cres[s][:, :, :])
                        link(ins)
                        for s in range(STREAMS):
                            ins = dve.tensor_tensor(cres[s][:, :, :], cres[s][:, :, :], cpart[s][:, :, p, :], ALU.subtract)
                        link(ins)
                    for s in range(STREAMS):
                        dve.tensor_copy(cpart[s][:, :, 2, :], cres[s][:, :, :]).then_inc(sig("comb_ready"), 1)
                    for j in range(1, FCH):
                        for s in range(STREAMS):
                            hidden(j, s)
                    for s in range(STREAMS):
                        residual(2, s, 0, "ffn0_out")
                        moments(3, s)
                    normed(3)
                    def square_sums(s):
                        dve.wait_ge(sig("squares"), NT * (s + 1))
                        dve.tensor_reduce(ss[s][:, :, :].rearrange("p t (b h) -> p (t b) h", h=AH),
                                          big[s][:, 0:2, :].rearrange("p a (b d h) -> p (a b) h d", d=AD, h=AH), AX.X, ALU.add) \
                            .then_inc(sig("square_sums"), 1)

                    def unit_vectors(s):
                        dve.wait_ge(sig("lengths"), s + 1)
                        link(dve.tensor_scalar(ss[s][:, :, :], ss[s][:, :, :], 1e-6, None, ALU.max))
                        link(dve.reciprocal(ss[s][:, :, :], ss[s][:, :, :]))
                        link(dve.tensor_tensor(ss[s][:, :, 0:2 * AH], ss[s][:, :, 0:2 * AH],
                                               qscale[:, :, :].rearrange("p m h -> p (m h)").unsqueeze(1)
                                               .broadcast_to([P, NT, 2 * AH]), ALU.mult))
                        for t in range(NT):
                            split = "p (b d h) -> p b d h"
                            ins = dve.tensor_tensor(qkn[s][:, t, :].rearrange(split, d=AD, h=AH),
                                                    bk(s, t)[:, 0:256].rearrange(split, d=AD, h=AH),
                                                    ss[s][:, t, :].rearrange("p (b h) -> p b h", h=AH).unsqueeze(2)
                                                    .broadcast_to([P, 2 * MAPS, AD, AH]), ALU.mult)
                        ins.then_inc(sig("unit_vectors"), 1)

                    def rests(s):
                        for a, part, b, got, gives in ((0, qpart, 1, "qpart0", "q_rest"), (1, kpart, 2, "kpart0", "k_rest")):
                            dve.wait_ge(sig(got), s + 1)
                            dve.tensor_tensor(big2[s][:, a, :], bk(s, b), part[s][:, 0, :], ALU.subtract) \
                                .then_inc(sig(gives), 1)
                        for name, part, a in (("q", qpart, 0), ("k", kpart, 1)):
                            dve.wait_ge(sig(f"{name}part1"), s + 1)
                            dve.tensor_tensor(part[s][:, 2, :], big2[s][:, a, :], part[s][:, 1, :], ALU.subtract) \
                                .then_inc(sig(f"{name}part2"), 1)

                    square_sums(0)
                    unit_vectors(0)
                    square_sums(1)
                    rests(0)
                    unit_vectors(1)
                    rests(1)
                    for s in range(STREAMS):
                        cross_blocks(1, s, 3)

                    def logits(n):
                        if n == 0:
                            dve.wait_ge(sig("kpart2"), STREAMS)
                        dve.wait_ge(sig("gate_ready"), n + 1)
                        for j in range(2):
                            dve.wait_ge(sig("scores_ready"), 2 * n + j + 1)
                            if n >= 2:
                                dve.wait_ge(sig("prob_ready"), 2 * (n - 1))
                            dve.tensor_tensor(logit[n % 2][:, j, :, :], quad[:, j, :, :],
                                              gate_t[:, n % 2, j, :].unsqueeze(1).broadcast_to([P, MAPS, T]), ALU.add) \
                                .then_inc(sig("logits_made"), 1)

                    def heads_out(g):
                        dve.wait_ge(sig("pair_used"), 2 * (g + 1))
                        if g >= 1:
                            dve.wait_ge(sig("heads_turned"), g)
                        dve.tensor_copy(accT[:, :], bank[0][:, :]).then_inc(sig("heads_out"), 1)

                    def heads_in(g):
                        s, hp = g // PAIRS, g % PAIRS
                        dve.wait_ge(sig("heads_turned"), g + 1)
                        dve.tensor_copy(on[s][:, :, 4 * hp:4 * hp + 4, :].rearrange("p t h d -> p t (h d)"),
                                        bank[1][:, :].rearrange("p (t c) -> p t c", t=NT)).then_inc(sig("heads_in"), 1)

                    def head_sums(s):
                        dve.wait_ge(sig("heads_in"), 4 * (s + 1))
                        o = on[s][:, :, :, :].rearrange("p t (h m) c -> p (t h) m c", m=MAPS)
                        link(dve.reciprocal(rzo[s][:, :, :], o[:, :, :, HV]))
                        return dve.tensor_scalar(rzo[s][:, :, 1], rzo[s][:, :, 1], lam[:, 0:1], None, ALU.mult)

                    def head_peaks(s):
                        y1, y2, y, pk = head_views(s)
                        link(dve.tensor_reduce(pk[0], y1, AX.X, ALU.max, apply_absolute_value=True))
                        link(dve.tensor_scalar(pk[0], pk[0], 1e-15, None, ALU.max))
                        dve.tensor_scalar(pk[2], pk[0], 2.0 ** -64, 1.0e3, ALU.mult, ALU.min)
                        return dve.reciprocal(pk[1], pk[0])

                    def head_mean_squares(s):
                        y1, y2, y, pk = head_views(s)
                        dve.scalar_tensor_tensor(pk[3], pk[1], RMS_EPS, pk[1], ALU.mult, ALU.mult)
                        link(dve.tensor_reduce(pk[0], y2, AX.X, ALU.add))
                        dve.scalar_tensor_tensor(ms[s][:, :], pk[0], 1.0 / HV, pk[3], ALU.mult, ALU.add) \
                            .then_inc(sig("mean_square"), 1)
                        link(dve.tensor_tensor(pk[2], pk[2], pk[2], ALU.mult))
                        link(dve.tensor_tensor(pk[2], pk[2], pk[0], ALU.mult))
                        return dve.tensor_scalar(pk[2], pk[2], 1.0, None, ALU.is_lt)

                    for n in range(UNITS):
                        logits(n)
                        g, c = n // 4 - 1, n % 4
                        if g >= 0 and c == 2:
                            heads_out(g)
                        if g >= 0 and c == 3:
                            heads_in(g)
                        if n == (PAIRS + 1) * 4:
                            head_sums(0).then_inc(sig("head_sums"), 1)
                        if n == (PAIRS + 2) * 4:
                            dve.wait_ge(sig("head_difference"), 1)
                            head_peaks(0).then_inc(sig("head_peaks"), 1)
                        if n == (PAIRS + 3) * 4:
                            dve.wait_ge(sig("head_squares"), 1)
                            head_mean_squares(0).then_inc(sig("head_guard"), 1)
                    dve.wait_ge(sig("y_turned"), 1)
                    dve.tensor_copy(cT[0][:, :], bk(0, 1)).then_inc(sig("y_ready"), 1)
                    heads_out(GROUPS - 1)
                    residual(3, 0, 2, "attn_out")
                    moments(4, 0)
                    heads_in(GROUPS - 1)
                    link(head_sums(1))
                    link(heads_over_sums(dve, link, 1))
                    normed_of(4, 0)
                    link(head_peaks(1))
                    link(heads_squared(dve, link, 1))
                    link(head_mean_squares(1))
                    dve.wait_ge(sig("head_length"), 1)
                    link(dve.reciprocal(rzo[1][:, :, 0], ms[1][:, :]))
                    heads_normed(dve, link, 1).then_inc(sig("y_made"), 1)
                    cap_and_max(1, (0, 0), (0, 1))
                    residual(3, 1, 2, "attn_out")
                    moments(4, 1)
                    cap_and_max(1, (0, 2), (0, 3))
                    normed_of(4, 1)
                    cross_end(1, 0, 0)
                    cross_end(1, 0, 1)
                    cap_and_max(1, (1, 0), (1, 1))
                    residual(4, 0, 1, "cross_out1")
                    moments(5, 0)
                    cap_and_max(1, (1, 2), (1, 3))
                    normed_of(5, 0)
                    for a in range(2):
                        cross_end(1, 1, a)
                    residual(4, 1, 1, "cross_out1")
                    moments(5, 1)
                    normed_of(5, 1)
                    for s in range(STREAMS):
                        residual(5, s, 3, "ffn1_out")

                @block.tensor
                def _(pe):
                    def keep_warm(dst, count):
                        for _ in range(count):
                            pe.matmul(dst, identb[:, :], mask_k[:, :, :].rearrange("p h k -> p (h k)").bitcast(BF16)[:, 0:T], start=True, stop=True)

                    def turn_in(k, s):
                        if k:
                            pe.wait_ge(sig("x_done"), turn(k - 1, s))
                        if s == 0 and k < 4:
                            keep_warm(bk(0, 0), WARM_UP_NORM)
                        pe.wait_ge(sig("xn_ready"), turn(k, s))
                        for t in range(NT):
                            ins = pe.transpose(bk(s, 0)[:, t * P:(t + 1) * P], xn[s][:, t, :], ident[:, :])
                        ins.then_inc(sig("xn_turned"), 1)

                    def to_tokens(dst, pairs, done):
                        for t in range(NT):
                            for a, (lhs, rhs) in enumerate(pairs):
                                ins = pe.matmul(dst[:, t * P:(t + 1) * P], lhs[:, t * P:(t + 1) * P], rhs,
                                                start=(a == 0), stop=(a == len(pairs) - 1))
                        ins.then_inc(sig(done), 1)

                    def context(l, s, b):
                        pe.wait_ge(sig(f"w_x{l}"), 16)
                        pe.wait_ge(sig(f"ctx_loaded{s}"), 16)
                        pe.matmul(bk(s, b)[:, 0:CTX], w(f"x{l}k"), ctxT[s][:, 0, :], start=True, stop=True)
                        pe.matmul(bk(s, b)[:, P:2 * P], ctxT[s][:, :, :].rearrange("p h k -> p (h k)"), w(f"x{l}v"),
                                  start=True, stop=True).then_inc(sig("kv_made"), 1)

                    def cross_q(l, k, s):
                        pe.wait_ge(sig("xT_ready"), turn(k, s))
                        pe.matmul(bk(s, 1), w(f"x{l}q"), xT[s][:, :], start=True, stop=True).then_inc(sig("q_made"), 1)

                    def cross_scores(l, s, t):
                        pe.wait_ge(sig("q_ready"), turn(l, s))
                        pe.wait_ge(sig("kv_blocks"), turn(l, s))
                        if t >= 2:
                            pe.wait_ge(sig(f"capped{s}"), l * NT + t - 1)
                        pe.matmul(bk(s, 2 + t % 2), qT[s][:, t * P:(t + 1) * P],
                                  key_blocks[s][:, :, :].rearrange("p h k -> p (h k)"),
                                  start=True, stop=True).then_inc(sig(f"scores_made{s}"), 1)

                    def cross_turn(l, s, t):
                        pe.wait_ge(sig(f"weights{s}"), l * NT + t + 1)
                        if t >= 2:
                            pe.wait_ge(sig(f"weightsT_ready{s}"), l * NT + t - 1)
                        for g in range(NG):
                            ins = pe.transpose(bk(s, t % 2)[:, g * P:(g + 1) * P], big[s][:, t, g * P:(g + 1) * P],
                                               ident[:, :])
                        ins.then_inc(sig(f"weights_turned{s}"), 1)

                    def cross_weigh(l, s, a):
                        pe.wait_ge(sig(f"weightsT_ready{s}"), l * NT + 2 * a + 2)
                        pe.wait_ge(sig(f"capped{s}"), l * NT + a + 3)
                        for half, lhs in ((0, None), (1, mask_v[:, 0, :, :].rearrange("p h d -> p (h d)"))):
                            for g in range(NG):
                                ins = pe.matmul(bk(s, 2 + a)[32 * g:32 * g + 32, half * HALF:(half + 1) * HALF],
                                                val_blocks[s][:, g, :] if lhs is None else lhs,
                                                big2[s][:, 2 * a:2 * a + 2, g * P:(g + 1) * P],
                                                start=True, stop=True)
                        ins.then_inc(sig(f"weighed{s}"), 1)

                    def cross_out(l, s, a):
                        pe.wait_ge(sig(f"ctx_ready{s}"), 2 * l + a + 1)
                        if a == 0:
                            pe.wait_ge(sig(f"weightsT_ready{s}"), l * NT + NT)
                        for t in (2 * a, 2 * a + 1):
                            ins = pe.matmul(bk(s, 1)[:, t * P:(t + 1) * P], cT[s][:, t * P:(t + 1) * P],
                                            w(f"x{l}o"), start=True, stop=True)
                        if a == 1:
                            ins.then_inc(sig(f"cross_out{l}"), 1)

                    def ternary_up(s, j):
                        pe.wait_ge(sig("xT_ready"), turn(5, s))
                        if j >= 2:
                            pe.wait_ge(sig(f"f1_hidden{s}"), j - 1)
                        pe.matmul(bk(s, 1 + j % 2), wch("f1w1", j), xT[s][:, :], start=True, stop=True) \
                            .then_inc(sig(f"f1_made{s}"), 1)

                    def ternary_down(s):
                        pe.wait_ge(sig(f"f1_hidden{s}"), F1CH)
                        to_tokens(bk(s, 3), [(big[s][:, j, :], wch("f1w2", j)) for j in range(F1CH)], "ffn1_out")

                    pe.wait_ge(sig("w_lru"), 16)
                    for s in range(STREAMS):
                        turn_in(0, s)
                    for s in range(STREAMS):
                        pe.wait_ge(sig("xT_ready"), s + 1)
                        pe.matmul(bk(s, 1), w("bt1"), xT[s][:, :], start=True, stop=True)
                        pe.matmul(bk(s, 2), w("bt2"), xT[s][:, :], start=True, stop=True).then_inc(sig("states_in"), 1)
                    for s in range(STREAMS):
                        pe.wait_ge(sig("rotated_in"), s + 1)
                        context(0, s, 2)
                    keep_warm(bk(0, 3), WARM_UP_SCAN)
                    for s in range(STREAMS):
                        pe.wait_ge(sig("rotated_out_c"), s + 1)
                        pe.wait_ge(sig("rotated_out_s"), s + 1)
                        to_tokens(bk(s, 3), [(big2[s][:, 0, :], w("wc1")), (big2[s][:, 1, :], w("wc2")),
                                             (xT[s], w("dt"))], "lru_out")
                    for s in range(STREAMS):
                        turn_in(1, s)
                    for s in range(STREAMS):
                        cross_q(0, 1, s)
                    for t in range(NT):
                        for s in range(STREAMS):
                            cross_scores(0, s, t)
                    for t in range(NT):
                        for s in range(STREAMS):
                            cross_turn(0, s, t)
                        if t == 1:
                            for s in range(STREAMS):
                                cross_weigh(0, s, 0)
                    for s in range(STREAMS):
                        cross_weigh(0, s, 1)
                    for a in range(2):
                        for s in range(STREAMS):
                            cross_out(0, s, a)

                    pe.wait_ge(sig("w_ffn0"), 16)
                    for s in range(STREAMS):
                        turn_in(2, s)
                    for s in range(STREAMS):
                        pe.wait_ge(sig("xT_ready"), turn(2, s))
                        for t in range(NT):
                            ins = pe.matmul(bk(s, 3)[:, t * EXPERTS:(t + 1) * EXPERTS], xT[s][:, t * P:(t + 1) * P],
                                            w("gate"), start=True, stop=True)
                        ins.then_inc(sig("gate_logits"), 1)

                    def turn_comb(s):
                        pe.wait_ge(sig("gate_exp"), s + 1)
                        pe.wait_ge(sig("comb_ready"), s + 1)
                        for t in range(NT):
                            ins = pe.transpose(bk(s, 3).bitcast(BF16)[0:3 * EXPERTS, t * P:(t + 1) * P],
                                               cpart[s][:, t, :, :].rearrange("p a e -> p (a e)"), identb[:, :])
                        ins.then_inc(sig("comb_turned"), 1)

                    def up(j, s):
                        if j:
                            pe.wait_ge(sig("hidden"), turn(j - 1, s))
                        c = FFN_ORDER[j]
                        pe.matmul(bk(s, 1), wch("wg", c), xT[s][:, :], start=True, stop=True).then_inc(sig("gated"), 1)
                        pe.matmul(bk(s, 2), wch("wu", c), xT[s][:, :], start=True, stop=True).then_inc(sig("upped"), 1)

                    def spread_comb(j, s):
                        pe.wait_ge(sig("combT_ready"), s + 1)
                        pe.matmul(bk(s, 3), expert_rows[:, FFN_ORDER[j], :], combT[s][:, :], start=True, stop=True) \
                            .then_inc(sig("comb_spread"), 1)

                    def down(j, s):
                        pe.wait_ge(sig("hidden"), turn(j, s))
                        for t in range(NT):
                            ins = pe.matmul(bk(s, 0)[:, t * P:(t + 1) * P], big2[s][:, j % 2, t * P:(t + 1) * P],
                                            wch("wd", FFN_ORDER[j]), start=(j == 0 and t == 0), stop=(j == FCH - 1),
                                            skip_group_check=True)
                        ins.then_inc(sig("down" if j < FCH - 1 else "ffn0_out"), 1)

                    for j in range(FCH):
                        for s in range(STREAMS):
                            up(j, s)
                            if j >= 2:
                                spread_comb(j, s)
                            if j:
                                down(j - 1, s)
                        if j == 1:
                            for s in range(STREAMS):
                                turn_comb(s)
                            for s in range(STREAMS):
                                spread_comb(1, s)
                    for s in range(STREAMS):
                        down(FCH - 1, s)

                    pe.wait_ge(sig("w_attn"), 16)
                    for s in range(STREAMS):
                        turn_in(3, s)
                    for s in range(STREAMS):
                        pe.wait_ge(sig("xT_ready"), turn(3, s))
                        for t in range(NT):
                            pe.matmul(bk(s, t)[:, 0:384], xT[s][:, t * P:(t + 1) * P], w("aqkv"),
                                      start=True, stop=True).then_inc(sig("qkv_made"), 1)
                    for s in range(STREAMS):
                        pe.wait_ge(sig("unit_vectors"), s + 1)
                        pe.wait_ge(sig("vals_ready"), NT * (s + 1))
                        for a, got in ((0, "q_turned"), (1, "k_turned")):
                            for t in range(NT):
                                ins = pe.transpose(bk(s, 1 + a)[:, t * P:(t + 1) * P],
                                                   qkn[s][:, t, a * P:(a + 1) * P], ident[:, :])
                            ins.then_inc(sig(got), 1)

                    pe.wait_ge(sig("k_rest"), STREAMS)
                    for s in range(STREAMS):
                        context(1, s, 3)
                    keep_warm(bank[1][:, :], WARM_UP)

                    def differences(n):
                        s, h, c = unit(n)
                        if n == 0:
                            pe.wait_ge(sig("k_rest"), STREAMS)
                            pe.wait_ge(sig("q_rest"), STREAMS)
                            pe.wait_ge(sig("kv_blocks"), 2 * STREAMS)
                        if n % (2 * PAIRS) == 0:
                            pe.wait_ge(sig(f"stacked{s}_{h // (AH // 2)}"), 16 * 2 * MAPS)
                        if n >= 1:
                            pe.wait_ge(sig("gate_ready"), n)
                        for j in range(2):
                            ins = pe.matmul(pair[:, j, :], kstack[s][:, h, (c + j) * P:(c + j + 1) * P],
                                            qstack[s][:, h, :], start=True, stop=True)
                        ins.then_inc(sig("diff_made"), 1)

                    def scores(n):
                        s, h, c = unit(n)
                        for j in range(2):
                            if n >= 1:
                                pe.wait_ge(sig("logits_made"), 2 * (n - 1) + j + 1)
                            for m in range(MAPS):
                                r = slice(MAP2 * m, MAP2 * m + MAP2)
                                ins = pe.matmul(quad[:, j, m, :], kstack[s][r, h, (c + j) * P:(c + j + 1) * P],
                                                qstack[s][r, h, :], start=True, stop=True)
                            ins.then_inc(sig("scores_ready"), 1)

                    def weigh(k, j):
                        s, h, c = unit(2 * k)
                        g = k // 2
                        if j == 0:
                            pe.wait_ge(sig("prob_ready"), 2 * (2 * k + 2))
                            if c == 0 and g >= 1:
                                pe.wait_ge(sig("heads_out"), g)
                        for hh in range(2):
                            for m in range(MAPS):
                                q = 32 * (2 * hh + m)
                                ins = pe.matmul(bank[0][q:q + 32, :], vals[s][:, c + j, h + hh, :],
                                                prob[(2 * k + hh) % 4][:, j, m, :], start=(c + j == 0),
                                                stop=(c + j == KC - 1), skip_group_check=True)
                        if j == 1:
                            ins.then_inc(sig("pair_used"), 1)

                    def heads_turn(g):
                        pe.wait_ge(sig("heads_out"), g + 1)
                        if g >= 1:
                            pe.wait_ge(sig("heads_in"), g)
                        for t in range(NT):
                            ins = pe.transpose(bank[1][:, t * P:(t + 1) * P], accT[:, t * P:(t + 1) * P], ident[:, :])
                        ins.then_inc(sig("heads_turned"), 1)

                    LAG = 4

                    def attention_turn(s):
                        pe.wait_ge(sig("y_made"), s + 1)
                        pe.wait_ge(sig("logits_made"), 2 * UNITS)
                        for t in range(NT):
                            ins = pe.transpose(bk(s, 1)[:, t * P:(t + 1) * P], xn[s][:, t, :], ident[:, :])
                        ins.then_inc(sig("y_turned"), 1)

                    def attention_out(s):
                        pe.wait_ge(sig("y_ready"), s + 1)
                        to_tokens(bk(s, 2), [(cT[s], w("ao"))], "attn_out")

                    for n in range(UNITS + LAG):
                        if n < UNITS:
                            differences(n)
                        if n == UNITS + 2:
                            attention_turn(0)
                        if n >= LAG:
                            weigh((n - LAG) // 2, (n - LAG) % 2)
                            if n >= 2 * LAG and n % 4 == 0:
                                heads_turn(n // 4 - 2)
                        if n < UNITS:
                            scores(n)
                    attention_out(0)
                    heads_turn(GROUPS - 1)

                    keep_warm(bk(0, 0), WARM_UP_HEADS)
                    turn_in(4, 0)
                    cross_q(1, 4, 0)
                    cross_scores(1, 0, 0)
                    cross_scores(1, 0, 1)
                    attention_turn(1)
                    attention_out(1)
                    cross_scores(1, 0, 2)
                    cross_scores(1, 0, 3)
                    cross_turn(1, 0, 0)
                    cross_turn(1, 0, 1)
                    cross_weigh(1, 0, 0)
                    turn_in(4, 1)
                    cross_turn(1, 0, 2)
                    cross_turn(1, 0, 3)
                    cross_q(1, 4, 1)
                    cross_weigh(1, 0, 1)
                    cross_scores(1, 1, 0)
                    cross_scores(1, 1, 1)
                    cross_out(1, 0, 0)
                    cross_out(1, 0, 1)
                    cross_scores(1, 1, 2)
                    cross_scores(1, 1, 3)
                    cross_turn(1, 1, 0)
                    cross_turn(1, 1, 1)
                    cross_weigh(1, 1, 0)
                    turn_in(5, 0)
                    cross_turn(1, 1, 2)
                    cross_turn(1, 1, 3)
                    cross_weigh(1, 1, 1)
                    ternary_up(0, 0)
                    ternary_up(0, 1)
                    cross_out(1, 1, 0)
                    cross_out(1, 1, 1)
                    ternary_up(0, 2)
                    ternary_up(0, 3)
                    ternary_down(0)
                    turn_in(5, 1)
                    for j in range(F1CH):
                        ternary_up(1, j)
                    ternary_down(1)

        with nc.Fori(0, B // STREAMS) as i:
            body(i)
            engines = [nc.gpsimd, nc.sync, nc.scalar, nc.vector, nc.tensor]
            for j, name in enumerate(n for n in sems if n not in keep):
                engines[j % len(engines)].sem_clear(sems[name])
            nc.all_engine_barrier()
        with nc.Block() as block:
            @block.sync
            def _(sp):
                sp.wait_ge(sig("x_free"), 16 * STREAMS)


def kernel(**inputs):
    import concourse.bacc as bacc
    from concourse.bass_utils import run_bass_kernel_spmd as run

    v = {k: np.asarray(a) for k, a in inputs.items()}
    t = lambda n: v[n].T
    routed = lambda n: v[n].reshape(EXPERTS * EI, D).T
    maps_first = lambda n: v[n].reshape(AH, MAPS, AD, D).transpose(1, 2, 0, 3).reshape(D, D).T
    down = v["L0_ffn_w_down"].transpose(0, 2, 1).reshape(RCH, P, D).transpose(1, 0, 2).reshape(P, RCH * D)
    w2 = v["L1_ffn_W2"].T.reshape(F1CH, P, D).transpose(1, 0, 2).reshape(P, F1CH * D)
    w = np.concatenate([
        t("L0_attn_B_re"), t("L0_attn_B_im"), t("L0_attn_B_im"), t("L0_attn_B_re"),
        np.concatenate([t("L0_attn_C_re"), t("L0_attn_C_im")]),
        np.concatenate([t("L0_attn_C_im"), t("L0_attn_C_re")]), t("L0_attn_D"),
        t("L1_ffn_W1"), w2,
        t("L0_xattn_Wq"), t("L0_xattn_Wk"), t("L0_xattn_Wv"), t("L0_xattn_Wo"),
        t("L0_ffn_gate_weight"), routed("L0_ffn_w_gate"), t("L0_ffn_ws_gate"),
        routed("L0_ffn_w_up"), t("L0_ffn_ws_up"), down, t("L0_ffn_ws_down"),
        maps_first("L1_attn_Wq"), maps_first("L1_attn_Wk"), t("L1_attn_Wv"), t("L1_attn_Wo"),
        t("L1_xattn_wq"), t("L1_xattn_wk"), t("L1_xattn_wv"), t("L1_xattn_wo")], axis=1)
    by_tile = lambda m: m.reshape(B, NT, P, CTX).transpose(0, 2, 1, 3)
    twice = lambda n: np.concatenate([v[n], v[n]])
    cols = np.stack([twice("L0_attn_nu_log"), twice("L0_attn_theta_log"), twice("L0_attn_gamma_log"),
                     v["L0_xattn_bq"], v["L0_xattn_bk"], v["L1_xattn_bq"], v["L1_xattn_bk"],
                     *v["L1_ffn_b1"].reshape(F1CH, P)], axis=1)
    rows = np.concatenate([v["L0_xattn_bv"], v["L1_xattn_bv"], v["L0_xattn_bo"], v["L1_attn_bo"],
                           v["L1_xattn_bo"], v["L1_ffn_b2"], v["L1_attn_delta_gain"], v["L1_attn_cos_head_delta"],
                           v["L1_attn_cos_logit_scale_raw"].reshape(1), v["L1_attn_lambda_q1"],
                           v["L1_attn_lambda_k1"], v["L1_attn_lambda_q2"], v["L1_attn_lambda_k2"],
                           v["L1_attn_subln_weight"]])
    assert w.shape == (P, WTOTAL) and cols.shape == (P, len(COLS)) and rows.shape == (RTOTAL,)
    arrays = {"x": v["x"], "ctx": v["ctx_1024"].transpose(0, 2, 1),
              "mask0": by_tile(v["mask_BxSxS2_bf0"]), "mask1": by_tile(v["mask_Bx1xSxS2_ik1"]), "w": w, "cols": cols, "rows": rows}
    arrays = {k: np.ascontiguousarray(a) for k, a in arrays.items()}
    nc = bacc.Bacc("TRN2", target_bir_lowering=False, num_devices=1)
    args = [nc.dram_tensor(f"{k}_in", a.shape, mybir.dt.from_np(a.dtype), kind="ExternalInput").ap()
            for k, a in arrays.items()]
    args.append(nc.dram_tensor("out", (B, T, D), F32, kind="ExternalOutput").ap())
    build(nc, *args)
    r = run(nc, [{f"{k}_in": a for k, a in arrays.items()}], core_ids=[0])
    return r.results[0]["out"]
```
